# Optimizing a Trainium2 kernel written in Bass

```python
import numpy as np
import jax
import jax.numpy as jnp

def _softmax(x, axis=-1):
    return jax.nn.softmax(x, axis=axis)

def _gelu(x):
    return jax.nn.gelu(x, approximate=True)

def _silu(x):
    return jax.nn.silu(x)

def _sigmoid(x):
    return jax.nn.sigmoid(x)

def _layernorm(x, axis=-1, eps=1e-05):
    m = jnp.mean(x, axis=axis, keepdims=True)
    v = jnp.var(x, axis=axis, keepdims=True)
    return (x - m) / jnp.sqrt(v + eps)

def _scatter_add(tgt, idx, src, axis=0):
    return tgt.at[idx].add(src)

def _segment_sum(src, seg, n):
    return jax.ops.segment_sum(src, seg, n)
kernel_name = 'mk_decoder_preln_d1_seqx_r4_5d173c'

def setup_inputs(seed: int=0):
    np.random.seed(seed)
    _w = jnp.asarray

    def _rec_inputs():
        import jax
        import jax.numpy as jnp
        _rk = jax.random.key(seed)
        x = 7.22e-05 + 1 * jax.random.normal(jax.random.fold_in(_rk, 1), (8, 512, 256), jnp.float32)
        _lenS = 512 - jax.random.randint(jax.random.fold_in(_rk, 7), (8,), 0, max(1, 512 // 4) + 1, jnp.int32)
        _lenS2 = 64 - jax.random.randint(jax.random.fold_in(_rk, 8), (8,), 0, max(1, 64 // 4) + 1, jnp.int32)
        _ctx_1024P = jax.random.normal(jax.random.fold_in(_rk, 11), (8, 16, 256), jnp.float32)
        _ctx_1024c = jax.random.dirichlet(jax.random.fold_in(_rk, 511), 0.3 * jnp.ones((16,), jnp.float32), (8, 64))
        _ctx_1024t = jnp.einsum('bsk,bkd->bsd', _ctx_1024c, _ctx_1024P)
        _ctx_1024t = _ctx_1024t * jax.lax.rsqrt(jnp.mean(jnp.square(_ctx_1024t)) + 1e-12) * 0.953939
        ctx_1024 = 4.13588e-05 + 0.999923 * (_ctx_1024t + 0.3 * jax.random.normal(jax.random.fold_in(_rk, 611), (8, 64, 256), jnp.float32))
        return (x, ctx_1024)
    x, ctx_1024 = _rec_inputs()

    def _L0_attn_setup():
        import jax, jax.numpy as jnp
        import numpy as np
        B, S, E = (4, 512, 256)
        H, KVH = (16, 4)
        D = E // H
        QL, KVL = (64, 32)
        ROPE_BASE = 10000.0

        def _rope(x):
            d = x.shape[-1]
            inv_freq = 1.0 / ROPE_BASE ** (jnp.arange(0, d, 2, dtype=jnp.float32) / d)
            t = jnp.arange(x.shape[1], dtype=jnp.float32)
            freqs = jnp.outer(t, inv_freq)
            cos = jnp.cos(freqs)[None, :, None, :].astype(x.dtype)
            sin = jnp.sin(freqs)[None, :, None, :].astype(x.dtype)
            x1, x2 = (x[..., ::2], x[..., 1::2])
            r1 = x1 * cos - x2 * sin
            r2 = x1 * sin + x2 * cos
            return jnp.stack([r1, r2], axis=-1).reshape(x.shape)
        key = jax.random.key(seed)
        ks = jax.random.split(key, 7)
        s = 0.02
        return {'x': jax.random.normal(ks[0], (B, S, E), dtype=jnp.float32), 'Wqa': jax.random.normal(ks[1], (E, QL), dtype=jnp.float32) * s, 'Wqb': jax.random.normal(ks[2], (QL, E), dtype=jnp.float32) * s, 'Wkva': jax.random.normal(ks[3], (E, KVL), dtype=jnp.float32) * s, 'Wkvb': jax.random.normal(ks[4], (KVL, KVH * D * 2), dtype=jnp.float32) * s, 'Wout': jax.random.normal(ks[5], (E, E), dtype=jnp.float32) * s, 'bout': jax.random.normal(ks[6], (E,), dtype=jnp.float32) * s}
    _L0_attn_all = _L0_attn_setup()
    _L0_attn_in = {k: v for k, v in _L0_attn_all.items() if k in ('Wqa', 'Wqb', 'Wkva', 'Wkvb', 'Wout', 'bout')}
    del _L0_attn_all

    def _L0_xattn_setup():
        import jax, jax.numpy as jnp
        import numpy as np
        DIM = 256
        HEADS = 16
        DIM_HEAD = 64
        INNER = HEADS * DIM_HEAD
        MLP = 1024
        EPS = 1e-05

        def _layernorm(x, g, b):
            mu = jnp.mean(x, axis=-1, keepdims=True)
            var = jnp.mean(jnp.square(x - mu), axis=-1, keepdims=True)
            return (x - mu) * jax.lax.rsqrt(var + EPS) * g + b

        def _l2norm(x):
            n = jnp.sqrt(jnp.sum(jnp.square(x), axis=-1, keepdims=True))
            return x / jnp.maximum(n, 1e-12)

        def _split_heads(x, B, N):
            return x.reshape(B, N, HEADS, DIM_HEAD).transpose(0, 2, 1, 3)
        key = jax.random.key(seed)
        ks = jax.random.split(key, 16)
        B, N = (4, 512)
        s = 0.02
        return {'Q': jax.random.normal(ks[0], (B, N, DIM), jnp.float32), 'K': jax.random.normal(ks[1], (B, N, DIM), jnp.float32), 'V': jax.random.normal(ks[2], (B, N, DIM), jnp.float32), 'wq': jax.random.normal(ks[3], (DIM, INNER), jnp.float32) * s, 'wk': jax.random.normal(ks[4], (DIM, INNER), jnp.float32) * s, 'wv': jax.random.normal(ks[5], (DIM, INNER), jnp.float32) * s, 'wo': jax.random.normal(ks[6], (INNER, DIM), jnp.float32) * s, 'bo': jnp.zeros((DIM,), jnp.float32), 'w1': jax.random.normal(ks[7], (DIM, MLP), jnp.float32) * s, 'b1': jnp.zeros((MLP,), jnp.float32), 'w2': jax.random.normal(ks[8], (MLP, DIM), jnp.float32) * s, 'b2': jnp.zeros((DIM,), jnp.float32), 'ln1_g': jnp.ones((DIM,), jnp.float32), 'ln1_b': jnp.zeros((DIM,), jnp.float32), 'ln2_g': jnp.ones((DIM,), jnp.float32), 'ln2_b': jnp.zeros((DIM,), jnp.float32)}
    _L0_xattn_all = _L0_xattn_setup()
    _L0_xattn_in = {k: v for k, v in _L0_xattn_all.items() if k in ('wq', 'wk', 'wv', 'wo', 'bo', 'w1', 'b1', 'w2', 'b2', 'ln1_g', 'ln1_b', 'ln2_g', 'ln2_b')}
    del _L0_xattn_all

    def _L0_ffn_setup():
        import jax, jax.numpy as jnp
        import numpy as np
        EMB = 256
        FF = 4 * EMB

        def _ternary(w):
            scale = jnp.maximum(jnp.mean(jnp.abs(w)), 1e-08)
            w_t = jnp.clip(jnp.round(w / scale), -1.0, 1.0)
            return w + jax.lax.stop_gradient(w_t - w)
        key = jax.random.key(seed)
        kx, k1, k2, kb1, kb2 = jax.random.split(key, 5)
        x = jax.random.normal(kx, (4, 512, EMB), dtype=jnp.float32)
        lim1 = 1.0 / np.sqrt(EMB)
        lim2 = 1.0 / np.sqrt(FF)
        W1 = jax.random.uniform(k1, (FF, EMB), jnp.float32, -lim1, lim1)
        b1 = jax.random.uniform(kb1, (FF,), jnp.float32, -lim1, lim1)
        W2 = jax.random.uniform(k2, (EMB, FF), jnp.float32, -lim2, lim2)
        b2 = jax.random.uniform(kb2, (EMB,), jnp.float32, -lim2, lim2)
        return {'x': x, 'W1': W1, 'b1': b1, 'W2': W2, 'b2': b2}
    _L0_ffn_all = _L0_ffn_setup()
    _L0_ffn_in = {k: v for k, v in _L0_ffn_all.items() if k in ('W1', 'b1', 'W2', 'b2')}
    del _L0_ffn_all
    return {'x': x, 'ctx_1024': ctx_1024, 'L0_attn_Wqa': _L0_attn_in['Wqa'], 'L0_attn_Wqb': _L0_attn_in['Wqb'], 'L0_attn_Wkva': _L0_attn_in['Wkva'], 'L0_attn_Wkvb': _L0_attn_in['Wkvb'], 'L0_attn_Wout': _L0_attn_in['Wout'], 'L0_attn_bout': _L0_attn_in['bout'], 'L0_xattn_wq': _L0_xattn_in['wq'], 'L0_xattn_wk': _L0_xattn_in['wk'], 'L0_xattn_wv': _L0_xattn_in['wv'], 'L0_xattn_wo': _L0_xattn_in['wo'], 'L0_xattn_bo': _L0_xattn_in['bo'], 'L0_xattn_w1': _L0_xattn_in['w1'], 'L0_xattn_b1': _L0_xattn_in['b1'], 'L0_xattn_w2': _L0_xattn_in['w2'], 'L0_xattn_b2': _L0_xattn_in['b2'], 'L0_xattn_ln1_g': _L0_xattn_in['ln1_g'], 'L0_xattn_ln1_b': _L0_xattn_in['ln1_b'], 'L0_xattn_ln2_g': _L0_xattn_in['ln2_g'], 'L0_xattn_ln2_b': _L0_xattn_in['ln2_b'], 'L0_ffn_W1': _L0_ffn_in['W1'], 'L0_ffn_b1': _L0_ffn_in['b1'], 'L0_ffn_W2': _L0_ffn_in['W2'], 'L0_ffn_b2': _L0_ffn_in['b2']}

def reference(x, ctx_1024, L0_attn_Wqa, L0_attn_Wqb, L0_attn_Wkva, L0_attn_Wkvb, L0_attn_Wout, L0_attn_bout, L0_xattn_wq, L0_xattn_wk, L0_xattn_wv, L0_xattn_wo, L0_xattn_bo, L0_xattn_w1, L0_xattn_b1, L0_xattn_w2, L0_xattn_b2, L0_xattn_ln1_g, L0_xattn_ln1_b, L0_xattn_ln2_g, L0_xattn_ln2_b, L0_ffn_W1, L0_ffn_b1, L0_ffn_W2, L0_ffn_b2):
    import jax
    import jax.numpy as jnp

    def _L0_attn_ref(x, Wqa, Wqb, Wkva, Wkvb, Wout, bout):
        import jax, jax.numpy as jnp
        import numpy as np
        B, S, E = (4, 512, 256)
        H, KVH = (16, 4)
        D = E // H
        QL, KVL = (64, 32)
        ROPE_BASE = 10000.0

        def _rope(x):
            d = x.shape[-1]
            inv_freq = 1.0 / ROPE_BASE ** (jnp.arange(0, d, 2, dtype=jnp.float32) / d)
            t = jnp.arange(x.shape[1], dtype=jnp.float32)
            freqs = jnp.outer(t, inv_freq)
            cos = jnp.cos(freqs)[None, :, None, :].astype(x.dtype)
            sin = jnp.sin(freqs)[None, :, None, :].astype(x.dtype)
            x1, x2 = (x[..., ::2], x[..., 1::2])
            r1 = x1 * cos - x2 * sin
            r2 = x1 * sin + x2 * cos
            return jnp.stack([r1, r2], axis=-1).reshape(x.shape)
        b, s, _ = x.shape
        scale = D ** (-0.5)
        q = (x @ Wqa @ Wqb).reshape(b, s, H, D)
        kv = (x @ Wkva @ Wkvb).reshape(b, s, KVH, D, 2)
        k, v = (kv[..., 0], kv[..., 1])
        q = _rope(q)
        k = _rope(k)
        g = H // KVH
        k = jnp.repeat(k, g, axis=2)
        v = jnp.repeat(v, g, axis=2)
        scores = jnp.einsum('bqhd,bkhd->bhqk', q, k) * scale
        causal = jnp.triu(jnp.ones((s, s), dtype=bool), k=1)
        scores = jnp.where(causal[None, None], -jnp.inf, scores)
        w = jax.nn.softmax(scores, axis=-1)
        out = jnp.einsum('bhqk,bkhd->bqhd', w, v).reshape(b, s, E)
        return out @ Wout + bout

    def _L0_xattn_ref(Q, K, V, wq, wk, wv, wo, bo, w1, b1, w2, b2, ln1_g, ln1_b, ln2_g, ln2_b):
        import jax, jax.numpy as jnp
        import numpy as np
        DIM = 256
        HEADS = 16
        DIM_HEAD = 64
        INNER = HEADS * DIM_HEAD
        MLP = 1024
        EPS = 1e-05

        def _layernorm(x, g, b):
            mu = jnp.mean(x, axis=-1, keepdims=True)
            var = jnp.mean(jnp.square(x - mu), axis=-1, keepdims=True)
            return (x - mu) * jax.lax.rsqrt(var + EPS) * g + b

        def _l2norm(x):
            n = jnp.sqrt(jnp.sum(jnp.square(x), axis=-1, keepdims=True))
            return x / jnp.maximum(n, 1e-12)

        def _split_heads(x, B, N):
            return x.reshape(B, N, HEADS, DIM_HEAD).transpose(0, 2, 1, 3)
        B, Nq, _ = Q.shape
        Nk = K.shape[1]
        Qn = _layernorm(Q, ln1_g, ln1_b)
        Kn = _layernorm(K, ln1_g, ln1_b)
        Vn = _layernorm(V, ln1_g, ln1_b)
        q = _split_heads(Qn @ wq, B, Nq)
        k = _split_heads(Kn @ wk, B, Nk)
        v = _split_heads(Vn @ wv, B, Nk)
        qn = _l2norm(q)
        kn = _l2norm(k)
        attn = jnp.einsum('bhqd,bhkd->bhqk', qn, kn)
        out = jnp.einsum('bhqk,bhkd->bhqd', attn, v)
        out = out.transpose(0, 2, 1, 3).reshape(B, Nq, INNER)
        x = Q + out @ wo + bo
        xn = _layernorm(x, ln2_g, ln2_b)
        h = jax.nn.gelu(xn @ w1 + b1, approximate=False)
        return x + h @ w2 + b2

    def _L0_ffn_ref(x, W1, b1, W2, b2):
        import jax, jax.numpy as jnp
        import numpy as np
        EMB = 256
        FF = 4 * EMB

        def _ternary(w):
            scale = jnp.maximum(jnp.mean(jnp.abs(w)), 1e-08)
            w_t = jnp.clip(jnp.round(w / scale), -1.0, 1.0)
            return w + jax.lax.stop_gradient(w_t - w)
        h = jnp.einsum('bsd,fd->bsf', x, _ternary(W1)) + b1
        h = jax.nn.gelu(h, approximate=False)
        out = jnp.einsum('bsf,df->bsd', h, _ternary(W2)) + b2
        return out
    x = x + _L0_attn_ref(_layernorm(x, axis=-1), L0_attn_Wqa, L0_attn_Wqb, L0_attn_Wkva, L0_attn_Wkvb, L0_attn_Wout, L0_attn_bout)
    x = x + _L0_xattn_ref(_layernorm(x, axis=-1), ctx_1024, ctx_1024, L0_xattn_wq, L0_xattn_wk, L0_xattn_wv, L0_xattn_wo, L0_xattn_bo, L0_xattn_w1, L0_xattn_b1, L0_xattn_w2, L0_xattn_b2, L0_xattn_ln1_g, L0_xattn_ln1_b, L0_xattn_ln2_g, L0_xattn_ln2_b)
    x = x + _L0_ffn_ref(_layernorm(x, axis=-1), L0_ffn_W1, L0_ffn_b1, L0_ffn_W2, L0_ffn_b2)
    return x

_drawn_inputs = setup_inputs


def setup_inputs(seed=0):
    import zlib

    import numpy as np

    out = dict(_drawn_inputs(seed))
    spreads = {'L0_xattn_bo': (0.0, 0.533),
     'L0_xattn_b1': (0.0, 0.557),
     'L0_xattn_b2': (0.0, 0.551),
     'L0_xattn_ln1_g': (1.0, 0.2),
     'L0_xattn_ln1_b': (0.0, 0.367),
     'L0_xattn_ln2_g': (1.0, 0.6),
     'L0_xattn_ln2_b': (0.0, 2.0)}
    factors = {'L0_attn_Wqa': 8.0,
     'L0_attn_Wqb': 8.0,
     'L0_attn_Wkva': 8.0,
     'L0_attn_Wkvb': 8.0,
     'L0_attn_Wout': 8.0,
     'L0_attn_bout': 15.154,
     'L0_ffn_b1': 22.701,
     'L0_ffn_b2': 64.0}
    for name, (base, spread) in spreads.items():
        noise = np.random.default_rng([zlib.crc32(name.encode()), seed]).standard_normal(out[name].shape)
        drawn = base * np.exp(spread * noise) if base else spread * noise
        out[name] = jnp.asarray(drawn.astype(out[name].dtype))
    for name, factor in factors.items():
        out[name] = (out[name] * factor).astype(out[name].dtype)
    return out
```

```python
from contextlib import ExitStack

import numpy as np
import concourse.bass as bass
from concourse import mybir

F32 = mybir.dt.float32
F32R = mybir.dt.float32r
BF16 = mybir.dt.bfloat16
ALU = mybir.AluOpType
ACT = mybir.ActivationFunctionType
AX_X = mybir.AxisListType.X

P = 128
B = 8
S = 512
TT = S // P
E = 256
C = E // P
H = 16
KVH = 4
G = H // KVH
D = E // H
QL = 64
KVL = 32
R = QL + KVL
XH = 16
XD = 64
XI = XH * XD
XT = XI // P
CTX = 64
FT = 1024 // P
EPS = 1e-5
ROPE_BASE = 10000.0
SCALE = float(D) ** -0.5
MASKED = -3.0e38

PAIRS = [(0, 0), (0, 1), (0, 2), (1, 0), (1, 1), (2, 0)]
SROWS = len(PAIRS) * D
MROWS = 3


def rope_tables():
    inv = (1.0 / ROPE_BASE ** (np.arange(0, D, 2, dtype=np.float32) / np.float32(D))).astype(np.float32)
    angle = np.outer(inv, np.arange(S, dtype=np.float32)).astype(np.float32)
    cos = np.repeat(np.cos(angle), 2, axis=0)
    sin = np.repeat(np.sin(angle), 2, axis=0)
    sin[0::2] *= -1.0
    n = P // D
    return np.stack([np.tile(cos, (n, 1)), np.tile(sin, (n, 1))]).astype(np.float32)


def causal_mask():
    q = np.arange(P)
    return np.where(q[None, :] <= q[:, None], 0.0, MASKED).astype(np.float32)


def head_selectors():
    sums = np.zeros((XT, P, P), np.float32)
    spread = np.zeros((XT, P, P), np.float32)
    for t in range(XT):
        for p in range(P):
            h = 2 * t + p // XD
            sums[t, p, h::XH] = 1.0
            spread[t, h, p] = 1.0
            spread[t, 32 + h, p] = 1.0
    return np.stack([sums, spread])


def project_phase(nc, a, scr):
    with ExitStack() as ctx:
        def sb(name, shape, dt):
            return ctx.enter_context(nc.sbuf_tensor("p1_" + name, shape, dt))

        def ps(name, shape):
            return ctx.enter_context(nc.psum_tensor("p1_" + name, shape, F32))

        def sem(name):
            return ctx.enter_context(nc.semaphore("p1_" + name))

        UNITS = 3
        RING = 3
        KW = KVH * D

        ident = sb("ident", [P, P], F32)
        wa = sb("wa", [P, C, R], F32)
        wq = sb("wq", [R, E], F32)
        wq_swap = sb("wq_swap", [R, E], F32)
        wkv = sb("wkv", [R, KVH, D, 2], F32)
        wk = sb("wk", [R, KW], F32)
        wk_swap = sb("wk_swap", [R, KW], F32)
        wv = sb("wv", [R, KW], F32)
        cos = sb("cos", [P, S], F32)
        sin = sb("sin", [P, S], F32)
        eps = sb("eps", [P, TT], F32)
        minus_half = sb("minus_half", [P, TT], F32)
        x = sb("x", [P, 2, TT, E], F32)
        stats = sb("stats", [P, 2, TT, 6], F32)
        mv = sb("mv", [P, 2, TT, 2], F32)
        var = sb("var", [P, 2, TT], F32)
        rstd = sb("rstd", [P, 2, TT], F32)
        xn = sb("xn", [P, 2, TT, E], F32)
        xnT = sb("xnT", [P, 2, C, S], F32)
        low = sb("low", [R, 2, S], F32)
        xc = sb("xc", [P, RING, S], F32)
        xs = sb("xs", [P, RING, S], F32)
        rot = sb("rot", [P, RING, S], F32)
        rem = sb("rem", [P, RING, S], F32)
        part = [sb(f"part{i}", [P, RING, S], BF16) for i in range(3)]
        v = sb("v", [P, 2, KVH, TT, 2 * D], F32)

        psT = [ps(f"psT{c}", [P, S]) for c in range(C)]
        psL = ps("psL", [P, S])
        psX = [ps(f"psX{i}", [P, S]) for i in range(2)]
        psR = [ps(f"psR{i}", [P, S]) for i in range(2)]
        psV = ps("psV", [P, TT, KVH, D])

        zeroed = sem("zeroed")
        loaded = sem("loaded")
        weights_pe = sem("weights_pe")
        x_in = [sem(f"x_in{k}") for k in range(2)]
        x_free = [sem(f"x_free{k}") for k in range(2)]
        dve_step = sem("dve_step")
        pool_step = sem("pool_step")
        stats_ready = sem("stats_ready")
        rstd_ready = sem("rstd_ready")
        xn_ready = sem("xn_ready")
        T_ready = sem("T_ready")
        xnT_ready = sem("xnT_ready")
        L_ready = sem("L_ready")
        low_ready = sem("low_ready")
        XR_ready = sem("XR_ready")
        XR_free = sem("XR_free")
        turned = sem("turned")
        rot_ready = sem("rot_ready")
        hi_ready = sem("hi_ready")
        rem_ready = sem("rem_ready")
        mid_ready = sem("mid_ready")
        parts_ready = sem("parts_ready")
        parts_out = [sem(f"parts_out{i}") for i in range(RING)]
        V_ready = sem("V_ready")
        V_free = sem("V_free")
        v_ready = sem("v_ready")
        v_out = [sem(f"v_out{k}") for k in range(2)]

        block = ctx.enter_context(nc.Block())

        @block.sync
        def _(sp):
            sp.wait_ge(zeroed, 2)
            sp.sem_inc(zeroed, -2)
            for dst, src in ((wa[:, :, 0:QL], a["L0_attn_Wqa"].rearrange("(c p) r -> p c r", p=P)),
                             (wa[:, :, QL:R], a["L0_attn_Wkva"].rearrange("(c p) r -> p c r", p=P)),
                             (wq[0:QL, :], a["L0_attn_Wqb"]),
                             (wkv[QL:R, :, :, :].rearrange("r k d z -> r (k d z)"), a["L0_attn_Wkvb"]),
                             (cos[:, :], a["rope"][0]), (sin[:, :], a["rope"][1]), (ident[:, :], a["ident"])):
                sp.dma_start(dst, src).then_inc(loaded, 16)
            for k in range(2):
                sp.dma_start(x[:, k], a["x"][k].rearrange("(t p) f -> p t f", p=P)).then_inc(x_in[k], 16)

            def stores(b, k):
                sp.wait_ge(v_ready, 1)
                sp.sem_inc(v_ready, -1)
                sp.dma_start(scr["v"][b].rearrange("g p n -> p g n"),
                             v[:, k].rearrange("p g t n -> p g (t n)")).then_inc(v_out[k], 16)
                for u in range(UNITS):
                    n = (k * UNITS + u) % RING
                    sp.wait_ge(parts_ready, 1)
                    sp.sem_inc(parts_ready, -1)
                    for i in range(3):
                        if u < 2:
                            sp.dma_start(scr["q"][i, u * P:(u + 1) * P, b, :], part[i][:, n, :]).then_inc(parts_out[n], 16)
                        else:
                            sp.dma_start(scr["k"][i, :, b, :], part[i][0:KW, n, :]).then_inc(parts_out[n], 16)

            with sp.Fori(0, B // 2 - 1) as it:
                for k in range(2):
                    sp.wait_ge(x_free[k], 1)
                    sp.sem_inc(x_free[k], -1)
                    sp.dma_start(x[:, k], a["x"][2 * it + (2 + k)].rearrange("(t p) f -> p t f", p=P)).then_inc(x_in[k], 16)
                for k in range(2):
                    stores(2 * it + k, k)
            for k in range(2):
                sp.wait_ge(x_free[k], 1)
                sp.sem_inc(x_free[k], -1)
            for k in range(2):
                stores(B - 2 + k, k)
            for k in range(2):
                sp.wait_ge(v_out[k], 16)
            for n in range(RING):
                sp.wait_ge(parts_out[n], 48)

        @block.vector
        def _(dve):
            nc.vector.memset(wq[:, :], 0.0).then_inc(zeroed, 1)
            nc.vector.memset(wkv[:, :, :, :], 0.0).then_inc(zeroed, 1)
            nc.vector.memset(v[:, :, :, :, :], 1.0)
            nc.vector.memset(eps[:, :], EPS)
            nc.vector.memset(minus_half[:, :], -0.5)
            dve.wait_ge(loaded, 7 * 16)
            dve.sem_inc(loaded, -(7 * 16))
            q2, s2 = (z[:, :].rearrange("r (n two) -> r n two", two=2) for z in (wq, wq_swap))
            nc.vector.tensor_copy(s2[:, :, 0], q2[:, :, 1])
            nc.vector.tensor_copy(s2[:, :, 1], q2[:, :, 0])
            for g in range(KVH):
                cols = slice(g * D, (g + 1) * D)
                src = wkv[:, g, :, 0].rearrange("r (n two) -> r n two", two=2)
                dst = wk_swap[:, cols].rearrange("r (n two) -> r n two", two=2)
                nc.vector.tensor_copy(dst[:, :, 0], src[:, :, 1])
                nc.vector.tensor_copy(dst[:, :, 1], src[:, :, 0])
                nc.vector.tensor_copy(wk[:, cols], wkv[:, g, :, 0])
                last = nc.vector.tensor_copy(wv[:, cols], wkv[:, g, :, 1])
            last.then_inc(weights_pe, 1)
            with dve.Fori(0, B // 2):
                for k in range(2):
                    dve.wait_ge(x_in[k], 16)
                    dve.sem_inc(x_in[k], -16)
                    for t in range(TT):
                        last = nc.vector.bn_stats(stats[:, k, t], x[:, k, t, :])
                    last.then_inc(dve_step, 1)
                    dve.wait_ge(dve_step, 1)
                    dve.sem_inc(dve_step, -1)
                    for t in range(TT):
                        last = nc.vector.bn_aggr(mv[:, k, t, :], stats[:, k, t])
                    last.then_inc(stats_ready, 1)
                for k in range(2):
                    dve.wait_ge(rstd_ready, 1)
                    dve.sem_inc(rstd_ready, -1)
                    for t in range(TT):
                        last = nc.vector.tensor_scalar(xn[:, k, t, :], x[:, k, t, :], mv[:, k, t, 0:1],
                                                       rstd[:, k, t:t + 1], ALU.subtract, ALU.mult)
                    last.then_inc(xn_ready, 1)
                    nc.vector.engine_nop().then_inc(x_free[k], 1)
                units = [(k, u) for k in range(2) for u in range(UNITS)]
                for step in range(len(units) + 2):
                    if step < len(units):
                        k, u = units[step]
                        n = step % RING
                        rows = P if u < 2 else KW
                        dve.wait_ge(XR_ready, 1)
                        dve.sem_inc(XR_ready, -1)
                        nc.vector.tensor_tensor(xc[0:rows, n], psX[step % 2][0:rows, :], cos[0:rows, :], ALU.mult)
                        nc.vector.tensor_tensor(xs[0:rows, n], psR[step % 2][0:rows, :], sin[0:rows, :],
                                                ALU.mult).then_inc(turned, 1)
                        nc.vector.engine_nop().then_inc(XR_free, 1)
                    if 1 <= step <= len(units):
                        n = (step - 1) % RING
                        rows = P if units[step - 1][1] < 2 else KW
                        dve.wait_ge(hi_ready, 1)
                        dve.sem_inc(hi_ready, -1)
                        nc.vector.tensor_tensor(rem[0:rows, n], rot[0:rows, n], part[0][0:rows, n],
                                                ALU.subtract).then_inc(rem_ready, 1)
                    if step >= 2:
                        n = (step - 2) % RING
                        rows = P if units[step - 2][1] < 2 else KW
                        dve.wait_ge(mid_ready, 1)
                        dve.sem_inc(mid_ready, -1)
                        nc.vector.tensor_tensor(part[2][0:rows, n], rem[0:rows, n], part[1][0:rows, n],
                                                ALU.subtract).then_inc(parts_ready, 1)

        @block.gpsimd
        def _(pool):
            with pool.Fori(0, B // 2):
                for k in range(2):
                    pool.wait_ge(stats_ready, 1)
                    pool.sem_inc(stats_ready, -1)
                    nc.gpsimd.tensor_tensor(var[:, k], mv[:, k, :, 1], eps[:, :], ALU.add).then_inc(pool_step, 1)
                    pool.wait_ge(pool_step, 1)
                    pool.sem_inc(pool_step, -1)
                    nc.gpsimd.tensor_tensor(rstd[:, k], var[:, k], minus_half[:, :], ALU.pow).then_inc(rstd_ready, 1)
                for k in range(2):
                    for u in range(UNITS):
                        n = (k * UNITS + u) % RING
                        rows = P if u < 2 else KW
                        pool.wait_ge(turned, 1)
                        pool.sem_inc(turned, -1)
                        nc.gpsimd.tensor_tensor(rot[0:rows, n], xc[0:rows, n], xs[0:rows, n],
                                                ALU.add).then_inc(rot_ready, 1)

        @block.scalar
        def _(act):
            for n in range(RING):
                act.sem_inc(parts_out[n], 48)
            for k in range(2):
                act.sem_inc(v_out[k], 16)
            with act.Fori(0, B // 2):
                for k in range(2):
                    act.wait_ge(T_ready, 1)
                    act.sem_inc(T_ready, -1)
                    nc.scalar.activation(xnT[:, k, 0, :], psT[0][:, :], ACT.Copy)
                    nc.scalar.activation(xnT[:, k, 1, :], psT[1][:, :], ACT.Copy).then_inc(xnT_ready, 1)
                for k in range(2):
                    act.wait_ge(L_ready, 1)
                    act.sem_inc(L_ready, -1)
                    nc.scalar.activation(low[:, k, :], psL[0:R, :], ACT.Copy).then_inc(low_ready, 1)
                units = [(k, u) for k in range(2) for u in range(UNITS)]
                for step in range(len(units) + 1):
                    if step < len(units):
                        k, u = units[step]
                        n = step % RING
                        rows = P if u < 2 else KW
                        if u == 0:
                            act.wait_ge(V_ready, 1)
                            act.sem_inc(V_ready, -1)
                            act.wait_ge(v_out[k], 16)
                            act.sem_inc(v_out[k], -16)
                            nc.scalar.activation(v[:, k, :, :, 0:D].rearrange("p g t d -> p t g d"), psV[:, :, :, :],
                                                 ACT.Copy).then_inc(V_free, 1)
                            act.drain().then_inc(v_ready, 1)
                        act.wait_ge(rot_ready, 1)
                        act.sem_inc(rot_ready, -1)
                        act.wait_ge(parts_out[n], 48)
                        act.sem_inc(parts_out[n], -48)
                        nc.scalar.activation(part[0][0:rows, n], rot[0:rows, n], ACT.Copy).then_inc(hi_ready, 1)
                    if step >= 1:
                        n = (step - 1) % RING
                        rows = P if units[step - 1][1] < 2 else KW
                        act.wait_ge(rem_ready, 1)
                        act.sem_inc(rem_ready, -1)
                        nc.scalar.activation(part[1][0:rows, n], rem[0:rows, n], ACT.Copy).then_inc(mid_ready, 1)

        @block.tensor
        def _(pe):
            pe.wait_ge(weights_pe, 1)
            pe.sem_inc(weights_pe, -1)
            pe.sem_inc(XR_free, 2)
            pe.sem_inc(V_free, 1)
            with pe.Fori(0, B // 2):
                for k in range(2):
                    pe.wait_ge(xn_ready, 1)
                    pe.sem_inc(xn_ready, -1)
                    if k == 1:
                        pe.wait_ge(xnT_ready, 1)
                        pe.sem_inc(xnT_ready, -1)
                    for t in range(TT):
                        for c in range(C):
                            last = nc.tensor.transpose(psT[c][:, t * P:(t + 1) * P], xn[:, k, t, c * P:(c + 1) * P],
                                                       ident[:, :])
                    last.then_inc(T_ready, 1)
                for k in range(2):
                    if k == 1:
                        pe.wait_ge(xnT_ready, 1)
                        pe.sem_inc(xnT_ready, -1)
                        pe.wait_ge(low_ready, 1)
                        pe.sem_inc(low_ready, -1)
                    for c in range(C):
                        last = nc.tensor.matmul(psL[0:R, :], wa[:, c, :], xnT[:, k, c, :], start=(c == 0), stop=(c == C - 1))
                    last.then_inc(L_ready, 1)
                for k in range(2):
                    if k == 1:
                        pe.wait_ge(low_ready, 1)
                        pe.sem_inc(low_ready, -1)
                    pe.wait_ge(V_free, 1)
                    pe.sem_inc(V_free, -1)
                    for t in range(TT):
                        last = nc.tensor.matmul(psV[:, t, :, :].rearrange("p g d -> p (g d)"), low[:, k, t * P:(t + 1) * P],
                                                wv[:, :], start=True, stop=True)
                    last.then_inc(V_ready, 1)
                    for u in range(UNITS):
                        i = (k * UNITS + u) % 2
                        rows = P if u < 2 else KW
                        w, ws = (wq[:, u * P:(u + 1) * P], wq_swap[:, u * P:(u + 1) * P]) if u < 2 else (wk[:, :], wk_swap[:, :])
                        pe.wait_ge(XR_free, 1)
                        pe.sem_inc(XR_free, -1)
                        nc.tensor.matmul(psX[i][0:rows, :], w, low[:, k, :], start=True, stop=True)
                        nc.tensor.matmul(psR[i][0:rows, :], ws, low[:, k, :], start=True, stop=True).then_inc(XR_ready, 1)


def attend_phase(nc, a, scr):
    with ExitStack() as ctx:
        def sb(name, shape, dt):
            return ctx.enter_context(nc.sbuf_tensor("p2_" + name, shape, dt))

        def ps(name, shape):
            return ctx.enter_context(nc.psum_tensor("p2_" + name, shape, F32))

        def sem(name):
            return ctx.enter_context(nc.semaphore("p2_" + name))

        ident = sb("ident", [P, P], F32)
        ident_b = sb("ident_b", [P, P], BF16)
        mask = sb("mask", [P, 2, P], F32)
        mask_b = sb("mask_b", [P, 2, P], BF16)
        qs = sb("qs", [P, 2, H, S], BF16)
        ks = sb("ks", [P, 2, KVH, S], BF16)
        v = sb("v", [P, 2, KVH, TT, 2 * D], F32)
        mx = sb("mx", [P, H, TT], F32)
        mparts = [sb(f"mpart{i}", [H * TT, P], BF16) for i in range(MROWS)]
        mrem = sb("mrem", [H * TT, P], F32)
        widths = [S - P * j for j in range(TT)]
        starts = [G * sum(widths[:j]) for j in range(TT)]
        probs = sb("probs", [P, 2, G * sum(widths)], F32)
        o = sb("o", [P, 2, S], F32)

        psA = [ps(f"psA{i}", [P, 2, S]) for i in range(2)]
        psS = [ps(f"psS{i}", [P, S]) for i in range(2)]
        psO = [ps(f"psO{i}", [P, S]) for i in range(2)]

        loaded = sem("loaded")
        consts_pe = sem("consts_pe")
        stack_in = [[sem(f"stack_in{k}_{g}") for g in range(KVH)] for k in range(2)]
        A_ready = sem("A_ready")
        A_free = sem("A_free")
        mT_ready = sem("mT_ready")
        dve_step = sem("dve_step")
        m_ready = sem("m_ready")
        m_in = [sem(f"m_in{k}") for k in range(2)]
        S_ready = sem("S_ready")
        exp_done = sem("exp_done")
        O_ready = sem("O_ready")
        o_ready = sem("o_ready")
        o_out = [sem(f"o_out{i}") for i in range(2)]

        NIN = 2 * len(PAIRS) + 1

        SUNITS = [(0, r, 1) for r in range(G)] + [(1, r, 1) for r in range(G)] + [(2, 0, 2), (2, 2, 2), (3, 0, 4)]
        LAST = [3, 7, 9, 10]
        AUNITS = [(i, rp) for i in range(TT) for rp in range(G // 2)]

        block = ctx.enter_context(nc.Block())

        @block.sync
        def _(sp):
            for dst, src in ((ident[:, :], a["ident"]), (mask[:, 0, :], a["mask"][0]), (mask[:, 1, :], a["mask"][1])):
                sp.dma_start(dst, src).then_inc(loaded, 16)

            def load(b, k, g):
                for row, (pq, pk) in enumerate(PAIRS):
                    rows = slice(row * D, (row + 1) * D)
                    sp.dma_start(qs[rows, k, g * G:(g + 1) * G, :],
                                 scr["q"][pq, g * G * D:(g + 1) * G * D, b, :].rearrange("(h d) t -> d h t", d=D)
                                 ).then_inc(stack_in[k][g], 16)
                    sp.dma_start(ks[rows, k, g, :], scr["k"][pk, g * D:(g + 1) * D, b, :]).then_inc(stack_in[k][g], 16)
                sp.dma_start(v[:, k, g].rearrange("p t n -> p (t n)"), scr["v"][b, g]).then_inc(stack_in[k][g], 16)

            def maxima(k):
                sp.wait_ge(m_ready, 1)
                sp.sem_inc(m_ready, -1)
                for i in range(MROWS):
                    row = SROWS + i
                    sp.dma_start(qs[row:row + 1, k].rearrange("o h (t q) -> o (h t) q", t=TT), mparts[i][:, :]
                                 ).then_inc(m_in[k], 16)

            def store(b, g):
                sp.wait_ge(o_ready, 1)
                sp.sem_inc(o_ready, -1)
                for r in range(G):
                    sp.dma_start(scr["o"][b, g * G + r], o[32 * r:32 * r + D + 1, g % 2, :]).then_inc(o_out[g % 2], 16)

            def batch(b, k, refill, has_next):
                for g in range(KVH):
                    if g == KVH - 1 and has_next:
                        maxima(1 - k)
                    store(b, g)
                    if refill:
                        load(b + 2, k, g)

            for k in range(2):
                for g in range(KVH):
                    load(k, k, g)
            maxima(0)
            with sp.Fori(0, B // 2 - 1) as it:
                for k in range(2):
                    batch(2 * it + k, k, True, True)
            batch(B - 2, 0, False, True)
            batch(B - 1, 1, False, False)
            for i in range(2):
                sp.wait_ge(o_out[i], 16 * G)

        @block.vector
        def _(dve):
            dve.wait_ge(loaded, 3 * 16)
            dve.sem_inc(loaded, -(3 * 16))
            nc.vector.memset(ks[SROWS:P, :, :, :], -1.0)
            nc.vector.tensor_copy(ident_b[:, :], ident[:, :])
            nc.vector.tensor_copy(mask_b[:, :, :], mask[:, :, :]).then_inc(consts_pe, 1)

            def maxima(g):
                for i, rp in AUNITS:
                    buf = (i * 2 + rp) % 2
                    h = g * G + 2 * rp
                    dve.wait_ge(A_ready, 1)
                    dve.sem_inc(A_ready, -1)
                    nc.vector.tensor_reduce(mx[:, h:h + 2, i], psA[buf][:, :, 0:P * (i + 1)], AX_X,
                                            ALU.max).then_inc(A_free, 1)

            def parts():
                dve.wait_ge(mT_ready, 1)
                dve.sem_inc(mT_ready, -1)
                mT = psA[0][0:H * TT, 0, 0:P]
                nc.vector.tensor_copy(mparts[0][:, :], mT).then_inc(dve_step, 1)
                dve.wait_ge(dve_step, 1)
                dve.sem_inc(dve_step, -1)
                nc.vector.tensor_tensor(mrem[:, :], mT, mparts[0][:, :], ALU.subtract).then_inc(dve_step, 1)
                nc.vector.engine_nop().then_inc(A_free, 2)
                dve.wait_ge(dve_step, 1)
                dve.sem_inc(dve_step, -1)
                nc.vector.tensor_copy(mparts[1][:, :], mrem[:, :]).then_inc(dve_step, 1)
                dve.wait_ge(dve_step, 1)
                dve.sem_inc(dve_step, -1)
                nc.vector.tensor_tensor(mparts[2][:, :], mrem[:, :], mparts[1][:, :], ALU.subtract).then_inc(m_ready, 1)

            def batch():
                for g in range(KVH):
                    maxima(g)
                parts()

            batch()
            with dve.Fori(0, B - 1):
                batch()

        @block.scalar
        def _(act):
            for i in range(2):
                act.sem_inc(o_out[i], 16 * G)

            def out(g):
                act.wait_ge(O_ready, 1)
                act.sem_inc(O_ready, -1)
                act.wait_ge(o_out[g % 2], 16 * G)
                act.sem_inc(o_out[g % 2], -(16 * G))
                nc.scalar.activation(o[:, g % 2, :], psO[g % 2][:, :], ACT.Copy).then_inc(o_ready, 1)

            with act.Fori(0, B):
                for g in range(KVH):
                    for s, (j, r0, n) in enumerate(SUNITS):
                        w = widths[j]
                        at = starts[j] + r0 * w
                        act.wait_ge(S_ready, 1)
                        act.sem_inc(S_ready, -1)
                        nc.scalar.activation(probs[:, g % 2, at:at + n * w], psS[(g * 11 + s) % 2][:, 0:n * w], ACT.Exp,
                                             scale=SCALE).then_inc(exp_done, 1)
                        if s == 4 and g >= 1:
                            out(g - 1)
                out(KVH - 1)

        @block.tensor
        def _(pe):
            pe.wait_ge(consts_pe, 1)
            pe.sem_inc(consts_pe, -1)
            pe.sem_inc(A_free, 2)

            def score_rows(k, g, i, rp):
                buf = (i * 2 + rp) % 2
                pe.wait_ge(A_free, 1)
                pe.sem_inc(A_free, -1)
                n = P * (i + 1)
                for z in range(2):
                    h = g * G + 2 * rp + z
                    nc.tensor.matmul(psA[buf][:, z, 0:n], qs[0:SROWS, k, h, i * P:(i + 1) * P], ks[0:SROWS, k, g, 0:n],
                                     start=True, stop=False)
                    last = nc.tensor.matmul(psA[buf][:, z, n - P:n], ident_b[:, :], mask_b[:, 0, :], start=False, stop=True)
                last.then_inc(A_ready, 1)

            def maxima():
                pe.wait_ge(A_free, 2)
                pe.sem_inc(A_free, -2)
                nc.tensor.transpose(psA[0][0:H * TT, 0, 0:P], mx[:, :, :].rearrange("p h t -> p (h t)"),
                                    ident[:, :]).then_inc(mT_ready, 1)

            def score_cols(k, g, s):
                j, r0, n = SUNITS[s]
                w = widths[j]
                bank = psS[(g * 11 + s) % 2]
                key = ks[0:SROWS + MROWS, k, g, j * P:(j + 1) * P]
                for z in range(n):
                    h = g * G + r0 + z
                    nc.tensor.matmul(bank[:, z * w:(z + 1) * w], key, qs[0:SROWS + MROWS, k, h, j * P:S],
                                     start=True, stop=False)
                    last = nc.tensor.matmul(bank[:, z * w:z * w + P], ident_b[:, :], mask_b[:, 1, :], start=False, stop=True)
                last.then_inc(S_ready, 1)

            def values(k, g, j):
                w = widths[j]
                for r in range(G):
                    at = starts[j] + r * w
                    last = nc.tensor.matmul(psO[g % 2][32 * r:32 * r + 32, j * P:S], v[:, k, g, j, :],
                                            probs[:, g % 2, at:at + w], start=(j == 0), stop=(j == TT - 1))
                if j == TT - 1:
                    last.then_inc(O_ready, 1)

            def batch(k, has_next):
                used = [0]

                def exps(n):
                    if n > used[0]:
                        pe.wait_ge(exp_done, n - used[0])
                        pe.sem_inc(exp_done, -(n - used[0]))
                        used[0] = n

                pe.wait_ge(m_in[k], 16 * MROWS)
                pe.sem_inc(m_in[k], -(16 * MROWS))
                for g in range(KVH):
                    first = g * len(SUNITS)
                    if has_next:
                        pe.wait_ge(stack_in[1 - k][g], 16 * NIN)
                        pe.sem_inc(stack_in[1 - k][g], -(16 * NIN))
                    for s in range(len(SUNITS)):
                        if first + s >= 2:
                            exps(first + s - 1)
                        score_cols(k, g, s)
                        if has_next and s < len(AUNITS):
                            score_rows(1 - k, g, *AUNITS[s])
                        if s == 1 and g >= 1:
                            for j in (2, 3):
                                exps(first - len(SUNITS) + LAST[j] + 1)
                                values(k, g - 1, j)
                        if s == 6:
                            exps(first + LAST[0] + 1)
                            values(k, g, 0)
                        if s == 9:
                            exps(first + LAST[1] + 1)
                            values(k, g, 1)
                    if g == KVH - 1 and has_next:
                        maxima()
                for j in (2, 3):
                    exps(KVH * len(SUNITS) - len(SUNITS) + LAST[j] + 1)
                    values(k, KVH - 1, j)

            for g in range(KVH):
                pe.wait_ge(stack_in[0][g], 16 * NIN)
                pe.sem_inc(stack_in[0][g], -(16 * NIN))
                for i, rp in AUNITS:
                    score_rows(0, g, i, rp)
            maxima()
            with pe.Fori(0, B // 2 - 1):
                batch(0, True)
                batch(1, True)
            batch(0, True)
            batch(1, False)


def prepare_phase(nc, a, scr, w):
    with ExitStack() as ctx:
        def sb(name, shape, dt):
            return ctx.enter_context(nc.sbuf_tensor("p3_" + name, shape, dt))

        def ps(name, shape):
            return ctx.enter_context(nc.psum_tensor("p3_" + name, shape, F32))

        def sem(name):
            return ctx.enter_context(nc.semaphore("p3_" + name))

        BT = P // CTX
        WN = 2048
        ident = sb("ident", [P, P], F32)
        ones = sb("ones", [P, P], F32)
        stage = [sb(f"stage{i}", [P, WN], F32) for i in range(2)]
        tern = sb("tern", [P, WN], F32)
        absw = sb("absw", [P, 2, WN], BF16)
        abs_sum = sb("abs_sum", [P, 2], F32)
        half = sb("half", [P, 1], F32)
        vecs = sb("vecs", [w["ncols"], P], F32)
        thr = sb("thr", [P, 1], F32)
        nthr = sb("nthr", [P, 1], F32)
        sums = sb("sums", [B * H, S], F32)
        sel = sb("sel", [P, 2, XT, P], F32)
        wk = sb("wk", [P, C, XI], F32)
        wv = sb("wv", [P, C, XI], F32)
        wo = sb("wo", [P, XT, E], F32)
        eps = sb("eps", [P, 1], F32)
        mhalf = sb("mhalf", [P, XH], F32)
        cx = sb("cx", [P, E], F32)
        stats = sb("stats", [P, 6], F32)
        mv = sb("mv", [P, 2], F32)
        var = sb("var", [P, 1], F32)
        rstd = sb("rstd", [P, 1], F32)
        cn = sb("cn", [P, E], F32)
        cnT = sb("cnT", [P, C, P], F32)
        k = sb("k", [P, XI], F32)
        v = sb("v", [P, XI], F32)
        k2 = sb("k2", [P, XI], F32)
        n2 = sb("n2", [P, XH], F32)
        rn = sb("rn", [P, XH], F32)
        bd = sb("bd", [P, XT, P], F32)
        nh = sb("nh", [P, BT, XT, E], F32R)
        nl = sb("nl", [P, BT, XT, E], F32R)

        psK = [ps(f"psK{i}", [P, S]) for i in range(2)]
        psV = [ps(f"psV{i}", [P, S]) for i in range(2)]
        psM = [ps(f"psM{i}", [P, S]) for i in range(2)]
        psN = [ps(f"psN{i}", [P, S]) for i in range(2)]

        const_in = sem("const_in")
        small_in = sem("small_in")
        cols_ready = sem("cols_ready")
        cols_done = sem("cols_done")
        stage_in = [sem(f"stage_in{i}") for i in range(2)]
        staged = sem("staged")
        stage_free = [sem(f"stage_free{i}") for i in range(2)]
        sum_pe = sem("sum_pe")
        total = sem("total")
        step = sem("step")
        tern_ready = sem("tern_ready")
        ternT_ready = sem("ternT_ready")
        ternT_free = sem("ternT_free")
        sums_in = sem("sums_in")
        rden_ready = sem("rden_ready")
        rden_out = sem("rden_out")
        ctxw_in = sem("ctxw_in")
        cx_in = sem("cx_in")
        cx_free = sem("cx_free")
        var_ready = sem("var_ready")
        rs_ready = sem("rs_ready")
        pool_step = sem("pool_step")
        cn_ready = sem("cn_ready")
        T_ready = sem("T_ready")
        cnT_ready = sem("cnT_ready")
        KV_ready = sem("KV_ready")
        k_ready = sem("k_ready")
        kn_ready = sem("kn_ready")
        M_ready = sem("M_ready")
        bd_ready = sem("bd_ready")
        N_ready = sem("N_ready")
        nh_ready = sem("nh_ready")
        nl_ready = sem("nl_ready")
        n_ready = sem("n_ready")
        n_out = sem("n_out")

        splits = [(a["L0_attn_Wout"].rearrange("(c p) n -> p c n", p=P), w["wout"]),
                  (a["L0_xattn_wq"].rearrange("(c p) n -> p c n", p=P), w["wq"]),
                  (a["L0_xattn_w1"].rearrange("(c p) n -> p c n", p=P), w["w1"]),
                  (a["L0_xattn_w2"].rearrange("(c p) n -> p c n", p=P), w["w2"])]
        terns = [(a["L0_ffn_W1"].rearrange("(c p) n -> p c n", p=P), FT, E),
                 (a["L0_ffn_W2"].rearrange("(c p) n -> p c n", p=P), C, FT * P)]

        block = ctx.enter_context(nc.Block())

        @block.sync
        def _(sp):
            sp.dma_start(ident[:, :], a["ident"]).then_inc(const_in, 16)
            sp.dma_start(sel[:, :, :, :], a["selectors"].rearrange("s t p m -> p s t m")).then_inc(const_in, 16)
            sp.dma_start(cx[:, :], a["ctx_1024"].rearrange("b s f -> (b s) f")[0:P, :]).then_inc(cx_in, 16)
            for name, at, n in w["vectors"]:
                sp.dma_start(vecs[at:at + n, :], a[name].rearrange("(c p) -> c p", p=P)).then_inc(small_in, 16)
            for i in range(2):
                src, dst = splits[i]
                n = dst[0].shape[2] * dst[0].shape[1]
                sp.dma_start(stage[i][:, 0:n].rearrange("p (c n) -> p c n", c=dst[0].shape[1]), src).then_inc(stage_in[i], 16)
            sp.dma_start(wk[:, :, :], a["L0_xattn_wk"].rearrange("(c p) n -> p c n", p=P)).then_inc(ctxw_in, 16)
            sp.dma_start(wv[:, :, :], a["L0_xattn_wv"].rearrange("(c p) n -> p c n", p=P)).then_inc(ctxw_in, 16)
            sp.dma_start(wo[:, :, :], a["L0_xattn_wo"].rearrange("(c p) n -> p c n", p=P)).then_inc(ctxw_in, 16)
            sp.dma_start(sums[:, :], scr["o"][:, :, D, :].rearrange("b h t -> (b h) t")).then_inc(sums_in, 16)
            for i in range(2, 6):
                sp.wait_ge(stage_free[i % 2], 1)
                sp.sem_inc(stage_free[i % 2], -1)
                if i < 4:
                    src, dst = splits[i]
                    cc = dst[0].shape[1]
                else:
                    src, cc, _ = terns[i - 4]
                sp.dma_start(stage[i % 2][:, :].rearrange("p (c n) -> p c n", c=cc), src).then_inc(stage_in[i % 2], 16)
            sp.wait_ge(rden_ready, 1)
            sp.sem_inc(rden_ready, -1)
            sp.dma_start(scr["rden"].rearrange("b h t -> (b h) t"), sums[:, :]).then_inc(rden_out, 16)

            def store(t):
                for z in range(BT):
                    sp.wait_ge(n_ready, 1)
                    sp.sem_inc(n_ready, -1)
                    for part, src in enumerate((nh, nl)):
                        sp.dma_start(scr["n"][BT * t + z, part], src[:, z].rearrange("p t n -> p (t n)").bitcast(F32)).then_inc(n_out, 16)

            with sp.Fori(0, B // BT - 1) as t:
                sp.wait_ge(cx_free, 1)
                sp.sem_inc(cx_free, -1)
                sp.dma_start(cx[:, :], a["ctx_1024"].rearrange("(t b) s f -> t (b s) f", b=BT)[t + 1]).then_inc(cx_in, 16)
                store(t)
            sp.wait_ge(cx_free, 1)
            sp.sem_inc(cx_free, -1)
            store(B // BT - 1)
            sp.wait_ge(rden_out, 16)
            sp.sem_inc(rden_out, -16)
            sp.wait_ge(n_out, 16 * 2 * BT)

        @block.gpsimd
        def _(pool):
            with pool.Fori(0, B // BT):
                pool.wait_ge(var_ready, 1)
                pool.sem_inc(var_ready, -1)
                nc.gpsimd.tensor_tensor(var[:, :], mv[:, 1:2], eps[:, :], ALU.add).then_inc(pool_step, 1)
                pool.wait_ge(pool_step, 1)
                pool.sem_inc(pool_step, -1)
                nc.gpsimd.tensor_tensor(rstd[:, :], var[:, :], mhalf[:, 0:1], ALU.pow).then_inc(rs_ready, 1)
                pool.wait_ge(var_ready, 1)
                pool.sem_inc(var_ready, -1)
                nc.gpsimd.tensor_tensor(rn[:, :], n2[:, :], mhalf[:, :], ALU.pow).then_inc(rs_ready, 1)

        @block.scalar
        def _(act):
            def part_of(i):
                act.wait_ge(stage_in[i % 2], 16)
                act.sem_inc(stage_in[i % 2], -16)
                if i < 4:
                    hi = splits[i][1][0]
                    n = hi.shape[1] * hi.shape[2]
                    nc.scalar.activation(hi[:, :, :].rearrange("p c n -> p (c n)"), stage[i % 2][:, 0:n], ACT.Copy).then_inc(staged, 1)
                else:
                    nc.scalar.activation(absw[:, i - 4, :], stage[i % 2][:, :], ACT.Abs, accum_out=abs_sum[:, i - 4:i - 3]).then_inc(staged, 1)

            for i in range(6):
                part_of(i)
            act.wait_ge(cols_ready, 1)
            act.sem_inc(cols_ready, -1)
            nc.scalar.activation(w["all_columns"][:, :], psN[1][:, 0:w["ncols"]], ACT.Copy).then_inc(cols_done, 1)
            act.wait_ge(cols_done, 1)
            act.sem_inc(cols_done, -1)
            act.sem_inc(n_out, 16 * 2 * BT)
            with act.Fori(0, B // BT):
                act.wait_ge(T_ready, 1)
                act.sem_inc(T_ready, -1)
                for c in range(C):
                    last = nc.scalar.activation(cnT[:, c, :], psM[0][:, c * P:(c + 1) * P], ACT.Identity,
                                                bias=w["ln1_b"][:, c:c + 1], scale=w["ln1_g"][:, c:c + 1])
                last.then_inc(cnT_ready, 1)
                act.wait_ge(KV_ready, 1)
                act.sem_inc(KV_ready, -1)
                for i in range(2):
                    nc.scalar.activation(k[:, i * S:(i + 1) * S], psK[i][:, :], ACT.Copy)
                for i in range(2):
                    last = nc.scalar.activation(v[:, i * S:(i + 1) * S], psV[i][:, :], ACT.Copy)
                last.then_inc(k_ready, 1)
                act.wait_ge(n_out, 16 * 2 * BT)
                act.sem_inc(n_out, -(16 * 2 * BT))
                for z in range(BT):
                    for i in range(XT // 2):
                        act.wait_ge(N_ready, 1)
                        act.sem_inc(N_ready, -1)
                        nc.scalar.activation(nh[:, z, 2 * i:2 * i + 2, :].rearrange("p t n -> p (t n)"), psN[i % 2][:, :],
                                             ACT.Copy).then_inc(nh_ready, 1)

        @block.vector
        def _(dve):
            nc.vector.memset(ones[:, :], 1.0)
            nc.vector.memset(eps[:, :], EPS)
            nc.vector.memset(mhalf[:, :], -0.5)
            nc.vector.memset(bd[:, :, :], 0.0)
            dve.wait_ge(const_in, 32)
            dve.sem_inc(const_in, -32)
            nc.vector.tensor_copy(w["sum_sel"][:, :, :], sel[:, 0])
            nc.vector.tensor_copy(w["spread_sel"][:, :, :], sel[:, 1])
            for i in range(4):
                hi, lo = splits[i][1]
                n = hi.shape[1] * hi.shape[2]
                dve.wait_ge(staged, 1)
                dve.sem_inc(staged, -1)
                nc.vector.tensor_tensor(lo[:, :, :].rearrange("p c n -> p (c n)"), stage[i % 2][:, 0:n],
                                        hi[:, :, :].rearrange("p c n -> p (c n)").bitcast(F32), ALU.subtract).then_inc(stage_free[i % 2], 1)
            dve.wait_ge(sums_in, 16)
            dve.sem_inc(sums_in, -16)
            nc.vector.reciprocal(sums[:, :], sums[:, :]).then_inc(rden_ready, 1)
            for i, (_, cc, nn) in enumerate(terns):
                dve.wait_ge(staged, 1)
                dve.sem_inc(staged, -1)
                nc.vector.engine_nop().then_inc(sum_pe, 1)
                dve.wait_ge(total, 1)
                dve.sem_inc(total, -1)
                nc.vector.tensor_scalar(thr[:, :], psN[0][:, 0:1], 1.0 / (cc * nn * P), 1e-8, ALU.mult, ALU.max).then_inc(step, 1)
                dve.wait_ge(step, 1)
                dve.sem_inc(step, -1)
                nc.vector.tensor_scalar(nthr[:, :], thr[:, :], -0.5, None, ALU.mult)
                nc.vector.tensor_scalar(half[:, :], thr[:, :], 0.5, None, ALU.mult).then_inc(step, 1)
                dve.wait_ge(step, 1)
                dve.sem_inc(step, -1)
                wst = stage[i % 2]
                nc.vector.tensor_scalar(tern[:, :], wst[:, :], nthr[:, 0:1], None, ALU.is_lt).then_inc(step, 1)
                dve.wait_ge(step, 1)
                dve.sem_inc(step, -1)
                nc.vector.scalar_tensor_tensor(out=tern[:, :], in0=wst[:, :], scalar=half[:, 0:1], in1=tern[:, :],
                                               op0=ALU.is_gt, op1=ALU.subtract).then_inc(tern_ready, 1)
                for q in range(4):
                    dve.wait_ge(ternT_ready, 1)
                    dve.sem_inc(ternT_ready, -1)
                    src = psM[q % 2] if q < 2 else psK[q % 2]
                    if i == 0:
                        dst = w["t1"][:, :, 2 * q * P:(2 * q + 2) * P]
                        s = src[:, :].rearrange("p (c n) -> p c n", c=C)
                    else:
                        dst = w["t2"][:, 2 * q:2 * q + 2, :]
                        s = src[:, :].rearrange("p (t n) -> p t n", t=2)
                    last = nc.vector.tensor_copy(dst, s)
                last.then_inc(ternT_free, 1)
            with dve.Fori(0, B // BT):
                dve.wait_ge(cx_in, 16)
                dve.sem_inc(cx_in, -16)
                nc.vector.bn_stats(stats[:, :], cx[:, :]).then_inc(step, 1)
                dve.wait_ge(step, 1)
                dve.sem_inc(step, -1)
                nc.vector.bn_aggr(mv[:, :], stats[:, :]).then_inc(var_ready, 1)
                dve.wait_ge(rs_ready, 1)
                dve.sem_inc(rs_ready, -1)
                nc.vector.tensor_scalar(cn[:, :], cx[:, :], mv[:, 0:1], rstd[:, 0:1], ALU.subtract, ALU.mult).then_inc(cn_ready, 1)
                nc.vector.engine_nop().then_inc(cx_free, 1)
                dve.wait_ge(k_ready, 1)
                dve.sem_inc(k_ready, -1)
                nc.vector.tensor_tensor(k2[:, :], k[:, :], k[:, :], ALU.mult).then_inc(step, 1)
                dve.wait_ge(step, 1)
                dve.sem_inc(step, -1)
                nc.vector.tensor_reduce(n2[:, :], k2[:, :].rearrange("p (h d) -> p h d", h=XH), AX_X, ALU.add).then_inc(step, 1)
                dve.wait_ge(step, 1)
                dve.sem_inc(step, -1)
                nc.vector.tensor_scalar(n2[:, :], n2[:, :], 1e-24, None, ALU.max).then_inc(var_ready, 1)
                dve.wait_ge(rs_ready, 1)
                dve.sem_inc(rs_ready, -1)
                nc.vector.tensor_tensor(k[:, :].rearrange("p (h d) -> p h d", h=XH), k[:, :].rearrange("p (h d) -> p h d", h=XH),
                                        rn[:, :].unsqueeze(2).broadcast_to([P, XH, XD]), ALU.mult).then_inc(kn_ready, 1)
                for z in range(BT):
                    dve.wait_ge(M_ready, 1)
                    dve.sem_inc(M_ready, -1)
                    for i in range(2):
                        m = psM[i][:, :].rearrange("p (t n) -> p t n", t=4)
                        for side in range(2):
                            r = slice(side * XD, (side + 1) * XD)
                            last = nc.vector.tensor_copy(bd[r, 4 * i:4 * i + 4, r], m[r, :, r])
                    last.then_inc(bd_ready, 1)
                    for i in range(XT // 2):
                        dve.wait_ge(nh_ready, 1)
                        dve.sem_inc(nh_ready, -1)
                        sl = nh[:, z, 2 * i:2 * i + 2, :].rearrange("p t n -> p (t n)").bitcast(F32)
                        nc.vector.tensor_tensor(nl[:, z, 2 * i:2 * i + 2, :].rearrange("p t n -> p (t n)"), psN[i % 2][:, :], sl,
                                                ALU.subtract).then_inc(nl_ready, 1)
                    nc.vector.engine_nop().then_inc(n_ready, 1)

        @block.tensor
        def _(pe):
            for i, (_, cc, nn) in enumerate(terns):
                pe.wait_ge(sum_pe, 1)
                pe.sem_inc(sum_pe, -1)
                nc.tensor.matmul(psN[0][:, 0:1], ones[:, :], abs_sum[:, i:i + 1], start=True, stop=True).then_inc(total, 1)
                pe.wait_ge(tern_ready, 1)
                pe.sem_inc(tern_ready, -1)
                t = tern[:, :].rearrange("p (c n) -> p c n", c=cc)
                for q in range(4):
                    dst = psM[q % 2] if q < 2 else psK[q % 2]
                    for y in range(2):
                        for c in range(C):
                            if i == 0:
                                out, src = dst[:, (c * 2 + y) * P:(c * 2 + y + 1) * P], t[:, 2 * q + y, c * P:(c + 1) * P]
                            else:
                                out, src = dst[:, (y * 2 + c) * P:(y * 2 + c + 1) * P], t[:, c, (2 * q + y) * P:(2 * q + y + 1) * P]
                            last = nc.tensor.transpose(out, src, ident[:, :])
                    last.then_inc(ternT_ready, 1)
                pe.wait_ge(ternT_free, 1)
                pe.sem_inc(ternT_free, -1)
            pe.wait_ge(small_in, 16 * len(w["vectors"]))
            pe.sem_inc(small_in, -(16 * len(w["vectors"])))
            nc.tensor.transpose(psN[1][:, 0:w["ncols"]], vecs[0:w["ncols"], :], ident[0:w["ncols"], 0:w["ncols"]]).then_inc(cols_ready, 1)
            pe.wait_ge(ctxw_in, 48)
            pe.sem_inc(ctxw_in, -48)
            with pe.Fori(0, B // BT):
                pe.wait_ge(cn_ready, 1)
                pe.sem_inc(cn_ready, -1)
                for c in range(C):
                    last = nc.tensor.transpose(psM[0][:, c * P:(c + 1) * P], cn[:, c * P:(c + 1) * P], ident[:, :])
                last.then_inc(T_ready, 1)
                pe.wait_ge(cnT_ready, 1)
                pe.sem_inc(cnT_ready, -1)
                for bank, weight in ((psK, wk), (psV, wv)):
                    for i in range(2):
                        for c in range(C):
                            last = nc.tensor.matmul(bank[i][:, :], cnT[:, c, :], weight[:, c, i * S:(i + 1) * S],
                                                    start=(c == 0), stop=(c == C - 1))
                last.then_inc(KV_ready, 1)
                pe.wait_ge(kn_ready, 1)
                pe.sem_inc(kn_ready, -1)
                for z in range(BT):
                    rows = slice(z * CTX, (z + 1) * CTX)
                    for t in range(XT):
                        cols = slice(t * P, (t + 1) * P)
                        last = nc.tensor.matmul(psM[t // 4][:, (t % 4) * P:(t % 4 + 1) * P], v[rows, cols], k[rows, cols],
                                                start=True, stop=True)
                    last.then_inc(M_ready, 1)
                    pe.wait_ge(bd_ready, 1)
                    pe.sem_inc(bd_ready, -1)
                    for i in range(XT // 2):
                        if i >= 2:
                            pe.wait_ge(nl_ready, 1)
                            pe.sem_inc(nl_ready, -1)
                        for y in range(2):
                            last = nc.tensor.matmul(psN[i % 2][:, y * E:(y + 1) * E], bd[:, 2 * i + y, :], wo[:, 2 * i + y, :],
                                                    start=True, stop=True)
                        last.then_inc(N_ready, 1)
                    pe.wait_ge(nl_ready, 2)
                    pe.sem_inc(nl_ready, -2)


def mix_phase(nc, a, scr, w, out):
    with ExitStack() as ctx:
        def sb(name, shape, dt):
            return ctx.enter_context(nc.sbuf_tensor("p4_" + name, shape, dt))

        def ps(name, shape):
            return ctx.enter_context(nc.psum_tensor("p4_" + name, shape, F32))

        def sem(name):
            return ctx.enter_context(nc.semaphore("p4_" + name))

        RING = 3
        ident = sb("ident", [P, P], F32)
        eps = sb("eps", [P, TT], F32)
        mhalf = sb("mhalf", [P, TT], F32)
        o = sb("o", [P, C, S], F32)
        rden = sb("rden", [P, C, S], F32)
        xin = sb("xin", [P, TT, E], F32)
        x1 = sb("x1", [P, TT, E], F32)
        q0 = sb("q0", [P, TT, E], F32)
        z = sb("z", [P, TT, E], F32)
        base = sb("base", [P, TT, E], F32)
        x2 = sb("x2", [P, TT, E], F32)
        stats = sb("stats", [P, TT, 6], F32)
        mv = sb("mv", [P, TT, 2], F32)
        var = sb("var", [P, TT], F32)
        rstd = sb("rstd", [P, TT], F32)
        feat_f = sb("feat_f", [P, C, S], F32)
        feat_b = sb("feat_b", [P, C, S], F32)
        fh, fl = sb("fh", [P, C, S], F32R), sb("fl", [P, C, S], F32R)
        bh, bl = sb("bh", [P, C, S], F32R), sb("bl", [P, C, S], F32R)
        q = sb("q", [P, XT, S], F32)
        sq = sb("sq", [P, RING, S], F32)
        sh, sl = sb("sh", [P, RING, S], F32R), sb("sl", [P, RING, S], F32R)
        n2 = sb("n2", [XH * 4, S], F32)
        rstack = sb("rstack", [P, S], F32R)
        h = sb("h", [P, RING, S], F32)
        hh, hl = sb("hh", [P, RING, S], F32R), sb("hl", [P, RING, S], F32R)
        nw = [sb(f"n{i}", [P, XT, E], F32R) for i in range(2)]

        psG = [ps(f"psG{i}", [P, S]) for i in range(RING)]
        psY = [ps(f"psY{i}", [P, S]) for i in range(C)]
        psT = [ps(f"psT{i}", [P, S]) for i in range(C)]
        psN = ps("psN", [P, S])

        const_in = sem("const_in")
        consts = sem("consts")
        o_in = sem("o_in")
        o_free = sem("o_free")
        x_in = sem("x_in")
        x_free = sem("x_free")
        n_in = sem("n_in")
        n_free = sem("n_free")
        out_ready = sem("out_ready")
        out_done = sem("out_done")
        o_parts = sem("o_parts")
        step = sem("step")
        pool_step = sem("pool_step")
        var_ready = sem("var_ready")
        rs_ready = sem("rs_ready")
        z_ready = sem("z_ready")
        Y_ready = sem("Y_ready")
        feat_ready = sem("feat_ready")
        T_ready = sem("T_ready")
        u_ready = sem("u_ready")
        u_parts = sem("u_parts")
        tok_ready = sem("tok_ready")
        tok_free = sem("tok_free")
        q_ready = sem("q_ready")
        sq_ready = sem("sq_ready")
        sq_parts = sem("sq_parts")
        n2_ready = sem("n2_ready")
        n2_act = sem("n2_act")
        norm_ready = sem("norm_ready")
        rn_ready = sem("rn_ready")
        g_ready = sem("g_ready")
        h_ready = sem("h_ready")
        h_parts = sem("h_parts")
        s_ready = sem("s_ready")
        qn_ready = sem("qn_ready")
        qh_ready = sem("qh_ready")
        qn_parts = sem("qn_parts")

        out_ap = out

        block = ctx.enter_context(nc.Block())

        @block.sync
        def _(sp):
            def load_o(b):
                for c in range(C):
                    for i in range(8):
                        hd = c * 8 + i
                        sp.dma_start(o[i * D:(i + 1) * D, c, :], scr["o"][b, hd, 0:D, :]).then_inc(o_in, 16)
                        sp.dma_start(rden[i * D:(i + 1) * D, c, :],
                                     scr["rden"][b, hd:hd + 1, :].broadcast_to([D, S])).then_inc(o_in, 16)

            def load_x(b):
                sp.dma_start(xin[:, :, :], a["x"][b].rearrange("(t p) f -> p t f", p=P)).then_inc(x_in, 16)

            def load_n(b):
                for i in range(2):
                    sp.dma_start(nw[i][:, :, :].rearrange("p t n -> p (t n)").bitcast(F32), scr["n"][b, i]).then_inc(n_in, 16)

            def store(b):
                sp.wait_ge(out_ready, 1)
                sp.sem_inc(out_ready, -1)
                sp.dma_start(out_ap[b].rearrange("(t p) f -> p t f", p=P), x2[:, :, :]).then_inc(out_done, 16)

            def round_(b, back, more):
                if more:
                    sp.wait_ge(o_free, 1)
                    sp.sem_inc(o_free, -1)
                    load_o(b + 1)
                    sp.wait_ge(x_free, 1)
                    sp.sem_inc(x_free, -1)
                    load_x(b + 1)
                if back:
                    store(b - 1)
                if more:
                    sp.wait_ge(n_free, 1)
                    sp.sem_inc(n_free, -1)
                    load_n(b + 1)

            sp.dma_start(ident[:, :], a["ident"]).then_inc(const_in, 16)
            load_o(0)
            load_x(0)
            load_n(0)
            round_(0, False, True)
            with sp.Fori(1, B - 1) as b:
                round_(b, True, True)
            round_(B - 1, True, False)
            sp.wait_ge(x_free, 1)
            sp.sem_inc(x_free, -1)
            sp.wait_ge(n_free, 1)
            sp.sem_inc(n_free, -1)
            store(B - 1)
            sp.wait_ge(out_done, 16)

        @block.gpsimd
        def _(pool):
            def rsqrt():
                pool.wait_ge(var_ready, 1)
                pool.sem_inc(var_ready, -1)
                nc.gpsimd.tensor_tensor(var[:, :], mv[:, :, 1], eps[:, :], ALU.add).then_inc(pool_step, 1)
                pool.wait_ge(pool_step, 1)
                pool.sem_inc(pool_step, -1)
                nc.gpsimd.tensor_tensor(rstd[:, :], var[:, :], mhalf[:, :], ALU.pow).then_inc(rs_ready, 1)

            for _i in range(3):
                rsqrt()
            with pool.Fori(1, B):
                for _i in range(4):
                    rsqrt()
            rsqrt()

        @block.scalar
        def _(act):
            def evacuate(dst, bias):
                act.wait_ge(Y_ready, 1)
                act.sem_inc(Y_ready, -1)
                for c in range(C):
                    last = nc.scalar.activation(dst[:, c, :], psY[c][:, :], ACT.Identity, bias=bias[:, c:c + 1])
                last.then_inc(feat_ready, 1)

            def affine(dst, g, b):
                act.wait_ge(T_ready, 1)
                act.sem_inc(T_ready, -1)
                for c in range(C):
                    last = nc.scalar.activation(dst[:, c, :], psT[c][:, :], ACT.Identity, bias=b[:, c:c + 1], scale=g[:, c:c + 1])
                last.then_inc(u_ready, 1)

            def gelu(bias):
                for m in range(FT):
                    act.wait_ge(g_ready, 1)
                    act.sem_inc(g_ready, -1)
                    nc.scalar.activation(h[:, m % RING, :], psG[m % RING][:, :], ACT.Gelu, bias=bias[:, m:m + 1]).then_inc(h_ready, 1)

            def round_(front, back):
                if front:
                    evacuate(feat_f, w["bout"])
                if back:
                    affine(feat_b, w["ln2_g"], w["ln2_b"])
                    gelu(w["b1"])
                    evacuate(feat_b, w["b2"])
                if front:
                    affine(feat_f, w["ln1_g"], w["ln1_b"])
                    for m in range(XT):
                        act.wait_ge(q_ready, 1)
                        act.sem_inc(q_ready, -1)
                        nc.scalar.activation(q[:, m, :], psG[m % RING][:, :], ACT.Copy)
                        nc.scalar.activation(sq[:, m % RING, :], psG[m % RING][:, :], ACT.Square).then_inc(sq_ready, 1)
                if back:
                    act.wait_ge(T_ready, 1)
                    act.sem_inc(T_ready, -1)
                    for c in range(C):
                        last = nc.scalar.activation(bh[:, c, :], psT[c][:, :], ACT.Copy)
                    last.then_inc(u_ready, 1)
                if front:
                    act.wait_ge(n2_act, 1)
                    act.sem_inc(n2_act, -1)
                    nc.scalar.activation(n2[:, :], n2[:, :], ACT.Sqrt).then_inc(norm_ready, 1)
                if back:
                    gelu(w["fb1"])
                    evacuate(feat_b, w["fb2"])
                if front:
                    for m in range(XT):
                        act.wait_ge(qn_ready, 1)
                        act.sem_inc(qn_ready, -1)
                        nc.scalar.activation(sh[:, m % RING, :], sq[:, m % RING, :], ACT.Copy).then_inc(qh_ready, 1)
                    evacuate(feat_f, w["bo"])

            round_(True, False)
            with act.Fori(1, B):
                round_(True, True)
            round_(False, True)

        @block.vector
        def _(dve):
            flat = "p c n -> p (c n)"

            def prepare_o():
                dve.wait_ge(o_in, 16 * 2 * H)
                dve.sem_inc(o_in, -(16 * 2 * H))
                nc.vector.tensor_tensor(o[:, :, :], o[:, :, :], rden[:, :, :], ALU.mult).then_inc(step, 1)
                dve.wait_ge(step, 1)
                dve.sem_inc(step, -1)
                nc.vector.tensor_copy(fh[:, :, :], o[:, :, :]).then_inc(step, 1)
                dve.wait_ge(step, 1)
                dve.sem_inc(step, -1)
                nc.vector.tensor_tensor(fl[:, :, :], o[:, :, :], fh[:, :, :].bitcast(F32), ALU.subtract).then_inc(o_parts, 1)
                nc.vector.engine_nop().then_inc(o_free, 1)

            def variance(src):
                for t in range(TT):
                    last = nc.vector.bn_stats(stats[:, t], src[:, t, :])
                last.then_inc(step, 1)
                dve.wait_ge(step, 1)
                dve.sem_inc(step, -1)
                for t in range(TT):
                    last = nc.vector.bn_aggr(mv[:, t, :], stats[:, t])
                last.then_inc(var_ready, 1)

            def normalise(dst, src, sem_):
                dve.wait_ge(rs_ready, 1)
                dve.sem_inc(rs_ready, -1)
                for t in range(TT):
                    last = nc.vector.tensor_scalar(dst[:, t, :], src[:, t, :], mv[:, t, 0:1], rstd[:, t:t + 1],
                                                   ALU.subtract, ALU.mult)
                last.then_inc(sem_, 1)

            def parts(hi, lo, src):
                dve.wait_ge(u_ready, 1)
                dve.sem_inc(u_ready, -1)
                nc.vector.tensor_copy(hi[:, :, :], src[:, :, :]).then_inc(step, 1)
                dve.wait_ge(step, 1)
                dve.sem_inc(step, -1)
                nc.vector.tensor_tensor(lo[:, :, :], src[:, :, :], hi[:, :, :].bitcast(F32), ALU.subtract).then_inc(u_parts, 1)

            def add_back(dst, src, banks, sem_):
                dve.wait_ge(tok_ready, 1)
                dve.sem_inc(tok_ready, -1)
                for i in range(2):
                    last = nc.vector.tensor_tensor(dst[:, 2 * i:2 * i + 2, :].rearrange("p t n -> p (t n)"), banks[i][:, :],
                                                   src[:, 2 * i:2 * i + 2, :].rearrange("p t n -> p (t n)"), ALU.add)
                last.then_inc(sem_, 1)
                nc.vector.engine_nop().then_inc(tok_free, 1)

            def hidden(m):
                s = m % RING
                dve.wait_ge(h_ready, 1)
                dve.sem_inc(h_ready, -1)
                nc.vector.tensor_copy(hh[:, s, :], h[:, s, :]).then_inc(step, 1)
                dve.wait_ge(step, 1)
                dve.sem_inc(step, -1)
                nc.vector.tensor_tensor(hl[:, s, :], h[:, s, :], hh[:, s, :].bitcast(F32), ALU.subtract).then_inc(h_parts, 1)

            def square(m):
                s = m % RING
                dve.wait_ge(sq_ready, 1)
                dve.sem_inc(sq_ready, -1)
                nc.vector.tensor_copy(sh[:, s, :], sq[:, s, :]).then_inc(step, 1)
                dve.wait_ge(step, 1)
                dve.sem_inc(step, -1)
                nc.vector.tensor_tensor(sl[:, s, :], sq[:, s, :], sh[:, s, :].bitcast(F32), ALU.subtract).then_inc(sq_parts, 1)

            def inverse_norms():
                dve.wait_ge(norm_ready, 1)
                dve.sem_inc(norm_ready, -1)
                nc.vector.reciprocal(n2[:, :], n2[:, :]).then_inc(step, 1)
                dve.wait_ge(step, 1)
                dve.sem_inc(step, -1)
                nc.vector.tensor_copy(rstack[0:XH, :], n2[0:XH, :])
                nc.vector.tensor_copy(rstack[32:32 + XH, :], n2[32:32 + XH, :]).then_inc(step, 1)
                dve.wait_ge(step, 1)
                dve.sem_inc(step, -1)
                nc.vector.tensor_tensor(rstack[32:32 + XH, :], n2[32:32 + XH, :], rstack[32:32 + XH, :].bitcast(F32),
                                        ALU.subtract).then_inc(rn_ready, 1)

            def interleave(tiles, tile, extras):
                for m in range(tiles):
                    tile(m)
                    for f in extras.get(m, ()):
                        f()

            def round_(front, back, more, x2_free):
                def norm_again():
                    normalise(q0, x1, step)
                    dve.wait_ge(step, 1)
                    dve.sem_inc(step, -1)
                    variance(q0)

                mlp = {}
                if back:
                    parts(bh, bl, feat_b)
                if front:
                    dve.wait_ge(x_in, 16)
                    dve.sem_inc(x_in, -16)
                    add_back(x1, xin, psG, step)
                    dve.wait_ge(step, 1)
                    dve.sem_inc(step, -1)
                    nc.vector.engine_nop().then_inc(x_free, 1)
                    variance(x1)
                    mlp = {0: [norm_again],
                           2: [lambda: normalise(z, q0, z_ready)]}
                interleave(FT, hidden if back else (lambda m: None), mlp)
                if front:
                    parts(fh, fl, feat_f)
                if back:
                    if x2_free:
                        dve.wait_ge(out_done, 16)
                        dve.sem_inc(out_done, -16)
                    add_back(x2, base, psG, step)
                    dve.wait_ge(step, 1)
                    dve.sem_inc(step, -1)
                    variance(x2)
                extra = {1: [lambda: normalise(z, x2, z_ready)]} if back else {}
                interleave(XT, square if front else (lambda m: None), extra)
                if front:
                    dve.wait_ge(n2_ready, 1)
                    dve.sem_inc(n2_ready, -1)
                    nc.vector.tensor_scalar(n2[:, :], psN[0:XH * 4, :], 1e-24, None, ALU.max).then_inc(n2_act, 1)
                if back:
                    dve.wait_ge(u_ready, 1)
                    dve.sem_inc(u_ready, -1)
                    for c in range(C):
                        last = nc.vector.tensor_tensor(bl[:, c, :], psT[c][:, :], bh[:, c, :].bitcast(F32), ALU.subtract)
                    last.then_inc(u_parts, 1)
                extra = {}
                if front:
                    extra[1] = [inverse_norms]
                if more:
                    extra[4] = [prepare_o]
                interleave(FT, hidden if back else (lambda m: None), extra)
                if front:
                    for m in range(XT + 1):
                        if m < XT:
                            dve.wait_ge(s_ready, 1)
                            dve.sem_inc(s_ready, -1)
                            nc.vector.tensor_tensor(sq[:, m % RING, :], psG[m % RING][:, :], q[:, m, :], ALU.mult).then_inc(qn_ready, 1)
                        if m >= 1:
                            s = (m - 1) % RING
                            dve.wait_ge(qh_ready, 1)
                            dve.sem_inc(qh_ready, -1)
                            nc.vector.tensor_tensor(sl[:, s, :], sq[:, s, :], sh[:, s, :].bitcast(F32), ALU.subtract).then_inc(qn_parts, 1)
                        if m == 3 and back:
                            add_back(x2, x2, psT, out_ready)
                    add_back(q0, q0, psG, step)
                    dve.wait_ge(step, 1)
                    dve.sem_inc(step, -1)
                    variance(q0)
                    nc.vector.tensor_tensor(base[:, :, :], x1[:, :, :], q0[:, :, :], ALU.add)
                    nc.vector.engine_nop().then_inc(n_free, 1)
                    normalise(z, q0, z_ready)
                elif back:
                    add_back(x2, x2, psT, out_ready)

            nc.vector.memset(eps[:, :], EPS)
            nc.vector.memset(mhalf[:, :], -0.5)
            nc.vector.memset(n2[:, :], 1.0)
            nc.vector.memset(rstack[:, :].bitcast(F32), 0.0).then_inc(step, 1)
            dve.wait_ge(step, 1)
            dve.sem_inc(step, -1)
            dve.wait_ge(const_in, 16)
            dve.sem_inc(const_in, -16)
            nc.vector.engine_nop().then_inc(consts, 1)
            prepare_o()
            round_(True, False, True, False)
            round_(True, True, True, False)
            with dve.Fori(2, B - 1):
                round_(True, True, True, True)
            round_(True, True, False, True)
            round_(False, True, False, True)

        @block.tensor
        def _(pe):
            def product(bank, hi, lo, whi, wlo, start, stop):
                terms = [(whi, hi), (whi, lo)] + ([(wlo, hi)] if wlo is not None else [])
                for i, (ww, xx) in enumerate(terms):
                    last = nc.tensor.matmul(bank, ww, xx, start=start and i == 0, stop=stop and i == len(terms) - 1)
                return last

            def transpose_rows():
                pe.wait_ge(z_ready, 1)
                pe.sem_inc(z_ready, -1)
                for t in range(TT):
                    for c in range(C):
                        last = nc.tensor.transpose(psT[c][:, t * P:(t + 1) * P], z[:, t, c * P:(c + 1) * P], ident[:, :])
                last.then_inc(T_ready, 1)

            def transpose_back(src, banks):
                pe.wait_ge(feat_ready, 1)
                pe.sem_inc(feat_ready, -1)
                for t in range(TT):
                    for c in range(C):
                        at = ((t % 2) * C + c) * P
                        last = nc.tensor.transpose(banks[t // 2][:, at:at + P], src[:, c, t * P:(t + 1) * P], ident[:, :])
                last.then_inc(tok_ready, 1)

            def mlp(w1, w2):
                pe.wait_ge(u_parts, 1)
                pe.sem_inc(u_parts, -1)
                for m in range(FT + RING):
                    if m >= RING:
                        k = m - RING
                        pe.wait_ge(h_parts, 1)
                        pe.sem_inc(h_parts, -1)
                        for c in range(C):
                            cols = slice(c * P, (c + 1) * P)
                            last = product(psY[c][:, :], hh[:, k % RING, :], hl[:, k % RING, :], w2[0][:, k, cols],
                                           w2[1][:, k, cols] if w2[1] is not None else None, k == 0, k == FT - 1)
                    if m < FT:
                        cols = slice(m * P, (m + 1) * P)
                        for c in range(C):
                            tile = product(psG[m % RING][:, :], bh[:, c, :], bl[:, c, :], w1[0][:, c, cols],
                                           w1[1][:, c, cols] if w1[1] is not None else None, c == 0, c == C - 1)
                        tile.then_inc(g_ready, 1)
                last.then_inc(Y_ready, 1)

            def round_(front, back):
                if front:
                    pe.wait_ge(o_parts, 1)
                    pe.sem_inc(o_parts, -1)
                    for c in range(C):
                        for k in range(C):
                            cols = slice(c * P, (c + 1) * P)
                            last = product(psY[c][:, :], fh[:, k, :], fl[:, k, :], w["wout"][0][:, k, cols],
                                           w["wout"][1][:, k, cols], k == 0, k == C - 1)
                    last.then_inc(Y_ready, 1)
                if back:
                    transpose_rows()
                if front:
                    transpose_back(feat_f, psG)
                    pe.wait_ge(tok_free, 1)
                    pe.sem_inc(tok_free, -1)
                if back:
                    mlp(w["w1"], w["w2"])
                if front:
                    transpose_rows()
                if back:
                    transpose_back(feat_b, psG)
                    pe.wait_ge(tok_free, 1)
                    pe.sem_inc(tok_free, -1)
                if front:
                    pe.wait_ge(u_parts, 1)
                    pe.sem_inc(u_parts, -1)
                    for m in range(XT + RING):
                        if m >= RING:
                            k = m - RING
                            pe.wait_ge(sq_parts, 1)
                            pe.sem_inc(sq_parts, -1)
                            nc.tensor.matmul(psN[:, :], w["sum_sel"][:, k, :], sh[:, k % RING, :], start=(k == 0), stop=False)
                            last = nc.tensor.matmul(psN[:, :], w["sum_sel"][:, k, :], sl[:, k % RING, :], start=False, stop=(k == XT - 1))
                        if m < XT:
                            cols = slice(m * P, (m + 1) * P)
                            for c in range(C):
                                tile = product(psG[m % RING][:, :], fh[:, c, :], fl[:, c, :], w["wq"][0][:, c, cols],
                                               w["wq"][1][:, c, cols], c == 0, c == C - 1)
                            tile.then_inc(q_ready, 1)
                    last.then_inc(n2_ready, 1)
                if back:
                    transpose_rows()
                    mlp((w["t1"], None), (w["t2"], None))
                if front:
                    pe.wait_ge(rn_ready, 1)
                    pe.sem_inc(rn_ready, -1)
                    pe.wait_ge(n_in, 32)
                    pe.sem_inc(n_in, -32)
                    if back:
                        transpose_back(feat_b, psT)
                    for m in range(XT + RING):
                        if m >= RING:
                            k = m - RING
                            pe.wait_ge(qn_parts, 1)
                            pe.sem_inc(qn_parts, -1)
                            for c in range(C):
                                cols = slice(c * P, (c + 1) * P)
                                last = product(psY[c][:, :], sh[:, k % RING, :], sl[:, k % RING, :], nw[0][:, k, cols],
                                               nw[1][:, k, cols], k == 0, k == XT - 1)
                        if m < XT:
                            nc.tensor.matmul(psG[m % RING][:, :], w["spread_sel"][:, m, :], rstack[:, :], start=True,
                                             stop=True).then_inc(s_ready, 1)
                    last.then_inc(Y_ready, 1)
                    if back:
                        pe.wait_ge(tok_free, 1)
                        pe.sem_inc(tok_free, -1)
                    transpose_back(feat_f, psG)
                    pe.wait_ge(tok_free, 1)
                    pe.sem_inc(tok_free, -1)
                elif back:
                    transpose_back(feat_b, psT)
                    pe.wait_ge(tok_free, 1)
                    pe.sem_inc(tok_free, -1)

            pe.wait_ge(consts, 1)
            pe.sem_inc(consts, -1)
            round_(True, False)
            with pe.Fori(1, B):
                round_(True, True)
            round_(False, True)


def decoder_block(nc, a, out):
    def dram(name, shape, dt=F32):
        return nc.dram_tensor(name, shape, dt).ap()

    scr = {"q": dram("q_parts", [3, H * D, B, S], BF16), "k": dram("k_parts", [3, KVH * D, B, S], BF16),
           "v": dram("v_ones", [B, KVH, P, TT * 2 * D]), "o": dram("o_sums", [B, H, D + 1, S]),
           "rden": dram("rden", [B, H, S]), "n": dram("n_parts", [B, 2, P, XT * E])}
    project_phase(nc, a, scr)
    attend_phase(nc, a, scr)
    mlp_block(nc, a, scr, out)


def mlp_block(nc, a, scr, out):
    with ExitStack() as ctx:
        def sb(name, shape, dt):
            return ctx.enter_context(nc.sbuf_tensor("w_" + name, shape, dt))

        w = {name: (sb(name + "_hi", [P, k, n], F32R), sb(name + "_lo", [P, k, n], F32R))
             for name, k, n in (("wout", C, E), ("wq", C, XI), ("w1", C, FT * P), ("w2", FT, E))}
        w["t1"] = sb("t1", [P, C, FT * P], F32R)
        w["t2"] = sb("t2", [P, FT, E], F32R)
        w["sum_sel"] = sb("sum_sel", [P, XT, P], F32R)
        w["spread_sel"] = sb("spread_sel", [P, XT, P], F32R)
        vectors = (("bout", "L0_attn_bout", C), ("ln1_g", "L0_xattn_ln1_g", C), ("ln1_b", "L0_xattn_ln1_b", C),
                   ("ln2_g", "L0_xattn_ln2_g", C), ("ln2_b", "L0_xattn_ln2_b", C), ("bo", "L0_xattn_bo", C),
                   ("b1", "L0_xattn_b1", FT), ("b2", "L0_xattn_b2", C), ("fb1", "L0_ffn_b1", FT), ("fb2", "L0_ffn_b2", C))
        w["ncols"] = sum(k for _, _, k in vectors)
        w["all_columns"] = sb("columns", [P, w["ncols"]], F32)
        w["vectors"] = []
        at = 0
        for name, source, k in vectors:
            w[name] = w["all_columns"][:, at:at + k]
            w["vectors"].append((source, at, k))
            at += k
        prepare_phase(nc, a, scr, w)
        mix_phase(nc, a, scr, w, out)


_INS = ["x", "ctx_1024", "L0_attn_Wqa", "L0_attn_Wqb", "L0_attn_Wkva", "L0_attn_Wkvb", "L0_attn_Wout", "L0_attn_bout",
        "L0_xattn_wq", "L0_xattn_wk", "L0_xattn_wv", "L0_xattn_wo", "L0_xattn_bo", "L0_xattn_w1", "L0_xattn_b1",
        "L0_xattn_w2", "L0_xattn_b2", "L0_xattn_ln1_g", "L0_xattn_ln1_b", "L0_xattn_ln2_g", "L0_xattn_ln2_b",
        "L0_ffn_W1", "L0_ffn_b1", "L0_ffn_W2", "L0_ffn_b2"]


def kernel(**inputs):
    import numpy as _np
    import concourse.bacc as _bacc
    from concourse import mybir as _mybir
    from concourse.bass_utils import run_bass_kernel_spmd as _run

    nc = _bacc.Bacc("TRN2", target_bir_lowering=False, num_devices=1)
    given = {name: _np.ascontiguousarray(inputs[name]) for name in _INS}
    given["rope"] = rope_tables()
    given["ident"] = _np.eye(P, dtype=_np.float32)
    given["mask"] = _np.stack([causal_mask(), _np.ascontiguousarray(causal_mask().T)])
    given["selectors"] = head_selectors()
    arrays, args = {}, {}
    for name, array in given.items():
        arrays[f"in_{name}_dram"] = array
        args[name] = nc.dram_tensor(f"in_{name}_dram", array.shape, _mybir.dt.from_np(array.dtype), kind="ExternalInput").ap()
    out = nc.dram_tensor("out_0_dram", (B, S, E), F32, kind="ExternalOutput").ap()
    decoder_block(nc, args, out)
    r = _run(nc, [arrays], core_ids=[0])
    return r.results[0]["out_0_dram"]
```

```python
from contextlib import ExitStack

import numpy as np
import concourse.bass as bass
from concourse import mybir

F32 = mybir.dt.float32
F32R = mybir.dt.float32r
BF16 = mybir.dt.bfloat16
ALU = mybir.AluOpType
ACT = mybir.ActivationFunctionType
AX_X = mybir.AxisListType.X

P = 128
B = 8
S = 512
TT = S // P
E = 256
C = E // P
H = 16
KVH = 4
G = H // KVH
D = E // H
QL = 64
KVL = 32
R = QL + KVL
XH = 16
XD = 64
XI = XH * XD
XT = XI // P
CTX = 64
FT = 1024 // P
EPS = 1e-5
ROPE_BASE = 10000.0
SCALE = float(D) ** -0.5
MASKED = -3.0e38

PAIRS = [(0, 0), (0, 1), (0, 2), (1, 0), (1, 1), (2, 0)]
SROWS = len(PAIRS) * D
MROWS = 3
SPLIT = 512


def rope_tables():
    inv = (1.0 / ROPE_BASE ** (np.arange(0, D, 2, dtype=np.float32) / np.float32(D))).astype(np.float32)
    angle = np.outer(inv, np.arange(S, dtype=np.float32)).astype(np.float32)
    cos = np.repeat(np.cos(angle), 2, axis=0)
    sin = np.repeat(np.sin(angle), 2, axis=0)
    sin[0::2] *= -1.0
    n = P // D
    return np.stack([np.tile(cos, (n, 1)), np.tile(sin, (n, 1))]).astype(np.float32)


def causal_mask():
    q = np.arange(P)
    return np.where(q[None, :] <= q[:, None], 0.0, MASKED).astype(np.float32)


def head_selectors():
    sums = np.zeros((XT, P, P), np.float32)
    spread = np.zeros((XT, P, P), np.float32)
    for t in range(XT):
        for p in range(P):
            h = 2 * t + p // XD
            sums[t, p, h::XH] = 1.0
            spread[t, h, p] = 1.0
            spread[t, 32 + h, p] = 1.0
    return np.stack([sums, spread])


def project_phase(nc, a, scr):
    with ExitStack() as ctx:
        def sb(name, shape, dt):
            return ctx.enter_context(nc.sbuf_tensor("p1_" + name, shape, dt))

        def ps(name, shape):
            return ctx.enter_context(nc.psum_tensor("p1_" + name, shape, F32))

        def sem(name):
            return ctx.enter_context(nc.semaphore("p1_" + name))

        UNITS = 3
        RING = 3
        KW = KVH * D

        ident = sb("ident", [P, P], F32)
        wa = sb("wa", [P, C, R], F32)
        wq = sb("wq", [R, E], F32)
        wq_swap = sb("wq_swap", [R, E], F32)
        wkv = sb("wkv", [R, KVH, D, 2], F32)
        wk = sb("wk", [R, KW], F32)
        wk_swap = sb("wk_swap", [R, KW], F32)
        wv = sb("wv", [R, KW], F32)
        cos = sb("cos", [P, S], F32)
        sin = sb("sin", [P, S], F32)
        eps = sb("eps", [P, TT], F32)
        minus_half = sb("minus_half", [P, TT], F32)
        x = sb("x", [P, 2, TT, E], F32)
        stats = sb("stats", [P, 2, TT, 6], F32)
        mv = sb("mv", [P, 2, TT, 2], F32)
        var = sb("var", [P, 2, TT], F32)
        rstd = sb("rstd", [P, 2, TT], F32)
        xn = sb("xn", [P, 2, TT, E], F32)
        xnT = sb("xnT", [P, 2, C, S], F32)
        low = sb("low", [R, 2, S], F32)
        xc = sb("xc", [P, RING, S], F32)
        xs = sb("xs", [P, RING, S], F32)
        rot = sb("rot", [P, RING, S], F32)
        rem = sb("rem", [P, RING, S], F32)
        part = [sb(f"part{i}", [P, RING, S], BF16) for i in range(3)]
        v = sb("v", [P, 2, KVH, TT, 2 * D], F32)

        psT = [ps(f"psT{c}", [P, S]) for c in range(C)]
        psL = ps("psL", [P, S])
        psX = [ps(f"psX{i}", [P, S]) for i in range(2)]
        psR = [ps(f"psR{i}", [P, S]) for i in range(2)]
        psV = ps("psV", [P, TT, KVH, D])

        zeroed = sem("zeroed")
        loaded = sem("loaded")
        weights_pe = sem("weights_pe")
        x_in = [sem(f"x_in{k}") for k in range(2)]
        x_free = [sem(f"x_free{k}") for k in range(2)]
        dve_step = sem("dve_step")
        pool_step = sem("pool_step")
        stats_ready = sem("stats_ready")
        rstd_ready = sem("rstd_ready")
        xn_ready = sem("xn_ready")
        T_ready = sem("T_ready")
        xnT_ready = sem("xnT_ready")
        L_ready = sem("L_ready")
        low_ready = sem("low_ready")
        XR_ready = sem("XR_ready")
        XR_free = sem("XR_free")
        turned = sem("turned")
        rot_ready = sem("rot_ready")
        hi_ready = sem("hi_ready")
        rem_ready = sem("rem_ready")
        mid_ready = sem("mid_ready")
        parts_ready = sem("parts_ready")
        parts_out = [sem(f"parts_out{i}") for i in range(RING)]
        V_ready = sem("V_ready")
        V_free = sem("V_free")
        v_ready = sem("v_ready")
        v_out = [sem(f"v_out{k}") for k in range(2)]

        block = ctx.enter_context(nc.Block())

        @block.sync
        def _(sp):
            sp.wait_ge(zeroed, 2)
            sp.sem_inc(zeroed, -2)
            for dst, src in ((wa[:, :, 0:QL], a["L0_attn_Wqa"].rearrange("(c p) r -> p c r", p=P)),
                             (wa[:, :, QL:R], a["L0_attn_Wkva"].rearrange("(c p) r -> p c r", p=P)),
                             (wq[0:QL, :], a["L0_attn_Wqb"]),
                             (wkv[QL:R, :, :, :].rearrange("r k d z -> r (k d z)"), a["L0_attn_Wkvb"]),
                             (cos[:, :], a["rope"][0]), (sin[:, :], a["rope"][1]), (ident[:, :], a["ident"])):
                sp.dma_start(dst, src).then_inc(loaded, 16)
            for k in range(2):
                sp.dma_start(x[:, k], a["x"][k].rearrange("(t p) f -> p t f", p=P)).then_inc(x_in[k], 16)

            def stores(b, k):
                sp.wait_ge(v_ready, 1)
                sp.sem_inc(v_ready, -1)
                sp.dma_start(scr["v"][b].rearrange("g p n -> p g n"),
                             v[:, k].rearrange("p g t n -> p g (t n)")).then_inc(v_out[k], 16)
                for u in range(UNITS):
                    n = (k * UNITS + u) % RING
                    sp.wait_ge(parts_ready, 1)
                    sp.sem_inc(parts_ready, -1)
                    for i in range(3):
                        if u < 2:
                            sp.dma_start(scr["q"][i, u * P:(u + 1) * P, b, :], part[i][:, n, :]).then_inc(parts_out[n], 16)
                        else:
                            sp.dma_start(scr["k"][i, :, b, :], part[i][0:KW, n, :]).then_inc(parts_out[n], 16)

            with sp.Fori(0, B // 2 - 1) as it:
                for k in range(2):
                    sp.wait_ge(x_free[k], 1)
                    sp.sem_inc(x_free[k], -1)
                    sp.dma_start(x[:, k], a["x"][2 * it + (2 + k)].rearrange("(t p) f -> p t f", p=P)).then_inc(x_in[k], 16)
                for k in range(2):
                    stores(2 * it + k, k)
            for k in range(2):
                sp.wait_ge(x_free[k], 1)
                sp.sem_inc(x_free[k], -1)
            for k in range(2):
                stores(B - 2 + k, k)
            for k in range(2):
                sp.wait_ge(v_out[k], 16)
            for n in range(RING):
                sp.wait_ge(parts_out[n], 48)

        @block.vector
        def _(dve):
            nc.vector.memset(wq[:, :], 0.0).then_inc(zeroed, 1)
            nc.vector.memset(wkv[:, :, :, :], 0.0).then_inc(zeroed, 1)
            nc.vector.memset(v[:, :, :, :, :], 1.0)
            nc.vector.memset(eps[:, :], EPS)
            nc.vector.memset(minus_half[:, :], -0.5)
            dve.wait_ge(loaded, 7 * 16)
            dve.sem_inc(loaded, -(7 * 16))
            q2, s2 = (z[:, :].rearrange("r (n two) -> r n two", two=2) for z in (wq, wq_swap))
            nc.vector.tensor_copy(s2[:, :, 0], q2[:, :, 1])
            nc.vector.tensor_copy(s2[:, :, 1], q2[:, :, 0])
            for g in range(KVH):
                cols = slice(g * D, (g + 1) * D)
                src = wkv[:, g, :, 0].rearrange("r (n two) -> r n two", two=2)
                dst = wk_swap[:, cols].rearrange("r (n two) -> r n two", two=2)
                nc.vector.tensor_copy(dst[:, :, 0], src[:, :, 1])
                nc.vector.tensor_copy(dst[:, :, 1], src[:, :, 0])
                nc.vector.tensor_copy(wk[:, cols], wkv[:, g, :, 0])
                last = nc.vector.tensor_copy(wv[:, cols], wkv[:, g, :, 1])
            last.then_inc(weights_pe, 1)
            with dve.Fori(0, B // 2):
                for k in range(2):
                    dve.wait_ge(x_in[k], 16)
                    dve.sem_inc(x_in[k], -16)
                    for t in range(TT):
                        last = nc.vector.bn_stats(stats[:, k, t], x[:, k, t, :])
                    last.then_inc(dve_step, 1)
                    dve.wait_ge(dve_step, 1)
                    dve.sem_inc(dve_step, -1)
                    for t in range(TT):
                        last = nc.vector.bn_aggr(mv[:, k, t, :], stats[:, k, t])
                    last.then_inc(stats_ready, 1)
                for k in range(2):
                    dve.wait_ge(rstd_ready, 1)
                    dve.sem_inc(rstd_ready, -1)
                    for t in range(TT):
                        last = nc.vector.tensor_scalar(xn[:, k, t, :], x[:, k, t, :], mv[:, k, t, 0:1],
                                                       rstd[:, k, t:t + 1], ALU.subtract, ALU.mult)
                    last.then_inc(xn_ready, 1)
                    nc.vector.engine_nop().then_inc(x_free[k], 1)
                units = [(k, u) for k in range(2) for u in range(UNITS)]
                for step in range(len(units) + 2):
                    if step < len(units):
                        k, u = units[step]
                        n = step % RING
                        rows = P if u < 2 else KW
                        dve.wait_ge(XR_ready, 1)
                        dve.sem_inc(XR_ready, -1)
                        nc.vector.tensor_tensor(xc[0:rows, n], psX[step % 2][0:rows, :], cos[0:rows, :], ALU.mult)
                        nc.vector.tensor_tensor(xs[0:rows, n], psR[step % 2][0:rows, :], sin[0:rows, :],
                                                ALU.mult).then_inc(turned, 1)
                        nc.vector.engine_nop().then_inc(XR_free, 1)
                    if 1 <= step <= len(units):
                        n = (step - 1) % RING
                        rows = P if units[step - 1][1] < 2 else KW
                        dve.wait_ge(hi_ready, 1)
                        dve.sem_inc(hi_ready, -1)
                        nc.vector.tensor_tensor(rem[0:rows, n], rot[0:rows, n], part[0][0:rows, n],
                                                ALU.subtract).then_inc(rem_ready, 1)
                    if step >= 2:
                        n = (step - 2) % RING
                        rows = P if units[step - 2][1] < 2 else KW
                        dve.wait_ge(mid_ready, 1)
                        dve.sem_inc(mid_ready, -1)
                        nc.vector.tensor_tensor(part[2][0:rows, n], rem[0:rows, n], part[1][0:rows, n],
                                                ALU.subtract).then_inc(parts_ready, 1)

        @block.gpsimd
        def _(pool):
            with pool.Fori(0, B // 2):
                for k in range(2):
                    pool.wait_ge(stats_ready, 1)
                    pool.sem_inc(stats_ready, -1)
                    nc.gpsimd.tensor_tensor(var[:, k], mv[:, k, :, 1], eps[:, :], ALU.add).then_inc(pool_step, 1)
                    pool.wait_ge(pool_step, 1)
                    pool.sem_inc(pool_step, -1)
                    nc.gpsimd.tensor_tensor(rstd[:, k], var[:, k], minus_half[:, :], ALU.pow).then_inc(rstd_ready, 1)
                for k in range(2):
                    for u in range(UNITS):
                        n = (k * UNITS + u) % RING
                        rows = P if u < 2 else KW
                        pool.wait_ge(turned, 1)
                        pool.sem_inc(turned, -1)
                        nc.gpsimd.tensor_tensor(rot[0:rows, n], xc[0:rows, n], xs[0:rows, n],
                                                ALU.add).then_inc(rot_ready, 1)

        @block.scalar
        def _(act):
            for n in range(RING):
                act.sem_inc(parts_out[n], 48)
            for k in range(2):
                act.sem_inc(v_out[k], 16)
            with act.Fori(0, B // 2):
                for k in range(2):
                    act.wait_ge(T_ready, 1)
                    act.sem_inc(T_ready, -1)
                    nc.scalar.activation(xnT[:, k, 0, :], psT[0][:, :], ACT.Copy)
                    nc.scalar.activation(xnT[:, k, 1, :], psT[1][:, :], ACT.Copy).then_inc(xnT_ready, 1)
                for k in range(2):
                    act.wait_ge(L_ready, 1)
                    act.sem_inc(L_ready, -1)
                    nc.scalar.activation(low[:, k, :], psL[0:R, :], ACT.Copy).then_inc(low_ready, 1)
                units = [(k, u) for k in range(2) for u in range(UNITS)]
                for step in range(len(units) + 1):
                    if step < len(units):
                        k, u = units[step]
                        n = step % RING
                        rows = P if u < 2 else KW
                        if u == 0:
                            act.wait_ge(V_ready, 1)
                            act.sem_inc(V_ready, -1)
                            act.wait_ge(v_out[k], 16)
                            act.sem_inc(v_out[k], -16)
                            nc.scalar.activation(v[:, k, :, :, 0:D].rearrange("p g t d -> p t g d"), psV[:, :, :, :],
                                                 ACT.Copy).then_inc(V_free, 1)
                            act.drain().then_inc(v_ready, 1)
                        act.wait_ge(rot_ready, 1)
                        act.sem_inc(rot_ready, -1)
                        act.wait_ge(parts_out[n], 48)
                        act.sem_inc(parts_out[n], -48)
                        nc.scalar.activation(part[0][0:rows, n], rot[0:rows, n], ACT.Copy).then_inc(hi_ready, 1)
                    if step >= 1:
                        n = (step - 1) % RING
                        rows = P if units[step - 1][1] < 2 else KW
                        act.wait_ge(rem_ready, 1)
                        act.sem_inc(rem_ready, -1)
                        nc.scalar.activation(part[1][0:rows, n], rem[0:rows, n], ACT.Copy).then_inc(mid_ready, 1)

        @block.tensor
        def _(pe):
            pe.wait_ge(weights_pe, 1)
            pe.sem_inc(weights_pe, -1)
            pe.sem_inc(XR_free, 2)
            pe.sem_inc(V_free, 1)
            with pe.Fori(0, B // 2):
                for k in range(2):
                    pe.wait_ge(xn_ready, 1)
                    pe.sem_inc(xn_ready, -1)
                    if k == 1:
                        pe.wait_ge(xnT_ready, 1)
                        pe.sem_inc(xnT_ready, -1)
                    for t in range(TT):
                        for c in range(C):
                            last = nc.tensor.transpose(psT[c][:, t * P:(t + 1) * P], xn[:, k, t, c * P:(c + 1) * P],
                                                       ident[:, :])
                    last.then_inc(T_ready, 1)
                for k in range(2):
                    if k == 1:
                        pe.wait_ge(xnT_ready, 1)
                        pe.sem_inc(xnT_ready, -1)
                        pe.wait_ge(low_ready, 1)
                        pe.sem_inc(low_ready, -1)
                    for c in range(C):
                        last = nc.tensor.matmul(psL[0:R, :], wa[:, c, :], xnT[:, k, c, :], start=(c == 0), stop=(c == C - 1))
                    last.then_inc(L_ready, 1)
                for k in range(2):
                    if k == 1:
                        pe.wait_ge(low_ready, 1)
                        pe.sem_inc(low_ready, -1)
                    pe.wait_ge(V_free, 1)
                    pe.sem_inc(V_free, -1)
                    for t in range(TT):
                        last = nc.tensor.matmul(psV[:, t, :, :].rearrange("p g d -> p (g d)"), low[:, k, t * P:(t + 1) * P],
                                                wv[:, :], start=True, stop=True)
                    last.then_inc(V_ready, 1)
                    for u in range(UNITS):
                        i = (k * UNITS + u) % 2
                        rows = P if u < 2 else KW
                        w, ws = (wq[:, u * P:(u + 1) * P], wq_swap[:, u * P:(u + 1) * P]) if u < 2 else (wk[:, :], wk_swap[:, :])
                        pe.wait_ge(XR_free, 1)
                        pe.sem_inc(XR_free, -1)
                        nc.tensor.matmul(psX[i][0:rows, :], w, low[:, k, :], start=True, stop=True)
                        nc.tensor.matmul(psR[i][0:rows, :], ws, low[:, k, :], start=True, stop=True).then_inc(XR_ready, 1)


def attend_phase(nc, a, scr, splits):
    with ExitStack() as ctx:
        def sb(name, shape, dt):
            return ctx.enter_context(nc.sbuf_tensor("p2_" + name, shape, dt))

        def ps(name, shape):
            return ctx.enter_context(nc.psum_tensor("p2_" + name, shape, F32))

        def sem(name):
            return ctx.enter_context(nc.semaphore("p2_" + name))

        ident = sb("ident", [P, P], F32)
        ident_b = sb("ident_b", [P, P], BF16)
        mask = sb("mask", [P, 2, P], F32)
        mask_b = sb("mask_b", [P, 2, P], BF16)
        qs = sb("qs", [P, 2, H, S], BF16)
        ks = sb("ks", [P, 2, KVH, S], BF16)
        v = sb("v", [P, 2, KVH, TT, 2 * D], F32)
        mx = sb("mx", [P, H, TT], F32)
        mparts = [sb(f"mpart{i}", [H * TT, P], BF16) for i in range(MROWS)]
        mrem = sb("mrem", [H * TT, P], F32)
        widths = [S - P * j for j in range(TT)]
        starts = [G * sum(widths[:j]) for j in range(TT)]
        probs = sb("probs", [P, 2, G * sum(widths)], F32)
        o = sb("o", [P, 2, S], F32)

        stage = [sb(f"stage{i}", [P, SPLIT], F32) for i in range(2)]

        psA = [ps(f"psA{i}", [P, 2, S]) for i in range(2)]
        psS = [ps(f"psS{i}", [P, S]) for i in range(2)]
        psO = [ps(f"psO{i}", [P, S]) for i in range(2)]

        loaded = sem("loaded")
        consts_pe = sem("consts_pe")
        stack_in = [[sem(f"stack_in{k}_{g}") for g in range(KVH)] for k in range(2)]
        A_ready = sem("A_ready")
        A_free = sem("A_free")
        mT_ready = sem("mT_ready")
        dve_step = sem("dve_step")
        m_ready = sem("m_ready")
        m_in = [sem(f"m_in{k}") for k in range(2)]
        S_ready = sem("S_ready")
        exp_done = sem("exp_done")
        O_ready = sem("O_ready")
        o_ready = sem("o_ready")
        o_out = [sem(f"o_out{i}") for i in range(2)]

        stage_in = [sem(f"stage_in{i}") for i in range(2)]
        hi_done = sem("hi_done")
        lo_done = sem("lo_done")

        NIN = 2 * len(PAIRS) + 1

        SUNITS = [(0, r, 1) for r in range(G)] + [(1, r, 1) for r in range(G)] + [(2, 0, 2), (2, 2, 2), (3, 0, 4)]
        LAST = [3, 7, 9, 10]
        AUNITS = [(i, rp) for i in range(TT) for rp in range(G // 2)]

        block = ctx.enter_context(nc.Block())

        @block.sync
        def _(sp):
            for dst, src in ((ident[:, :], a["ident"]), (mask[:, 0, :], a["mask"][0]), (mask[:, 1, :], a["mask"][1])):
                sp.dma_start(dst, src).then_inc(loaded, 16)

            def load(b, k, g):
                for row, (pq, pk) in enumerate(PAIRS):
                    rows = slice(row * D, (row + 1) * D)
                    sp.dma_start(qs[rows, k, g * G:(g + 1) * G, :],
                                 scr["q"][pq, g * G * D:(g + 1) * G * D, b, :].rearrange("(h d) t -> d h t", d=D)
                                 ).then_inc(stack_in[k][g], 16)
                    sp.dma_start(ks[rows, k, g, :], scr["k"][pk, g * D:(g + 1) * D, b, :]).then_inc(stack_in[k][g], 16)
                sp.dma_start(v[:, k, g].rearrange("p t n -> p (t n)"), scr["v"][b, g]).then_inc(stack_in[k][g], 16)

            def maxima(k):
                sp.wait_ge(m_ready, 1)
                sp.sem_inc(m_ready, -1)
                for i in range(MROWS):
                    row = SROWS + i
                    sp.dma_start(qs[row:row + 1, k].rearrange("o h (t q) -> o (h t) q", t=TT), mparts[i][:, :]
                                 ).then_inc(m_in[k], 16)

            def store(b, g):
                sp.wait_ge(o_ready, 1)
                sp.sem_inc(o_ready, -1)
                for r in range(G):
                    sp.dma_start(scr["o"][b, g * G + r], o[32 * r:32 * r + D + 1, g % 2, :]).then_inc(o_out[g % 2], 16)

            def batch(b, k, refill, has_next):
                for g in range(KVH):
                    if g == KVH - 1 and has_next:
                        maxima(1 - k)
                    store(b, g)
                    if refill:
                        load(b + 2, k, g)

            for k in range(2):
                for g in range(KVH):
                    load(k, k, g)
            maxima(0)
            with sp.Fori(0, B // 2 - 1) as it:
                for k in range(2):
                    batch(2 * it + k, k, True, True)
            batch(B - 2, 0, False, True)
            batch(B - 1, 1, False, False)
            for i in range(2):
                sp.wait_ge(o_out[i], 16 * G)

        @block.vector
        def _(dve):
            dve.wait_ge(loaded, 3 * 16)
            dve.sem_inc(loaded, -(3 * 16))
            nc.vector.memset(ks[SROWS:P, :, :, :], -1.0)
            nc.vector.tensor_copy(ident_b[:, :], ident[:, :])
            nc.vector.tensor_copy(mask_b[:, :, :], mask[:, :, :]).then_inc(consts_pe, 1)

            def maxima(g):
                for i, rp in AUNITS:
                    buf = (i * 2 + rp) % 2
                    h = g * G + 2 * rp
                    dve.wait_ge(A_ready, 1)
                    dve.sem_inc(A_ready, -1)
                    nc.vector.tensor_reduce(mx[:, h:h + 2, i], psA[buf][:, :, 0:P * (i + 1)], AX_X,
                                            ALU.max).then_inc(A_free, 1)

            def parts():
                dve.wait_ge(mT_ready, 1)
                dve.sem_inc(mT_ready, -1)
                mT = psA[0][0:H * TT, 0, 0:P]
                nc.vector.tensor_copy(mparts[0][:, :], mT).then_inc(dve_step, 1)
                dve.wait_ge(dve_step, 1)
                dve.sem_inc(dve_step, -1)
                nc.vector.tensor_tensor(mrem[:, :], mT, mparts[0][:, :], ALU.subtract).then_inc(dve_step, 1)
                nc.vector.engine_nop().then_inc(A_free, 2)
                dve.wait_ge(dve_step, 1)
                dve.sem_inc(dve_step, -1)
                nc.vector.tensor_copy(mparts[1][:, :], mrem[:, :]).then_inc(dve_step, 1)
                dve.wait_ge(dve_step, 1)
                dve.sem_inc(dve_step, -1)
                nc.vector.tensor_tensor(mparts[2][:, :], mrem[:, :], mparts[1][:, :], ALU.subtract).then_inc(m_ready, 1)

            def batch():
                for g in range(KVH):
                    maxima(g)
                parts()

            batch()
            with dve.Fori(0, B - 1):
                batch()

        @block.gpsimd
        def _(pool):
            split_weights(nc, pool, stage, stage_in, hi_done, lo_done, splits)

        @block.scalar
        def _(act):
            for i in range(2):
                act.sem_inc(o_out[i], 16 * G)

            def out(g):
                act.wait_ge(O_ready, 1)
                act.sem_inc(O_ready, -1)
                act.wait_ge(o_out[g % 2], 16 * G)
                act.sem_inc(o_out[g % 2], -(16 * G))
                nc.scalar.activation(o[:, g % 2, :], psO[g % 2][:, :], ACT.Copy).then_inc(o_ready, 1)

            with act.Fori(0, B):
                for g in range(KVH):
                    for s, (j, r0, n) in enumerate(SUNITS):
                        w = widths[j]
                        at = starts[j] + r0 * w
                        act.wait_ge(S_ready, 1)
                        act.sem_inc(S_ready, -1)
                        nc.scalar.activation(probs[:, g % 2, at:at + n * w], psS[(g * 11 + s) % 2][:, 0:n * w], ACT.Exp,
                                             scale=SCALE).then_inc(exp_done, 1)
                        if s == 4 and g >= 1:
                            out(g - 1)
                out(KVH - 1)

        @block.tensor
        def _(pe):
            pe.wait_ge(consts_pe, 1)
            pe.sem_inc(consts_pe, -1)
            pe.sem_inc(A_free, 2)

            def score_rows(k, g, i, rp):
                buf = (i * 2 + rp) % 2
                pe.wait_ge(A_free, 1)
                pe.sem_inc(A_free, -1)
                n = P * (i + 1)
                for z in range(2):
                    h = g * G + 2 * rp + z
                    nc.tensor.matmul(psA[buf][:, z, 0:n], qs[0:SROWS, k, h, i * P:(i + 1) * P], ks[0:SROWS, k, g, 0:n],
                                     start=True, stop=False)
                    last = nc.tensor.matmul(psA[buf][:, z, n - P:n], ident_b[:, :], mask_b[:, 0, :], start=False, stop=True)
                last.then_inc(A_ready, 1)

            def maxima():
                pe.wait_ge(A_free, 2)
                pe.sem_inc(A_free, -2)
                nc.tensor.transpose(psA[0][0:H * TT, 0, 0:P], mx[:, :, :].rearrange("p h t -> p (h t)"),
                                    ident[:, :]).then_inc(mT_ready, 1)

            def score_cols(k, g, s):
                j, r0, n = SUNITS[s]
                w = widths[j]
                bank = psS[(g * 11 + s) % 2]
                key = ks[0:SROWS + MROWS, k, g, j * P:(j + 1) * P]
                for z in range(n):
                    h = g * G + r0 + z
                    nc.tensor.matmul(bank[:, z * w:(z + 1) * w], key, qs[0:SROWS + MROWS, k, h, j * P:S],
                                     start=True, stop=False)
                    last = nc.tensor.matmul(bank[:, z * w:z * w + P], ident_b[:, :], mask_b[:, 1, :], start=False, stop=True)
                last.then_inc(S_ready, 1)

            def values(k, g, j):
                w = widths[j]
                for r in range(G):
                    at = starts[j] + r * w
                    last = nc.tensor.matmul(psO[g % 2][32 * r:32 * r + 32, j * P:S], v[:, k, g, j, :],
                                            probs[:, g % 2, at:at + w], start=(j == 0), stop=(j == TT - 1))
                if j == TT - 1:
                    last.then_inc(O_ready, 1)

            def batch(k, has_next):
                used = [0]

                def exps(n):
                    if n > used[0]:
                        pe.wait_ge(exp_done, n - used[0])
                        pe.sem_inc(exp_done, -(n - used[0]))
                        used[0] = n

                pe.wait_ge(m_in[k], 16 * MROWS)
                pe.sem_inc(m_in[k], -(16 * MROWS))
                for g in range(KVH):
                    first = g * len(SUNITS)
                    if has_next:
                        pe.wait_ge(stack_in[1 - k][g], 16 * NIN)
                        pe.sem_inc(stack_in[1 - k][g], -(16 * NIN))
                    for s in range(len(SUNITS)):
                        if first + s >= 2:
                            exps(first + s - 1)
                        score_cols(k, g, s)
                        if has_next and s < len(AUNITS):
                            score_rows(1 - k, g, *AUNITS[s])
                        if s == 1 and g >= 1:
                            for j in (2, 3):
                                exps(first - len(SUNITS) + LAST[j] + 1)
                                values(k, g - 1, j)
                        if s == 6:
                            exps(first + LAST[0] + 1)
                            values(k, g, 0)
                        if s == 9:
                            exps(first + LAST[1] + 1)
                            values(k, g, 1)
                    if g == KVH - 1 and has_next:
                        maxima()
                for j in (2, 3):
                    exps(KVH * len(SUNITS) - len(SUNITS) + LAST[j] + 1)
                    values(k, KVH - 1, j)

            for g in range(KVH):
                pe.wait_ge(stack_in[0][g], 16 * NIN)
                pe.sem_inc(stack_in[0][g], -(16 * NIN))
                for i, rp in AUNITS:
                    score_rows(0, g, i, rp)
            maxima()
            with pe.Fori(0, B // 2 - 1):
                batch(0, True)
                batch(1, True)
            batch(0, True)
            batch(1, False)


def prepare_phase(nc, a, scr, w, cw):
    with ExitStack() as ctx:
        def sb(name, shape, dt):
            return ctx.enter_context(nc.sbuf_tensor("p3_" + name, shape, dt))

        def ps(name, shape):
            return ctx.enter_context(nc.psum_tensor("p3_" + name, shape, F32))

        def sem(name):
            return ctx.enter_context(nc.semaphore("p3_" + name))

        BT = P // CTX
        NTILE = B // BT
        WN = 2048
        ident = sb("ident", [P, P], F32)
        ones = sb("ones", [P, P], F32)
        stage = [sb(f"stage{i}", [P, WN], F32) for i in range(2)]
        abs_sum = sb("abs_sum", [P, 2], F32)
        half = sb("half", [P, 1], F32)
        vecs = sb("vecs", [w["ncols"], P], F32)
        thr = sb("thr", [P, 1], F32)
        nthr = sb("nthr", [P, 1], F32)
        sums = sb("sums", [B * H, S], F32)
        eps = sb("eps", [P, 1], F32)
        mhalf = sb("mhalf", [P, XH], F32)
        cx = sb("cx", [P, E], F32)
        stats = sb("stats", [P, 6], F32)
        mv = sb("mv", [P, 2], F32)
        var = sb("var", [P, 1], F32)
        rstd = sb("rstd", [P, 1], F32)
        cn = sb("cn", [P, E], F32)
        cnT = sb("cnT", [P, C, P], F32)
        cnh, cnl = sb("cnh", [P, C, P], F32R), sb("cnl", [P, C, P], F32R)
        k = sb("k", [P, XI], F32)
        v = sb("v", [P, XI], F32)
        k2 = sb("k2", [P, XI], F32)
        n2 = sb("n2", [P, XH], F32)
        rn = sb("rn", [P, XH], F32)
        woh, wol = sb("woh", [P, XT, E], F32R), sb("wol", [P, XT, E], F32R)
        bdh, bdl = sb("bdh", [P, XT, P], F32R), sb("bdl", [P, XT, P], F32R)
        nh = sb("nh", [P, BT, XT, E], F32R)
        nl = sb("nl", [P, BT, XT, E], F32R)

        absw = nh[:, :, :, :].bitcast(F32).rearrange("p z t n -> p z (t n)")
        tern = nl[:, 0, :, :].bitcast(F32).rearrange("p t n -> p (t n)")
        wo = nl[:, 1, :, :].bitcast(F32)

        psK = [ps(f"psK{i}", [P, S]) for i in range(2)]
        psV = [ps(f"psV{i}", [P, S]) for i in range(2)]
        psM = [ps(f"psM{i}", [P, S]) for i in range(2)]
        psN = [ps(f"psN{i}", [P, S]) for i in range(2)]

        const_in = sem("const_in")
        small_in = sem("small_in")
        cols_ready = sem("cols_ready")
        cols_done = sem("cols_done")
        stage_in = [sem(f"stage_in{i}") for i in range(2)]
        staged = sem("staged")
        sum_pe = sem("sum_pe")
        total = sem("total")
        step = sem("step")
        tern_ready = sem("tern_ready")
        ternT_ready = sem("ternT_ready")
        ternT_free = sem("ternT_free")
        wo_in = sem("wo_in")
        woh_ready = sem("woh_ready")
        wo_parts = sem("wo_parts")
        sums_in = sem("sums_in")
        rden_ready = sem("rden_ready")
        rden_out = sem("rden_out")
        cx_in = sem("cx_in")
        cx_free = sem("cx_free")
        var_ready = sem("var_ready")
        rs_ready = sem("rs_ready")
        pool_step = sem("pool_step")
        cn_ready = sem("cn_ready")
        T_ready = sem("T_ready")
        cnT_done = sem("cnT_done")
        cn_parts = sem("cn_parts")
        KV_ready = sem("KV_ready")
        k_ready = sem("k_ready")
        kn_ready = sem("kn_ready")
        M_ready = sem("M_ready")
        bdh_ready = sem("bdh_ready")
        bd_ready = sem("bd_ready")
        N_ready = sem("N_ready")
        nh_ready = sem("nh_ready")
        nl_ready = sem("nl_ready")
        n_ready = sem("n_ready")
        n_out = sem("n_out")

        terns = [(a["L0_ffn_W1"].rearrange("(c p) n -> p c n", p=P), FT, E),
                 (a["L0_ffn_W2"].rearrange("(c p) n -> p c n", p=P), C, FT * P)]

        block = ctx.enter_context(nc.Block())

        @block.sync
        def _(sp):
            tiles = a["ctx_1024"].rearrange("(t b) s f -> t (b s) f", b=BT)

            def load(t):
                sp.dma_start(cx[:, :], tiles[t]).then_inc(cx_in, 16)

            def store(t):
                for z in range(BT):
                    sp.wait_ge(n_ready, 1)
                    sp.sem_inc(n_ready, -1)
                    for part, src in enumerate((nh, nl)):
                        sp.dma_start(scr["n"][BT * t + z, part], src[:, z].rearrange("p t n -> p (t n)").bitcast(F32)).then_inc(n_out, 16)

            load(0)
            sp.dma_start(ident[:, :], a["ident"]).then_inc(const_in, 16)
            for name, at, n in w["vectors"]:
                sp.dma_start(vecs[at:at + n, :], a[name].rearrange("(c p) -> c p", p=P)).then_inc(small_in, 16)
            sp.wait_ge(cx_free, 1)
            sp.sem_inc(cx_free, -1)
            load(1)
            for i, (src, cc, _) in enumerate(terns):
                sp.dma_start(stage[i][:, :].rearrange("p (c n) -> p c n", c=cc), src).then_inc(stage_in[i], 16)
            sp.dma_start(sums[:, :], scr["o"][:, :, D, :].rearrange("b h t -> (b h) t")).then_inc(sums_in, 16)
            sp.dma_start(wo, a["L0_xattn_wo"].rearrange("(c p) n -> p c n", p=P)).then_inc(wo_in, 16)
            sp.wait_ge(cx_free, 1)
            sp.sem_inc(cx_free, -1)
            load(2)
            sp.wait_ge(rden_ready, 1)
            sp.sem_inc(rden_ready, -1)
            sp.dma_start(scr["rden"].rearrange("b h t -> (b h) t"), sums[:, :]).then_inc(rden_out, 16)
            store(0)
            sp.wait_ge(cx_free, 1)
            sp.sem_inc(cx_free, -1)
            load(3)
            for t in range(1, NTILE):
                store(t)
            sp.wait_ge(cx_free, 1)
            sp.sem_inc(cx_free, -1)
            sp.wait_ge(rden_out, 16)
            sp.sem_inc(rden_out, -16)
            sp.wait_ge(n_out, 16 * 2 * BT)

        @block.gpsimd
        def _(pool):
            def of_rows():
                pool.wait_ge(var_ready, 1)
                pool.sem_inc(var_ready, -1)
                nc.gpsimd.tensor_tensor(var[:, :], mv[:, 1:2], eps[:, :], ALU.add).then_inc(pool_step, 1)
                pool.wait_ge(pool_step, 1)
                pool.sem_inc(pool_step, -1)
                nc.gpsimd.tensor_tensor(rstd[:, :], var[:, :], mhalf[:, 0:1], ALU.pow).then_inc(rs_ready, 1)

            def of_heads():
                pool.wait_ge(var_ready, 1)
                pool.sem_inc(var_ready, -1)
                nc.gpsimd.tensor_tensor(rn[:, :], n2[:, :], mhalf[:, :], ALU.pow).then_inc(rs_ready, 1)

            of_rows()
            of_rows()
            of_heads()
            with pool.Fori(0, NTILE - 2):
                of_rows()
                of_heads()
            of_heads()

        @block.scalar
        def _(act):
            def affine():
                act.wait_ge(T_ready, 1)
                act.sem_inc(T_ready, -1)
                for c in range(C):
                    last = nc.scalar.activation(cnT[:, c, :], psM[0][:, c * P:(c + 1) * P], ACT.Identity,
                                                bias=w["ln1_b"][:, c:c + 1], scale=w["ln1_g"][:, c:c + 1])
                last.then_inc(cnT_done, 1)

            def keys():
                act.wait_ge(KV_ready, 1)
                act.sem_inc(KV_ready, -1)
                for dst, bank in ((k, psK), (v, psV)):
                    for i in range(2):
                        last = nc.scalar.activation(dst[:, i * S:(i + 1) * S], bank[i][:, :], ACT.Copy)
                last.then_inc(k_ready, 1)

            def tile(ahead, follows):
                for z in range(BT):
                    for i in range(2):
                        act.wait_ge(M_ready, 1)
                        act.sem_inc(M_ready, -1)
                        m = psM[i][:, :].rearrange("p (t n) -> p t n", t=4)
                        for side in range(2):
                            r = slice(side * XD, (side + 1) * XD)
                            last = nc.scalar.activation(bdh[r, 4 * i:4 * i + 4, r], m[r, :, r], ACT.Copy)
                        last.then_inc(bdh_ready, 1)
                    if z == 1 and follows:
                        keys()
                    if z == 1 and ahead:
                        affine()
                    if z == 0:
                        act.wait_ge(n_out, 16 * 2 * BT)
                        act.sem_inc(n_out, -(16 * 2 * BT))
                    for i in range(XT // 2):
                        act.wait_ge(N_ready, 1)
                        act.sem_inc(N_ready, -1)
                        nc.scalar.activation(nh[:, z, 2 * i:2 * i + 2, :].rearrange("p t n -> p (t n)"), psN[i % 2][:, :],
                                             ACT.Copy).then_inc(nh_ready, 1)

            act.wait_ge(cols_ready, 1)
            act.sem_inc(cols_ready, -1)
            nc.scalar.activation(w["all_columns"][:, :], psN[1][:, 0:w["ncols"]], ACT.Copy).then_inc(cols_done, 1)
            act.wait_ge(cols_done, 1)
            act.sem_inc(cols_done, -1)
            affine()
            keys()
            affine()
            for i in range(2):
                act.wait_ge(stage_in[i], 16)
                act.sem_inc(stage_in[i], -16)
                nc.scalar.activation(absw[:, i, :], stage[i][:, :], ACT.Abs, accum_out=abs_sum[:, i:i + 1]).then_inc(staged, 1)
            act.wait_ge(wo_in, 16)
            act.sem_inc(wo_in, -16)
            nc.scalar.activation(woh[:, :, :], wo, ACT.Copy).then_inc(woh_ready, 1)
            act.sem_inc(n_out, 16 * 2 * BT)
            with act.Fori(0, NTILE - 2):
                tile(True, True)
            tile(False, True)
            tile(False, False)

        @block.vector
        def _(dve):
            def rows():
                dve.wait_ge(cx_in, 16)
                dve.sem_inc(cx_in, -16)
                nc.vector.bn_stats(stats[:, :], cx[:, :]).then_inc(step, 1)
                dve.wait_ge(step, 1)
                dve.sem_inc(step, -1)
                nc.vector.bn_aggr(mv[:, :], stats[:, :]).then_inc(var_ready, 1)
                dve.wait_ge(rs_ready, 1)
                dve.sem_inc(rs_ready, -1)
                nc.vector.tensor_scalar(cn[:, :], cx[:, :], mv[:, 0:1], rstd[:, 0:1], ALU.subtract, ALU.mult).then_inc(cn_ready, 1)
                nc.vector.engine_nop().then_inc(cx_free, 1)

            def row_parts():
                dve.wait_ge(cnT_done, 1)
                dve.sem_inc(cnT_done, -1)
                nc.vector.tensor_copy(cnh[:, :, :], cnT[:, :, :]).then_inc(step, 1)
                dve.wait_ge(step, 1)
                dve.sem_inc(step, -1)
                nc.vector.tensor_tensor(cnl[:, :, :], cnT[:, :, :], cnh[:, :, :].bitcast(F32), ALU.subtract).then_inc(cn_parts, 1)

            def normalise_keys():
                dve.wait_ge(k_ready, 1)
                dve.sem_inc(k_ready, -1)
                nc.vector.tensor_tensor(k2[:, :], k[:, :], k[:, :], ALU.mult).then_inc(step, 1)
                dve.wait_ge(step, 1)
                dve.sem_inc(step, -1)
                nc.vector.tensor_reduce(n2[:, :], k2[:, :].rearrange("p (h d) -> p h d", h=XH), AX_X, ALU.add).then_inc(step, 1)
                dve.wait_ge(step, 1)
                dve.sem_inc(step, -1)
                nc.vector.tensor_scalar(n2[:, :], n2[:, :], 1e-24, None, ALU.max).then_inc(var_ready, 1)
                dve.wait_ge(rs_ready, 1)
                dve.sem_inc(rs_ready, -1)
                nc.vector.tensor_tensor(k[:, :].rearrange("p (h d) -> p h d", h=XH), k[:, :].rearrange("p (h d) -> p h d", h=XH),
                                        rn[:, :].unsqueeze(2).broadcast_to([P, XH, XD]), ALU.mult).then_inc(kn_ready, 1)

            def ternary(i, cc, nn):
                dve.wait_ge(staged, 1)
                dve.sem_inc(staged, -1)
                nc.vector.engine_nop().then_inc(sum_pe, 1)
                dve.wait_ge(total, 1)
                dve.sem_inc(total, -1)
                nc.vector.tensor_scalar(thr[:, :], psN[0][:, 0:1], 1.0 / (cc * nn * P), 1e-8, ALU.mult, ALU.max).then_inc(step, 1)
                dve.wait_ge(step, 1)
                dve.sem_inc(step, -1)
                nc.vector.tensor_scalar(nthr[:, :], thr[:, :], -0.5, None, ALU.mult)
                nc.vector.tensor_scalar(half[:, :], thr[:, :], 0.5, None, ALU.mult).then_inc(step, 1)
                dve.wait_ge(step, 1)
                dve.sem_inc(step, -1)
                wst = stage[i]
                nc.vector.tensor_scalar(tern[:, :], wst[:, :], nthr[:, 0:1], None, ALU.is_lt).then_inc(step, 1)
                dve.wait_ge(step, 1)
                dve.sem_inc(step, -1)
                nc.vector.scalar_tensor_tensor(out=tern[:, :], in0=wst[:, :], scalar=half[:, 0:1], in1=tern[:, :],
                                               op0=ALU.is_gt, op1=ALU.subtract).then_inc(tern_ready, 1)
                for q in range(4):
                    dve.wait_ge(ternT_ready, 1)
                    dve.sem_inc(ternT_ready, -1)
                    src = psM[q % 2] if q < 2 else psN[q % 2]
                    if i == 0:
                        dst = w["t1"][:, :, 2 * q * P:(2 * q + 2) * P]
                        s = src[:, :].rearrange("p (c n) -> p c n", c=C)
                    else:
                        dst = w["t2"][:, 2 * q:2 * q + 2, :]
                        s = src[:, :].rearrange("p (t n) -> p t n", t=2)
                    last = nc.vector.tensor_copy(dst, s)
                last.then_inc(ternT_free, 1)

            def tile(ahead, follows):
                for z in range(BT):
                    for i in range(2):
                        dve.wait_ge(bdh_ready, 1)
                        dve.sem_inc(bdh_ready, -1)
                        m = psM[i][:, :].rearrange("p (t n) -> p t n", t=4)
                        for side in range(2):
                            r = slice(side * XD, (side + 1) * XD)
                            last = nc.vector.tensor_tensor(bdl[r, 4 * i:4 * i + 4, r], m[r, :, r],
                                                           bdh[r, 4 * i:4 * i + 4, r].bitcast(F32), ALU.subtract)
                        last.then_inc(bd_ready, 1)
                    if z == 0 and ahead:
                        rows()
                    for i in range(XT // 2):
                        dve.wait_ge(nh_ready, 1)
                        dve.sem_inc(nh_ready, -1)
                        high = nh[:, z, 2 * i:2 * i + 2, :].rearrange("p t n -> p (t n)").bitcast(F32)
                        nc.vector.tensor_tensor(nl[:, z, 2 * i:2 * i + 2, :].rearrange("p t n -> p (t n)"), psN[i % 2][:, :],
                                                high, ALU.subtract).then_inc(nl_ready, 1)
                    nc.vector.engine_nop().then_inc(n_ready, 1)
                if ahead:
                    row_parts()
                if follows:
                    normalise_keys()

            nc.vector.memset(ones[:, :], 1.0)
            nc.vector.memset(eps[:, :], EPS)
            nc.vector.memset(mhalf[:, :], -0.5)
            nc.vector.memset(bdh[:, :, :].bitcast(F32), 0.0)
            nc.vector.memset(bdl[:, :, :].bitcast(F32), 0.0)
            rows()
            row_parts()
            rows()
            normalise_keys()
            row_parts()
            dve.wait_ge(sums_in, 16)
            dve.sem_inc(sums_in, -16)
            nc.vector.reciprocal(sums[:, :], sums[:, :]).then_inc(rden_ready, 1)
            for i, (_, cc, nn) in enumerate(terns):
                ternary(i, cc, nn)
            dve.wait_ge(woh_ready, 1)
            dve.sem_inc(woh_ready, -1)
            nc.vector.tensor_tensor(wol[:, :, :], wo, woh[:, :, :].bitcast(F32), ALU.subtract).then_inc(wo_parts, 1)
            with dve.Fori(0, NTILE - 2):
                tile(True, True)
            tile(False, True)
            tile(False, False)

        @block.tensor
        def _(pe):
            def transpose_rows():
                pe.wait_ge(cn_ready, 1)
                pe.sem_inc(cn_ready, -1)
                for c in range(C):
                    last = nc.tensor.transpose(psM[0][:, c * P:(c + 1) * P], cn[:, c * P:(c + 1) * P], ident[:, :])
                last.then_inc(T_ready, 1)

            def project_rows():
                pe.wait_ge(cn_parts, 1)
                pe.sem_inc(cn_parts, -1)
                for bank, (whi, wlo) in ((psK, cw["wk"]), (psV, cw["wv"])):
                    for i in range(2):
                        cols = slice(i * S, (i + 1) * S)
                        for c in range(C):
                            nc.tensor.matmul(bank[i][:, :], cnh[:, c, :], whi[:, c, cols], start=(c == 0), stop=False)
                            nc.tensor.matmul(bank[i][:, :], cnh[:, c, :], wlo[:, c, cols], start=False, stop=False)
                            last = nc.tensor.matmul(bank[i][:, :], cnl[:, c, :], whi[:, c, cols], start=False, stop=(c == C - 1))
                last.then_inc(KV_ready, 1)

            def ternary(i, cc):
                pe.wait_ge(sum_pe, 1)
                pe.sem_inc(sum_pe, -1)
                nc.tensor.matmul(psN[0][:, 0:1], ones[:, :], abs_sum[:, i:i + 1], start=True, stop=True).then_inc(total, 1)
                pe.wait_ge(tern_ready, 1)
                pe.sem_inc(tern_ready, -1)
                t = tern[:, :].rearrange("p (c n) -> p c n", c=cc)
                for q in range(4):
                    dst = psM[q % 2] if q < 2 else psN[q % 2]
                    for y in range(2):
                        for c in range(C):
                            if i == 0:
                                out, src = dst[:, (c * 2 + y) * P:(c * 2 + y + 1) * P], t[:, 2 * q + y, c * P:(c + 1) * P]
                            else:
                                out, src = dst[:, (y * 2 + c) * P:(y * 2 + c + 1) * P], t[:, c, (2 * q + y) * P:(2 * q + y + 1) * P]
                            last = nc.tensor.transpose(out, src, ident[:, :])
                    last.then_inc(ternT_ready, 1)
                pe.wait_ge(ternT_free, 1)
                pe.sem_inc(ternT_free, -1)

            def tile(ahead):
                pe.wait_ge(kn_ready, 1)
                pe.sem_inc(kn_ready, -1)
                for z in range(BT):
                    rows = slice(z * CTX, (z + 1) * CTX)
                    for t in range(XT):
                        cols = slice(t * P, (t + 1) * P)
                        last = nc.tensor.matmul(psM[t // 4][:, (t % 4) * P:(t % 4 + 1) * P], v[rows, cols], k[rows, cols],
                                                start=True, stop=True)
                        if t % 4 == 3:
                            last.then_inc(M_ready, 1)
                    pe.wait_ge(bd_ready, 1)
                    pe.sem_inc(bd_ready, -1)
                    if z == 1 and ahead:
                        transpose_rows()
                    for i in range(XT // 2):
                        if i >= 2:
                            pe.wait_ge(nl_ready, 1)
                            pe.sem_inc(nl_ready, -1)
                        if i == 2:
                            pe.wait_ge(bd_ready, 1)
                            pe.sem_inc(bd_ready, -1)
                        for y in range(2):
                            t = 2 * i + y
                            bank = psN[i % 2][:, y * E:(y + 1) * E]
                            nc.tensor.matmul(bank, bdh[:, t, :], woh[:, t, :], start=True, stop=False)
                            nc.tensor.matmul(bank, bdh[:, t, :], wol[:, t, :], start=False, stop=False)
                            last = nc.tensor.matmul(bank, bdl[:, t, :], woh[:, t, :], start=False, stop=True)
                        last.then_inc(N_ready, 1)
                    pe.wait_ge(nl_ready, 2)
                    pe.sem_inc(nl_ready, -2)
                if ahead:
                    project_rows()

            pe.wait_ge(const_in, 16)
            pe.sem_inc(const_in, -16)
            pe.wait_ge(small_in, 16 * len(w["vectors"]))
            pe.sem_inc(small_in, -(16 * len(w["vectors"])))
            nc.tensor.transpose(psN[1][:, 0:w["ncols"]], vecs[0:w["ncols"], :], ident[0:w["ncols"], 0:w["ncols"]]).then_inc(cols_ready, 1)
            transpose_rows()
            project_rows()
            transpose_rows()
            project_rows()
            for i, (_, cc, _) in enumerate(terns):
                ternary(i, cc)
            pe.wait_ge(wo_parts, 1)
            pe.sem_inc(wo_parts, -1)
            with pe.Fori(0, NTILE - 2):
                tile(True)
            tile(False)
            tile(False)


def mix_phase(nc, a, scr, w, out):
    with ExitStack() as ctx:
        def sb(name, shape, dt):
            return ctx.enter_context(nc.sbuf_tensor("p4_" + name, shape, dt))

        def ps(name, shape):
            return ctx.enter_context(nc.psum_tensor("p4_" + name, shape, F32))

        def sem(name):
            return ctx.enter_context(nc.semaphore("p4_" + name))

        RING = 3
        ident = sb("ident", [P, P], F32)
        eps = sb("eps", [P, TT], F32)
        mhalf = sb("mhalf", [P, TT], F32)
        o = sb("o", [P, C, S], F32)
        rden = sb("rden", [P, C, S], F32)
        xin = sb("xin", [P, TT, E], F32)
        x1 = sb("x1", [P, TT, E], F32)
        q0 = sb("q0", [P, TT, E], F32)
        z = sb("z", [P, TT, E], F32)
        base = sb("base", [P, TT, E], F32)
        x2 = sb("x2", [P, TT, E], F32)
        stats = sb("stats", [P, TT, 6], F32)
        mv = sb("mv", [P, TT, 2], F32)
        var = sb("var", [P, TT], F32)
        rstd = sb("rstd", [P, TT], F32)
        feat_f = sb("feat_f", [P, C, S], F32)
        feat_b = sb("feat_b", [P, C, S], F32)
        fh, fl = sb("fh", [P, C, S], F32R), sb("fl", [P, C, S], F32R)
        bh, bl = sb("bh", [P, C, S], F32R), sb("bl", [P, C, S], F32R)
        q = sb("q", [P, XT, S], F32)
        sq = sb("sq", [P, RING, S], F32)
        sh, sl = sb("sh", [P, RING, S], F32R), sb("sl", [P, RING, S], F32R)
        h = sb("h", [P, RING, S], F32)
        hh, hl = sb("hh", [P, RING, S], F32R), sb("hl", [P, RING, S], F32R)
        nw = [sb(f"n{i}", [P, XT, E], F32R) for i in range(2)]

        n2 = sb("n2", [XH * 4, S], F32)
        rstack = sb("rstack", [P, 2, S], F32R)
        idle = sb("idle", [P, 1], F32)

        psG = [ps(f"psG{i}", [P, S]) for i in range(RING)]
        psY = [ps(f"psY{i}", [P, S]) for i in range(C)]
        psT = [ps(f"psT{i}", [P, S]) for i in range(C)]
        psN = ps("psN", [P, S])

        oh, ol = hh[:, 0:C, :], hl[:, 0:C, :]

        const_in = sem("const_in")
        consts = sem("consts")
        act_go = sem("act_go")
        fetched = sem("fetched")
        o_in = sem("o_in")
        x_in = sem("x_in")
        ox_free = sem("ox_free")
        n_in = sem("n_in")
        n_free = sem("n_free")
        out_ready = sem("out_ready")
        out_done = sem("out_done")
        o_parts = sem("o_parts")
        step = sem("step")
        pool_step = sem("pool_step")
        var_ready = sem("var_ready")
        rs_ready = sem("rs_ready")
        z_ready = sem("z_ready")
        Y_ready = sem("Y_ready")
        feat_ready = sem("feat_ready")
        T_ready = sem("T_ready")
        u_ready = sem("u_ready")
        u_parts = sem("u_parts")
        tok_ready = sem("tok_ready")
        tok_free = sem("tok_free")
        q_ready = sem("q_ready")
        sq_ready = sem("sq_ready")
        sq_parts = sem("sq_parts")
        n2_ready = sem("n2_ready")
        norm_ready = sem("norm_ready")
        rn_ready = sem("rn_ready")
        g_ready = sem("g_ready")
        h_ready = sem("h_ready")
        h_parts = sem("h_parts")
        s_ready = sem("s_ready")
        qn_ready = sem("qn_ready")
        qh_ready = sem("qh_ready")
        qn_parts = sem("qn_parts")

        Z1_AT = 6
        W2_BACK = 1
        Z3_AT = 6
        HALF = XT // 2
        NORMS_AT = (HALF + RING - 2, 1)
        X2_AT, X1_AT = 1, 6
        O_BACK = 2
        CROSS_AT = (2, 3, 3, 4)
        X2_SUM, X2_NORM, BASE_AT = 1, 3, 4
        F_AT = (0, 2, 4)
        O_AT = 5
        Y_BACK = 1
        Z2_AT = 7
        Q_AT, S_AT, T_AT = FT, FT + XT, FT + 2 * XT

        out_ap = out

        block = ctx.enter_context(nc.Block())

        @block.sync
        def _(sp):
            def load_o(b):
                for c in range(C):
                    for i in range(8):
                        hd = c * 8 + i
                        sp.dma_start(o[i * D:(i + 1) * D, c, :], scr["o"][b, hd, 0:D, :]).then_inc(o_in, 16)
                        sp.dma_start(rden[i * D:(i + 1) * D, c, :],
                                     scr["rden"][b, hd:hd + 1, :].broadcast_to([D, S])).then_inc(o_in, 16)

            def load_x(b):
                sp.dma_start(xin[:, :, :], a["x"][b].rearrange("(t p) f -> p t f", p=P)).then_inc(x_in, 16)

            def load_n(b):
                for i in range(2):
                    sp.dma_start(nw[i][:, :, :].rearrange("p t n -> p (t n)").bitcast(F32), scr["n"][b, i]).then_inc(n_in, 16)

            def store(b):
                sp.wait_ge(out_ready, 1)
                sp.sem_inc(out_ready, -1)
                sp.dma_start(out_ap[b].rearrange("(t p) f -> p t f", p=P), x2[:, :, :]).then_inc(out_done, 16)

            def round_(b, old, more_o, more_n):
                if old:
                    store(b - 2)
                if more_o:
                    sp.wait_ge(ox_free, 1)
                    sp.sem_inc(ox_free, -1)
                    load_o(b + 2)
                    load_x(b + 2)
                if more_n:
                    sp.wait_ge(n_free, 1)
                    sp.sem_inc(n_free, -1)
                    load_n(b + 1)

            sp.dma_start(ident[:, :], a["ident"]).then_inc(const_in, 16)
            load_o(0)
            load_x(0)
            load_n(0)
            sp.wait_ge(ox_free, 1)
            sp.sem_inc(ox_free, -1)
            load_o(1)
            load_x(1)
            round_(0, False, True, True)
            round_(1, False, True, True)
            with sp.Fori(2, B - 2) as b:
                round_(b, True, True, True)
            round_(B - 2, True, False, True)
            round_(B - 1, True, False, False)
            store(B - 2)
            store(B - 1)
            sp.wait_ge(out_done, 16)

        @block.gpsimd
        def _(pool):
            def rsqrt():
                pool.wait_ge(var_ready, 1)
                pool.sem_inc(var_ready, -1)
                nc.gpsimd.tensor_tensor(var[:, :], mv[:, :, 1], eps[:, :], ALU.add).then_inc(pool_step, 1)
                pool.wait_ge(pool_step, 1)
                pool.sem_inc(pool_step, -1)
                nc.gpsimd.tensor_tensor(rstd[:, :], var[:, :], mhalf[:, :], ALU.pow).then_inc(rs_ready, 1)

            def low(m):
                s = m % RING
                pool.wait_ge(sq_ready, 1)
                pool.sem_inc(sq_ready, -1)
                nc.gpsimd.tensor_tensor(sl[:, s, :], sq[:, s, :], sh[:, s, :].bitcast(F32), ALU.subtract).then_inc(sq_parts, 1)

            def round_(back, front):
                if front:
                    rsqrt()
                    rsqrt()
                for m in range(XT):
                    if front:
                        low(m)
                    if back and m == X2_AT:
                        rsqrt()
                if front:
                    rsqrt()

            round_(False, True)
            with pool.Fori(1, B):
                round_(True, True)
            round_(True, False)

        @block.scalar
        def _(act):
            def evacuate(dst, bias):
                for c in range(C):
                    act.wait_ge(Y_ready, 1)
                    act.sem_inc(Y_ready, -1)
                    nc.scalar.activation(dst[:, c, :], psY[c][:, :], ACT.Identity, bias=bias[:, c:c + 1]).then_inc(feat_ready, 1)

            def affine(dst, g, b):
                act.wait_ge(T_ready, 1)
                act.sem_inc(T_ready, -1)
                for c in range(C):
                    nc.scalar.activation(dst[:, c, :], psT[c][:, :], ACT.Identity, bias=b[:, c:c + 1],
                                         scale=g[:, c:c + 1]).then_inc(u_ready, 1)

            def gelu(bias, m, bank):
                act.wait_ge(g_ready, 1)
                act.sem_inc(g_ready, -1)
                nc.scalar.activation(h[:, m % RING, :], psG[bank][:, :], ACT.Gelu, bias=bias[:, m:m + 1])
                nc.scalar.activation(hh[:, m % RING, :], psG[bank][:, :], ACT.Gelu, bias=bias[:, m:m + 1]).then_inc(h_ready, 1)

            def preload(func):
                nc.scalar.activation(idle[:, :], eps[:, 0:1], func).then_inc(fetched, 1)
                act.wait_ge(fetched, 1)
                act.sem_inc(fetched, -1)

            def norms(half):
                act.wait_ge(n2_ready, 1)
                act.sem_inc(n2_ready, -1)
                nc.scalar.activation(n2[:, :], (psY[0], psN)[half][0:XH * 4, :], ACT.Sqrt).then_inc(norm_ready, 1)

            def round_(old, back, front, more):
                if old:
                    evacuate(feat_f, w["fb2"])
                if back:
                    for m in range(FT):
                        gelu(w["b1"], m, m % RING)
                        if front and m == Z1_AT:
                            affine(feat_f, w["ln1_g"], w["ln1_b"])
                    evacuate(feat_b, w["b2"])
                elif front:
                    affine(feat_f, w["ln1_g"], w["ln1_b"])
                for m in range(XT):
                    if front:
                        bank = (Q_AT + m) % RING
                        act.wait_ge(q_ready, 1)
                        act.sem_inc(q_ready, -1)
                        nc.scalar.activation(q[:, m, :], psG[bank][:, :], ACT.Copy)
                        nc.scalar.activation(sq[:, m % RING, :], psG[bank][:, :], ACT.Square)
                        nc.scalar.activation(sh[:, m % RING, :], psG[bank][:, :], ACT.Square).then_inc(sq_ready, 1)
                        if m == NORMS_AT[0] - 1:
                            preload(ACT.Sqrt)
                        if m == NORMS_AT[0]:
                            norms(0)
                    if back and m == Z3_AT:
                        act.wait_ge(T_ready, 1)
                        act.sem_inc(T_ready, -1)
                        for c in range(C):
                            nc.scalar.activation(bh[:, c, :], psT[c][:, :], ACT.Copy).then_inc(u_ready, 1)
                if front:
                    if more:
                        evacuate(feat_f, w["bout"])
                    norms(1)
                    for m in range(XT):
                        act.wait_ge(qn_ready, 1)
                        act.sem_inc(qn_ready, -1)
                        nc.scalar.activation(sh[:, m % RING, :], sq[:, m % RING, :], ACT.Copy).then_inc(qh_ready, 1)
                    preload(ACT.Gelu)
                    evacuate(feat_f, w["bo"])
                if back:
                    for m in range(FT):
                        gelu(w["fb1"], m, (T_AT + m) % RING)
                if front:
                    affine(feat_b, w["ln2_g"], w["ln2_b"])

            act.wait_ge(act_go, 1)
            act.sem_inc(act_go, -1)
            preload(ACT.Gelu)
            evacuate(feat_f, w["bout"])
            round_(False, False, True, True)
            round_(False, True, True, True)
            with act.Fori(2, B - 1):
                round_(True, True, True, True)
            round_(True, True, True, False)
            round_(True, True, False, False)
            evacuate(feat_f, w["fb2"])

        @block.vector
        def _(dve):
            flat = "p c n -> p (c n)"

            def prepare_o():
                dve.wait_ge(o_in, 16 * 2 * H)
                dve.sem_inc(o_in, -(16 * 2 * H))
                nc.vector.tensor_tensor(o[:, :, :], o[:, :, :], rden[:, :, :], ALU.mult).then_inc(step, 1)
                dve.wait_ge(step, 1)
                dve.sem_inc(step, -1)
                nc.vector.tensor_copy(oh, o[:, :, :]).then_inc(step, 1)
                dve.wait_ge(step, 1)
                dve.sem_inc(step, -1)
                nc.vector.tensor_tensor(ol, o[:, :, :], oh.bitcast(F32), ALU.subtract).then_inc(o_parts, 1)

            def variance(src):
                for t in range(TT):
                    last = nc.vector.bn_stats(stats[:, t], src[:, t, :])
                last.then_inc(step, 1)
                dve.wait_ge(step, 1)
                dve.sem_inc(step, -1)
                for t in range(TT):
                    last = nc.vector.bn_aggr(mv[:, t, :], stats[:, t])
                last.then_inc(var_ready, 1)

            def normalise(dst, src, sem_):
                dve.wait_ge(rs_ready, 1)
                dve.sem_inc(rs_ready, -1)
                for t in range(TT):
                    last = nc.vector.tensor_scalar(dst[:, t, :], src[:, t, :], mv[:, t, 0:1], rstd[:, t:t + 1],
                                                   ALU.subtract, ALU.mult)
                last.then_inc(sem_, 1)

            def parts(hi, lo, src):
                for c in range(C):
                    dve.wait_ge(u_ready, 1)
                    dve.sem_inc(u_ready, -1)
                    nc.vector.tensor_copy(hi[:, c, :], src[:, c, :]).then_inc(step, 1)
                    dve.wait_ge(step, 1)
                    dve.sem_inc(step, -1)
                    nc.vector.tensor_tensor(lo[:, c, :], src[:, c, :], hi[:, c, :].bitcast(F32), ALU.subtract).then_inc(u_parts, 1)

            def add_back(dst, src, sem_):
                dve.wait_ge(tok_ready, 1)
                dve.sem_inc(tok_ready, -1)
                for i in range(2):
                    last = nc.vector.tensor_tensor(dst[:, 2 * i:2 * i + 2, :].rearrange("p t n -> p (t n)"), psT[i][:, :],
                                                   src[:, 2 * i:2 * i + 2, :].rearrange("p t n -> p (t n)"), ALU.add)
                last.then_inc(sem_, 1)
                nc.vector.engine_nop().then_inc(tok_free, 1)

            def hidden(m):
                s = m % RING
                dve.wait_ge(h_ready, 1)
                dve.sem_inc(h_ready, -1)
                nc.vector.tensor_tensor(hl[:, s, :], h[:, s, :], hh[:, s, :].bitcast(F32), ALU.subtract).then_inc(h_parts, 1)

            def inverse_norms(half):
                dve.wait_ge(norm_ready, 1)
                dve.sem_inc(norm_ready, -1)
                n, r = n2[:, :], rstack[:, half, :]
                nc.vector.tensor_scalar(n, n, 1e-12, None, ALU.max).then_inc(step, 1)
                dve.wait_ge(step, 1)
                dve.sem_inc(step, -1)
                nc.vector.reciprocal(n, n).then_inc(step, 1)
                dve.wait_ge(step, 1)
                dve.sem_inc(step, -1)
                nc.vector.tensor_copy(r[0:XH], n[0:XH])
                nc.vector.tensor_copy(r[32:32 + XH], n[32:32 + XH]).then_inc(step, 1)
                dve.wait_ge(step, 1)
                dve.sem_inc(step, -1)
                nc.vector.tensor_tensor(r[32:32 + XH], n[32:32 + XH], r[32:32 + XH].bitcast(F32), ALU.subtract).then_inc(rn_ready, 1)

            def add_x1():
                dve.wait_ge(x_in, 16)
                dve.sem_inc(x_in, -16)
                add_back(x1, xin, step)
                dve.wait_ge(step, 1)
                dve.sem_inc(step, -1)
                nc.vector.engine_nop().then_inc(ox_free, 1)

            def norm_x1():
                normalise(q0, x1, step)
                dve.wait_ge(step, 1)
                dve.sem_inc(step, -1)
                variance(q0)

            def add_mlp(old):
                if old:
                    dve.wait_ge(out_done, 16)
                    dve.sem_inc(out_done, -16)
                add_back(x2, base, step)
                dve.wait_ge(step, 1)
                dve.sem_inc(step, -1)
                variance(x2)

            def low_z3():
                for c in range(C):
                    dve.wait_ge(u_ready, 1)
                    dve.sem_inc(u_ready, -1)
                    nc.vector.tensor_tensor(bl[:, c, :], psT[c][:, :], bh[:, c, :].bitcast(F32), ALU.subtract).then_inc(u_parts, 1)

            def add_cross(dst, signal):
                for i in range(2):
                    d = dst[:, 2 * i:2 * i + 2, :].rearrange("p t n -> p (t n)")
                    last = nc.vector.tensor_tensor(d, psT[i][:, :], d, ALU.add)
                last.then_inc(signal, 1)

            def cross_q0():
                dve.wait_ge(tok_ready, 1)
                dve.sem_inc(tok_ready, -1)
                add_cross(q0, step)
                nc.vector.engine_nop().then_inc(n_free, 1)

            def variance_q0():
                dve.wait_ge(step, 1)
                dve.sem_inc(step, -1)
                variance(q0)

            def spread(m):
                if m < XT:
                    dve.wait_ge(s_ready, 1)
                    dve.sem_inc(s_ready, -1)
                    nc.vector.tensor_tensor(sq[:, m % RING, :], psG[(S_AT + m) % RING][:, :], q[:, m, :], ALU.mult).then_inc(qn_ready, 1)
                if m >= 1:
                    s = (m - 1) % RING
                    dve.wait_ge(qh_ready, 1)
                    dve.sem_inc(qh_ready, -1)
                    nc.vector.tensor_tensor(sl[:, s, :], sq[:, s, :], sh[:, s, :].bitcast(F32), ALU.subtract).then_inc(qn_parts, 1)

            def none(m):
                pass

            def beside(first, end, tile, extras):
                for m in range(first, end):
                    tile(m)
                    for f in extras.get(m, ()):
                        f()

            def round_(old, back, front, more):
                if back:
                    parts(bh, bl, feat_b)
                extras = {m: [] for m in range(-1, FT + 1)}
                if old:
                    extras[1].append(lambda: add_back(x2, x2, out_ready))
                if front:
                    extras[F_AT[0]].append(lambda: variance(x1))
                    extras[F_AT[1]].append(norm_x1)
                    extras[F_AT[2]].append(lambda: normalise(z, q0, z_ready))
                    extras[Z1_AT].append(lambda: parts(fh, fl, feat_f))
                beside(0, FT, hidden if back else none, extras)
                extras = {m: [] for m in range(-1, FT + 1)}
                if back:
                    extras[X2_SUM].append(lambda: add_mlp(old))
                    extras[X2_NORM].append(lambda: normalise(z, x2, z_ready))
                if front:
                    extras[BASE_AT].append(lambda: nc.vector.tensor_tensor(base[:, :, :], x1[:, :, :], q0[:, :, :], ALU.add))
                if front:
                    extras[NORMS_AT[0]].append(lambda: inverse_norms(0))
                if more:
                    extras[O_AT].append(prepare_o)
                if back:
                    extras[Z3_AT].append(low_z3)
                beside(0, XT, none, extras)
                if front:
                    extras = {NORMS_AT[1]: [lambda: inverse_norms(1)]}
                    if more:
                        extras[X1_AT] = [add_x1]
                    beside(0, XT + 1, spread, extras)
                extras = {m: [] for m in range(-1, FT + 1)}
                if front:
                    extras[CROSS_AT[0]].append(cross_q0)
                    extras[CROSS_AT[1]].append(variance_q0)
                    extras[CROSS_AT[2]].append(lambda: add_cross(base, tok_free))
                    extras[CROSS_AT[3]].append(lambda: normalise(z, q0, z_ready))
                beside(0, FT, hidden if back else none, extras)

            nc.vector.memset(eps[:, :], EPS)
            nc.vector.memset(mhalf[:, :], -0.5)
            nc.vector.memset(rstack[:, :, :].bitcast(F32), 0.0).then_inc(step, 1)
            dve.wait_ge(step, 1)
            dve.sem_inc(step, -1)
            nc.vector.engine_nop().then_inc(act_go, 1)
            dve.wait_ge(const_in, 16)
            dve.sem_inc(const_in, -16)
            nc.vector.engine_nop().then_inc(consts, 1)
            prepare_o()
            add_x1()
            round_(False, False, True, True)
            round_(False, True, True, True)
            with dve.Fori(2, B - 1):
                round_(True, True, True, True)
            round_(True, True, True, False)
            round_(True, True, False, False)
            add_back(x2, x2, out_ready)

        @block.tensor
        def _(pe):
            def product(bank, hi, lo, whi, wlo, start, stop):
                terms = [(whi, hi), (whi, lo)] + ([(wlo, hi)] if wlo is not None else [])
                for i, (ww, xx) in enumerate(terms):
                    last = nc.tensor.matmul(bank, ww, xx, start=start and i == 0, stop=stop and i == len(terms) - 1)
                return last

            def product_of(hi, lo, k, whi, wlo, first, last_):
                for c in range(C):
                    cols = slice(c * P, (c + 1) * P)
                    done = product(psY[c][:, :], hi, lo, whi[:, k, cols], wlo[:, k, cols] if wlo is not None else None, first, last_)
                    if last_:
                        done.then_inc(Y_ready, 1)

            def tile_of(bank, hi, lo, whi, wlo, m, signal, fresh=False):
                cols = slice(m * P, (m + 1) * P)
                for c in range(C):
                    if fresh:
                        pe.wait_ge(u_parts, 1)
                        pe.sem_inc(u_parts, -1)
                    done = product(psG[bank % RING][:, :], hi[:, c, :], lo[:, c, :], whi[:, c, cols],
                                   wlo[:, c, cols] if wlo is not None else None, c == 0, c == C - 1)
                done.then_inc(signal, 1)

            def transpose_rows():
                pe.wait_ge(z_ready, 1)
                pe.sem_inc(z_ready, -1)
                for t in range(TT):
                    for c in range(C):
                        last = nc.tensor.transpose(psT[c][:, t * P:(t + 1) * P], z[:, t, c * P:(c + 1) * P], ident[:, :])
                last.then_inc(T_ready, 1)

            def transpose_back(src):
                for t in range(TT):
                    for c in range(C):
                        at = ((t % 2) * C + c) * P
                        last = nc.tensor.transpose(psT[t // 2][:, at:at + P], src[:, c, t * P:(t + 1) * P], ident[:, :])
                last.then_inc(tok_ready, 1)

            def project_o():
                pe.wait_ge(o_parts, 1)
                pe.sem_inc(o_parts, -1)
                for k in range(C):
                    product_of(oh[:, k, :], ol[:, k, :], k, w["wout"][0], w["wout"][1], k == 0, k == C - 1)

            def second(k, w2):
                product_of(hh[:, k % RING, :], hl[:, k % RING, :], k, w2[0], w2[1], k == 0, k == FT - 1)

            def mlp(old, front):
                if old:
                    pe.wait_ge(feat_ready, C)
                    pe.sem_inc(feat_ready, -C)
                    transpose_back(feat_f)
                for m in range(FT + RING):
                    if m >= RING:
                        pe.wait_ge(h_parts, 1)
                        pe.sem_inc(h_parts, -1)
                        second(m - RING, w["w2"])
                    if m < FT:
                        tile_of(m, bh, bl, w["w1"][0], w["w1"][1], m, g_ready, m == 0)
                    if old and m == Z1_AT - 1:
                        pe.wait_ge(tok_free, 1)
                        pe.sem_inc(tok_free, -1)
                    if front and m == Z1_AT:
                        transpose_rows()

            def queries(back, more):
                for m in range(XT + RING):
                    if m >= RING:
                        k = m - RING
                        sums = (psY[0], psN)[k // HALF]
                        pe.wait_ge(sq_parts, 1)
                        pe.sem_inc(sq_parts, -1)
                        nc.tensor.matmul(sums[:, :], w["sum_sel"][:, k, :], sh[:, k % RING, :], start=(k % HALF == 0), stop=False)
                        last = nc.tensor.matmul(sums[:, :], w["sum_sel"][:, k, :], sl[:, k % RING, :], start=False,
                                                stop=(k % HALF == HALF - 1))
                        if k % HALF == HALF - 1:
                            last.then_inc(n2_ready, 1)
                    if m < XT:
                        tile_of(Q_AT + m, fh, fl, w["wq"][0], w["wq"][1], m, q_ready, m == 0)
                    if back and m == W2_BACK:
                        pe.wait_ge(feat_ready, C)
                        pe.sem_inc(feat_ready, -C)
                        transpose_back(feat_b)
                    if back and m == Z3_AT:
                        pe.wait_ge(tok_free, 1)
                        pe.sem_inc(tok_free, -1)
                        transpose_rows()
                    if m == XT:
                        pe.wait_ge(rn_ready, 1)
                        pe.sem_inc(rn_ready, -1)
                        if more:
                            project_o()
                    if m > XT:
                        spread(m - XT - 1)

            def spread(m):
                nc.tensor.matmul(psG[(S_AT + m) % RING][:, :], w["spread_sel"][:, m, :], rstack[:, m // HALF, :], start=True,
                                 stop=True).then_inc(s_ready, 1)

            def cross(back, more):
                if back:
                    pe.wait_ge(u_parts, C)
                    pe.sem_inc(u_parts, -C)
                pe.wait_ge(n_in, 32)
                pe.sem_inc(n_in, -32)
                for m in range(2, XT + RING):
                    if m >= RING:
                        k = m - RING
                        pe.wait_ge(qn_parts, 1)
                        pe.sem_inc(qn_parts, -1)
                        product_of(sh[:, k % RING, :], sl[:, k % RING, :], k, nw[0], nw[1], k == 0, k == XT - 1)
                    if m == HALF:
                        pe.wait_ge(rn_ready, 1)
                        pe.sem_inc(rn_ready, -1)
                    if m < XT:
                        spread(m)
                    if more and m == O_BACK:
                        pe.wait_ge(feat_ready, C)
                        pe.sem_inc(feat_ready, -C)
                        transpose_back(feat_f)
                if more:
                    pe.wait_ge(tok_free, 1)
                    pe.sem_inc(tok_free, -1)

            def ternary(front):
                for m in range(FT + RING):
                    if m >= RING:
                        pe.wait_ge(h_parts, 1)
                        pe.sem_inc(h_parts, -1)
                        second(m - RING, (w["t2"], None))
                    if m < FT:
                        tile_of(T_AT + m, bh, bl, w["t1"], None, m, g_ready)
                    if front and m == Y_BACK:
                        pe.wait_ge(feat_ready, C)
                        pe.sem_inc(feat_ready, -C)
                        transpose_back(feat_f)
                    if front and m == Z2_AT:
                        pe.wait_ge(tok_free, 1)
                        pe.sem_inc(tok_free, -1)
                        transpose_rows()

            def round_(old, back, front, more):
                if back:
                    mlp(old, front)
                elif front:
                    transpose_rows()
                if front:
                    queries(back, more)
                else:
                    pe.wait_ge(feat_ready, C)
                    pe.sem_inc(feat_ready, -C)
                    transpose_back(feat_b)
                    pe.wait_ge(tok_free, 1)
                    pe.sem_inc(tok_free, -1)
                    transpose_rows()
                    pe.wait_ge(u_parts, C)
                    pe.sem_inc(u_parts, -C)
                if front:
                    cross(back, more)
                if back:
                    ternary(front)
                else:
                    pe.wait_ge(feat_ready, C)
                    pe.sem_inc(feat_ready, -C)
                    transpose_back(feat_f)
                    pe.wait_ge(tok_free, 1)
                    pe.sem_inc(tok_free, -1)
                    transpose_rows()

            pe.wait_ge(consts, 1)
            pe.sem_inc(consts, -1)
            project_o()
            pe.wait_ge(feat_ready, C)
            pe.sem_inc(feat_ready, -C)
            transpose_back(feat_f)
            pe.wait_ge(tok_free, 1)
            pe.sem_inc(tok_free, -1)
            round_(False, False, True, True)
            round_(False, True, True, True)
            with pe.Fori(2, B - 1):
                round_(True, True, True, True)
            round_(True, True, True, False)
            round_(True, True, False, False)
            pe.wait_ge(feat_ready, C)
            pe.sem_inc(feat_ready, -C)
            transpose_back(feat_f)


def decoder_block(nc, a, out):
    def dram(name, shape, dt=F32):
        return nc.dram_tensor(name, shape, dt).ap()

    scr = {"q": dram("q_parts", [3, H * D, B, S], BF16), "k": dram("k_parts", [3, KVH * D, B, S], BF16),
           "v": dram("v_ones", [B, KVH, P, TT * 2 * D]), "o": dram("o_sums", [B, H, D + 1, S]),
           "rden": dram("rden", [B, H, S]), "n": dram("n_parts", [B, 2, P, XT * E])}
    project_phase(nc, a, scr)
    with ExitStack() as ctx:
        w = mixing_weights(nc, ctx)
        with ExitStack() as until_n:
            cw = context_weights(nc, until_n)
            attend_phase(nc, a, scr, split_list(a, w, cw))
            prepare_phase(nc, a, scr, w, cw)
        mix_phase(nc, a, scr, w, out)


def mixing_weights(nc, ctx):
    def sb(name, shape, dt):
        return ctx.enter_context(nc.sbuf_tensor("w_" + name, shape, dt))

    w = {name: (sb(name + "_hi", [P, k, n], F32R), sb(name + "_lo", [P, k, n], F32R))
         for name, k, n in (("wout", C, E), ("wq", C, XI), ("w1", C, FT * P), ("w2", FT, E))}
    w["t1"] = sb("t1", [P, C, FT * P], F32R)
    w["t2"] = sb("t2", [P, FT, E], F32R)
    w["sum_sel"] = sb("sum_sel", [P, XT, P], F32R)
    w["spread_sel"] = sb("spread_sel", [P, XT, P], F32R)
    vectors = (("bout", "L0_attn_bout", C), ("ln1_g", "L0_xattn_ln1_g", C), ("ln1_b", "L0_xattn_ln1_b", C),
               ("ln2_g", "L0_xattn_ln2_g", C), ("ln2_b", "L0_xattn_ln2_b", C), ("bo", "L0_xattn_bo", C),
               ("b1", "L0_xattn_b1", FT), ("b2", "L0_xattn_b2", C), ("fb1", "L0_ffn_b1", FT), ("fb2", "L0_ffn_b2", C))
    w["ncols"] = sum(k for _, _, k in vectors)
    w["all_columns"] = sb("columns", [P, w["ncols"]], F32)
    w["vectors"] = []
    at = 0
    for name, source, k in vectors:
        w[name] = w["all_columns"][:, at:at + k]
        w["vectors"].append((source, at, k))
        at += k
    return w


def context_weights(nc, ctx):
    return {name: tuple(ctx.enter_context(nc.sbuf_tensor(f"c_{name}_{part}", [P, k, n], F32R)) for part in ("hi", "lo"))
            for name, k, n in (("wk", C, XI), ("wv", C, XI))}


def split_list(a, w, cw):
    some = SPLIT // P
    selectors = [(a["selectors"][i, t:t + some].rearrange("t p m -> p t m"), dst[:, t:t + some, :], None)
                 for i, dst in enumerate((w["sum_sel"], w["spread_sel"])) for t in range(0, XT, some)]
    def piece(at, n):
        return slice(at, min(at + SPLIT, n))

    return selectors + [(a[source][c * P:(c + 1) * P, piece(at, hi.shape[2])], hi[:, c, piece(at, hi.shape[2])], lo[:, c, piece(at, hi.shape[2])])
            for source, (hi, lo) in (("L0_xattn_wk", cw["wk"]), ("L0_xattn_wv", cw["wv"]),
                                     ("L0_attn_Wout", w["wout"]), ("L0_xattn_w1", w["w1"]), ("L0_xattn_w2", w["w2"]),
                                     ("L0_xattn_wq", w["wq"]))
            for c in range(hi.shape[1]) for at in range(0, hi.shape[2], SPLIT)]


def split_weights(nc, pool, stage, stage_in, hi_done, lo_done, splits):
    def staged(i):
        shape = splits[i][0].shape
        if len(shape) == 3:
            return stage[i % 2][:, 0:shape[1] * shape[2]].rearrange("p (t m) -> p t m", t=shape[1])
        return stage[i % 2][:, 0:shape[1]]

    def load(i):
        pool.dma_start(staged(i), splits[i][0]).then_inc(stage_in[i % 2], 16)

    load(0)
    for i, (src, hi, lo) in enumerate(splits):
        if i + 1 < len(splits):
            if i >= 1:
                pool.wait_ge(lo_done, 1)
                pool.sem_inc(lo_done, -1)
            load(i + 1)
        whole = staged(i)
        pool.wait_ge(stage_in[i % 2], 16 * (i // 2 + 1))
        if lo is None:
            nc.gpsimd.tensor_copy(hi, whole).then_inc(lo_done, 1)
            continue
        nc.gpsimd.tensor_copy(hi, whole).then_inc(hi_done, 1)
        pool.wait_ge(hi_done, 1)
        pool.sem_inc(hi_done, -1)
        nc.gpsimd.tensor_tensor(lo, whole, hi.bitcast(F32), ALU.subtract).then_inc(lo_done, 1)


_INS = ["x", "ctx_1024", "L0_attn_Wqa", "L0_attn_Wqb", "L0_attn_Wkva", "L0_attn_Wkvb", "L0_attn_Wout", "L0_attn_bout",
        "L0_xattn_wq", "L0_xattn_wk", "L0_xattn_wv", "L0_xattn_wo", "L0_xattn_bo", "L0_xattn_w1", "L0_xattn_b1",
        "L0_xattn_w2", "L0_xattn_b2", "L0_xattn_ln1_g", "L0_xattn_ln1_b", "L0_xattn_ln2_g", "L0_xattn_ln2_b",
        "L0_ffn_W1", "L0_ffn_b1", "L0_ffn_W2", "L0_ffn_b2"]


def kernel(**inputs):
    import numpy as _np
    import concourse.bacc as _bacc
    from concourse import mybir as _mybir
    from concourse.bass_utils import run_bass_kernel_spmd as _run

    nc = _bacc.Bacc("TRN2", target_bir_lowering=False, num_devices=1)
    given = {name: _np.ascontiguousarray(inputs[name]) for name in _INS}
    given["rope"] = rope_tables()
    given["ident"] = _np.eye(P, dtype=_np.float32)
    given["mask"] = _np.stack([causal_mask(), _np.ascontiguousarray(causal_mask().T)])
    given["selectors"] = head_selectors()
    arrays, args = {}, {}
    for name, array in given.items():
        arrays[f"in_{name}_dram"] = array
        args[name] = nc.dram_tensor(f"in_{name}_dram", array.shape, _mybir.dt.from_np(array.dtype), kind="ExternalInput").ap()
    out = nc.dram_tensor("out_0_dram", (B, S, E), F32, kind="ExternalOutput").ap()
    decoder_block(nc, args, out)
    r = _run(nc, [arrays], core_ids=[0])
    return r.results[0]["out_0_dram"]
```

```python
from contextlib import ExitStack

import numpy as np
import concourse.bass as bass
from concourse import mybir

F32 = mybir.dt.float32
F32R = mybir.dt.float32r
BF16 = mybir.dt.bfloat16
ALU = mybir.AluOpType
ACT = mybir.ActivationFunctionType
AX_X = mybir.AxisListType.X

P = 128
B = 8
S = 512
TT = S // P
E = 256
C = E // P
H = 16
KVH = 4
G = H // KVH
D = E // H
QL = 64
KVL = 32
R = QL + KVL
XH = 16
XD = 64
XI = XH * XD
XT = XI // P
CTX = 64
FT = 1024 // P
EPS = 1e-5
ROPE_BASE = 10000.0
SCALE = float(D) ** -0.5
MASKED = -3.0e38

PAIRS = [(0, 0), (0, 1), (0, 2), (1, 0), (1, 1), (2, 0)]
PARTS = 3
SROWS = len(PAIRS) * D
MROWS = 3
SPLIT = 512


def rope_tables():
    inv = (1.0 / ROPE_BASE ** (np.arange(0, D, 2, dtype=np.float32) / np.float32(D))).astype(np.float32)
    angle = np.outer(inv, np.arange(S, dtype=np.float32)).astype(np.float32)
    cos = np.repeat(np.cos(angle), 2, axis=0)
    sin = np.repeat(np.sin(angle), 2, axis=0)
    sin[0::2] *= -1.0
    n = P // D
    return np.stack([np.tile(cos, (n, 1)), np.tile(sin, (n, 1))]).astype(np.float32)


def causal_mask():
    q = np.arange(P)
    return np.where(q[None, :] <= q[:, None], 0.0, MASKED).astype(np.float32)


def head_selectors():
    sums = np.zeros((XT, P, P), np.float32)
    spread = np.zeros((XT, P, P), np.float32)
    for t in range(XT):
        for p in range(P):
            h = 2 * t + p // XD
            sums[t, p, h::XH] = 1.0
            spread[t, h, p] = 1.0
            spread[t, 32 + h, p] = 1.0
    return np.stack([sums, spread])


def project_phase(nc, a, scr):
    with ExitStack() as ctx:
        def sb(name, shape, dt):
            return ctx.enter_context(nc.sbuf_tensor("p1_" + name, shape, dt))

        def ps(name, shape):
            return ctx.enter_context(nc.psum_tensor("p1_" + name, shape, F32))

        def sem(name):
            return ctx.enter_context(nc.semaphore("p1_" + name))

        UNITS = 3
        RING = 2 * UNITS
        T0_AT = 3
        NOUT = (6 * 16, 6 * 16, 3 * 16)
        KW = KVH * D

        ident = sb("ident", [P, P], F32)
        wa = sb("wa", [P, C, R], F32)
        wq = sb("wq", [R, E], F32)
        wq_swap = sb("wq_swap", [R, E], F32)
        wkv = sb("wkv", [R, KVH, D, 2], F32)
        wk = sb("wk", [R, KW], F32)
        wk_swap = sb("wk_swap", [R, KW], F32)
        wv = sb("wv", [R, KW], F32)
        cos = sb("cos", [P, S], F32)
        sin = sb("sin", [P, S], F32)
        eps = sb("eps", [P, TT], F32)
        minus_half = sb("minus_half", [P, TT], F32)
        x = sb("x", [P, 2, TT, E], F32)
        stats = sb("stats", [P, 2, TT, 6], F32)
        mv = sb("mv", [P, 2, TT, 2], F32)
        var = sb("var", [P, 2, TT], F32)
        rstd = sb("rstd", [P, 2, TT], F32)
        xn = sb("xn", [P, 2, TT, E], F32)
        xnT = sb("xnT", [P, 2, C, S], F32)
        low = sb("low", [R, 2, S], F32)
        lowh, lowl = sb("lowh", [R, 2, S], F32R), sb("lowl", [R, 2, S], F32R)
        wh, wl = sb("wh", [R, 2 * E + 2 * KW], F32R), sb("wl", [R, 2 * E + 2 * KW], F32R)
        xc = sb("xc", [P, RING, S], F32)
        xs = sb("xs", [P, RING, S], F32)
        rot = sb("rot", [P, RING, S], F32)
        rem = sb("rem", [P, RING, S], F32)
        part = [sb(f"part{i}", [P, RING, S], BF16) for i in range(3)]
        v = sb("v", [P, 2, KVH, TT, 2 * D], F32)

        psT = [ps(f"psT{c}", [P, S]) for c in range(C)]
        psL = ps("psL", [P, S])
        psX = [ps(f"psX{i}", [P, S]) for i in range(2)]
        psR = [ps(f"psR{i}", [P, S]) for i in range(2)]
        psV = ps("psV", [P, TT, KVH, D])
        low_bank = (psL, psT[0])

        zeroed = sem("zeroed")
        loaded = sem("loaded")
        weights_pe = sem("weights_pe")
        x_in = [sem(f"x_in{k}") for k in range(2)]
        x_free = sem("x_free")
        dve_step = sem("dve_step")
        pool_step = sem("pool_step")
        stats_ready = sem("stats_ready")
        rstd_ready = sem("rstd_ready")
        xn_ready = sem("xn_ready")
        T_ready = sem("T_ready")
        xnT_ready = sem("xnT_ready")
        L_ready = sem("L_ready")
        low_ready = sem("low_ready")
        low_parts = sem("low_parts")
        XR_ready = sem("XR_ready")
        XR_free = sem("XR_free")
        turned = sem("turned")
        rot_ready = sem("rot_ready")
        hi_ready = sem("hi_ready")
        rem_ready = sem("rem_ready")
        mid_ready = sem("mid_ready")
        parts_ready = sem("parts_ready")
        parts_out = [sem(f"parts_out{i}") for i in range(RING)]
        V_ready = sem("V_ready")
        V_free = sem("V_free")
        v_ready = sem("v_ready")
        v_out = [sem(f"v_out{k}") for k in range(2)]

        block = ctx.enter_context(nc.Block())

        @block.sync
        def _(sp):
            sp.wait_ge(zeroed, 2)
            sp.sem_inc(zeroed, -2)
            for dst, src in ((wa[:, :, 0:QL], a["L0_attn_Wqa"].rearrange("(c p) r -> p c r", p=P)),
                             (wa[:, :, QL:R], a["L0_attn_Wkva"].rearrange("(c p) r -> p c r", p=P)),
                             (wq[0:QL, :], a["L0_attn_Wqb"]),
                             (wkv[QL:R, :, :, :].rearrange("r k d z -> r (k d z)"), a["L0_attn_Wkvb"]),
                             (cos[:, :], a["rope"][0]), (sin[:, :], a["rope"][1]), (ident[:, :], a["ident"])):
                sp.dma_start(dst, src).then_inc(loaded, 16)

            def load(b, k):
                sp.dma_start(x[:, k], a["x"][b].rearrange("(t p) f -> p t f", p=P)).then_inc(x_in[k], 16)

            def stores(b, k):
                sp.wait_ge(v_ready, 1)
                sp.sem_inc(v_ready, -1)
                sp.dma_start(scr["v"][b].rearrange("g p n -> p g n"),
                             v[:, k].rearrange("p g t n -> p g (t n)")).then_inc(v_out[k], 16)
                for u in range(UNITS):
                    n = k * UNITS + u
                    sp.wait_ge(parts_ready, 1)
                    sp.sem_inc(parts_ready, -1)
                    for i in range(3):
                        if u < 2:
                            for z in range(2):
                                g = 2 * u + z
                                sp.dma_start(scr["q"][i, g, :, b, :].rearrange("d (h t) -> h d t", h=G),
                                             part[i][z * G * D:(z + 1) * G * D, n, :]).then_inc(parts_out[n], 16)
                        else:
                            sp.dma_start(scr["k"][i, :, b, :], part[i][0:KW, n, :]).then_inc(parts_out[n], 16)

            for k in range(2):
                load(k, k)
            for k in range(2):
                sp.wait_ge(x_free, 1)
                sp.sem_inc(x_free, -1)
                load(2 + k, k)
            with sp.Fori(0, B // 2 - 2) as it:
                for k in range(2):
                    sp.wait_ge(x_free, 1)
                    sp.sem_inc(x_free, -1)
                    load(2 * it + (4 + k), k)
                for k in range(2):
                    stores(2 * it + k, k)
            for k in range(2):
                stores(B - 4 + k, k)
                sp.wait_ge(x_free, 1)
                sp.sem_inc(x_free, -1)
            for k in range(2):
                stores(B - 2 + k, k)
            for k in range(2):
                sp.wait_ge(v_out[k], 16)
            for n in range(RING):
                sp.wait_ge(parts_out[n], NOUT[n % UNITS])

        @block.vector
        def _(dve):
            nc.vector.memset(wq[:, :], 0.0).then_inc(zeroed, 1)
            nc.vector.memset(wkv[:, :, :, :], 0.0).then_inc(zeroed, 1)
            nc.vector.memset(v[:, :, :, :, :], 1.0)
            nc.vector.memset(eps[:, :], EPS)
            nc.vector.memset(minus_half[:, :], -0.5)
            dve.wait_ge(loaded, 7 * 16)
            dve.sem_inc(loaded, -(7 * 16))
            q2, s2 = (z[:, :].rearrange("r (n two) -> r n two", two=2) for z in (wq, wq_swap))
            nc.vector.tensor_copy(s2[:, :, 0], q2[:, :, 1])
            nc.vector.tensor_copy(s2[:, :, 1], q2[:, :, 0])
            for g in range(KVH):
                cols = slice(g * D, (g + 1) * D)
                src = wkv[:, g, :, 0].rearrange("r (n two) -> r n two", two=2)
                dst = wk_swap[:, cols].rearrange("r (n two) -> r n two", two=2)
                nc.vector.tensor_copy(dst[:, :, 0], src[:, :, 1])
                nc.vector.tensor_copy(dst[:, :, 1], src[:, :, 0])
                nc.vector.tensor_copy(wk[:, cols], wkv[:, g, :, 0])
                last = nc.vector.tensor_copy(wv[:, cols], wkv[:, g, :, 1])
            last.then_inc(dve_step, 1)
            dve.wait_ge(dve_step, 1)
            dve.sem_inc(dve_step, -1)
            at = 0
            for src, n in ((wq, E), (wq_swap, E), (wk, KW), (wk_swap, KW)):
                nc.vector.tensor_copy(wh[:, at:at + n], src[:, :]).then_inc(dve_step, 1)
                dve.wait_ge(dve_step, 1)
                dve.sem_inc(dve_step, -1)
                last = nc.vector.tensor_tensor(wl[:, at:at + n], src[:, :], wh[:, at:at + n].bitcast(F32), ALU.subtract)
                at += n
            last.then_inc(weights_pe, 1)

            def moments(k):
                dve.wait_ge(x_in[k], 16)
                dve.sem_inc(x_in[k], -16)
                for t in range(TT):
                    last = nc.vector.bn_stats(stats[:, k, t], x[:, k, t, :])
                last.then_inc(dve_step, 1)
                dve.wait_ge(dve_step, 1)
                dve.sem_inc(dve_step, -1)
                for t in range(TT):
                    last = nc.vector.bn_aggr(mv[:, k, t, :], stats[:, k, t])
                last.then_inc(stats_ready, 1)

            def normalise(k):
                dve.wait_ge(rstd_ready, 1)
                dve.sem_inc(rstd_ready, -1)
                for t in range(TT):
                    last = nc.vector.tensor_scalar(xn[:, k, t, :], x[:, k, t, :], mv[:, k, t, 0:1],
                                                   rstd[:, k, t:t + 1], ALU.subtract, ALU.mult)
                last.then_inc(xn_ready, 1)
                nc.vector.engine_nop().then_inc(x_free, 1)

            def low_part(k):
                dve.wait_ge(low_ready, 1)
                dve.sem_inc(low_ready, -1)
                nc.vector.tensor_tensor(lowl[:, k, :], low[:, k, :], lowh[:, k, :].bitcast(F32), ALU.subtract).then_inc(low_parts, 1)

            def pair(ahead):
                for step in range(RING + 3):
                    if step < RING:
                        rows = P if step % UNITS < 2 else KW
                        dve.wait_ge(XR_ready, 1)
                        dve.sem_inc(XR_ready, -1)
                        nc.vector.tensor_tensor(xc[0:rows, step], psX[step % 2][0:rows, :], cos[0:rows, :], ALU.mult)
                        nc.vector.tensor_tensor(xs[0:rows, step], psR[step % 2][0:rows, :], sin[0:rows, :],
                                                ALU.mult).then_inc(turned, 1)
                        nc.vector.engine_nop().then_inc(XR_free, 1)
                    if 2 <= step < RING + 2:
                        n = step - 2
                        rows = P if n % UNITS < 2 else KW
                        dve.wait_ge(hi_ready, 1)
                        dve.sem_inc(hi_ready, -1)
                        nc.vector.tensor_tensor(rem[0:rows, n], rot[0:rows, n], part[0][0:rows, n],
                                                ALU.subtract).then_inc(rem_ready, 1)
                    if step >= 3:
                        n = step - 3
                        rows = P if n % UNITS < 2 else KW
                        dve.wait_ge(mid_ready, 1)
                        dve.sem_inc(mid_ready, -1)
                        nc.vector.tensor_tensor(part[2][0:rows, n], rem[0:rows, n], part[1][0:rows, n],
                                                ALU.subtract).then_inc(parts_ready, 1)
                    if ahead and step < 2:
                        moments(step)
                    elif ahead and step < 4:
                        normalise(step - 2)
                if ahead:
                    low_part(0)
                    low_part(1)

            for k in range(2):
                moments(k)
            for k in range(2):
                normalise(k)
            low_part(0)
            low_part(1)
            with dve.Fori(0, B // 2 - 1):
                pair(True)
            pair(False)

        @block.gpsimd
        def _(pool):
            def rsqrt(k):
                pool.wait_ge(stats_ready, 1)
                pool.sem_inc(stats_ready, -1)
                nc.gpsimd.tensor_tensor(var[:, k], mv[:, k, :, 1], eps[:, :], ALU.add).then_inc(pool_step, 1)
                pool.wait_ge(pool_step, 1)
                pool.sem_inc(pool_step, -1)
                nc.gpsimd.tensor_tensor(rstd[:, k], var[:, k], minus_half[:, :], ALU.pow).then_inc(rstd_ready, 1)

            def pair(ahead):
                for step in range(RING):
                    rows = P if step % UNITS < 2 else KW
                    pool.wait_ge(turned, 1)
                    pool.sem_inc(turned, -1)
                    nc.gpsimd.tensor_tensor(rot[0:rows, step], xc[0:rows, step], xs[0:rows, step], ALU.add).then_inc(rot_ready, 1)
                    if ahead and step < 2:
                        rsqrt(step)

            for k in range(2):
                rsqrt(k)
            with pool.Fori(0, B // 2 - 1):
                pair(True)
            pair(False)

        @block.scalar
        def _(act):
            for n in range(RING):
                act.sem_inc(parts_out[n], NOUT[n % UNITS])
            for k in range(2):
                act.sem_inc(v_out[k], 16)
            def transposed(k):
                act.wait_ge(T_ready, 1)
                act.sem_inc(T_ready, -1)
                nc.scalar.activation(xnT[:, k, 0, :], psT[0][:, :], ACT.Copy)
                nc.scalar.activation(xnT[:, k, 1, :], psT[1][:, :], ACT.Copy).then_inc(xnT_ready, 1)

            def low_rank(k):
                act.wait_ge(L_ready, 1)
                act.sem_inc(L_ready, -1)
                nc.scalar.activation(low[:, k, :], low_bank[k][0:R, :], ACT.Copy)
                nc.scalar.activation(lowh[:, k, :], low_bank[k][0:R, :], ACT.Copy).then_inc(low_ready, 1)

            def pair(ahead):
                for step in range(RING + 2):
                    if step < RING:
                        k, u = divmod(step, UNITS)
                        rows = P if u < 2 else KW
                        if u == 0:
                            act.wait_ge(V_ready, 1)
                            act.sem_inc(V_ready, -1)
                            act.wait_ge(v_out[k], 16)
                            act.sem_inc(v_out[k], -16)
                            nc.scalar.activation(v[:, k, :, :, 0:D].rearrange("p g t d -> p t g d"), psV[:, :, :, :],
                                                 ACT.Copy).then_inc(V_free, 1)
                            act.drain().then_inc(v_ready, 1)
                        if ahead and step == T0_AT:
                            transposed(0)
                        act.wait_ge(rot_ready, 1)
                        act.sem_inc(rot_ready, -1)
                        act.wait_ge(parts_out[step], NOUT[u])
                        act.sem_inc(parts_out[step], -(NOUT[u]))
                        nc.scalar.activation(part[0][0:rows, step], rot[0:rows, step], ACT.Copy).then_inc(hi_ready, 1)
                    if step == RING and ahead:
                        transposed(1)
                    if step >= 2:
                        n = step - 2
                        rows = P if n % UNITS < 2 else KW
                        act.wait_ge(rem_ready, 1)
                        act.sem_inc(rem_ready, -1)
                        nc.scalar.activation(part[1][0:rows, n], rem[0:rows, n], ACT.Copy).then_inc(mid_ready, 1)
                if ahead:
                    low_rank(0)
                    low_rank(1)

            for k in range(2):
                transposed(k)
            low_rank(0)
            low_rank(1)
            with act.Fori(0, B // 2 - 1):
                pair(True)
            pair(False)

        @block.tensor
        def _(pe):
            pe.wait_ge(weights_pe, 1)
            pe.sem_inc(weights_pe, -1)
            pe.sem_inc(XR_free, 2)
            pe.sem_inc(V_free, 1)

            def transpose_rows(k):
                pe.wait_ge(xn_ready, 1)
                pe.sem_inc(xn_ready, -1)
                for t in range(TT):
                    for c in range(C):
                        last = nc.tensor.transpose(psT[c][:, t * P:(t + 1) * P], xn[:, k, t, c * P:(c + 1) * P], ident[:, :])
                last.then_inc(T_ready, 1)

            def low_rank(k):
                for c in range(C):
                    last = nc.tensor.matmul(low_bank[k][0:R, :], wa[:, c, :], xnT[:, k, c, :], start=(c == 0), stop=(c == C - 1))
                last.then_inc(L_ready, 1)

            def values(k):
                pe.wait_ge(V_free, 1)
                pe.sem_inc(V_free, -1)
                for t in range(TT):
                    last = nc.tensor.matmul(psV[:, t, :, :].rearrange("p g d -> p (g d)"), low[:, k, t * P:(t + 1) * P],
                                            wv[:, :], start=True, stop=True)
                last.then_inc(V_ready, 1)

            def unit(step):
                k, u = divmod(step, UNITS)
                rows = P if u < 2 else KW
                at, twin = (u * P, E + u * P) if u < 2 else (2 * E, 2 * E + KW)
                pe.wait_ge(XR_free, 1)
                pe.sem_inc(XR_free, -1)
                for bank, col in ((psX, at), (psR, twin)):
                    out = bank[step % 2][0:rows, :]
                    cols = slice(col, col + rows)
                    nc.tensor.matmul(out, wh[:, cols], lowh[:, k, :], start=True, stop=False)
                    nc.tensor.matmul(out, wl[:, cols], lowh[:, k, :], start=False, stop=False)
                    last = nc.tensor.matmul(out, wh[:, cols], lowl[:, k, :], start=False, stop=True)
                last.then_inc(XR_ready, 1)

            def pair(ahead):
                pe.wait_ge(low_parts, 1)
                pe.sem_inc(low_parts, -1)
                values(0)
                unit(0)
                unit(1)
                unit(2)
                pe.wait_ge(low_parts, 1)
                pe.sem_inc(low_parts, -1)
                values(1)
                unit(3)
                unit(4)
                if ahead:
                    transpose_rows(0)
                unit(5)
                if ahead:
                    pe.wait_ge(xnT_ready, 1)
                    pe.sem_inc(xnT_ready, -1)
                    transpose_rows(1)
                    low_rank(0)
                    pe.wait_ge(xnT_ready, 1)
                    pe.sem_inc(xnT_ready, -1)
                    low_rank(1)

            transpose_rows(0)
            pe.wait_ge(xnT_ready, 1)
            pe.sem_inc(xnT_ready, -1)
            transpose_rows(1)
            low_rank(0)
            pe.wait_ge(xnT_ready, 1)
            pe.sem_inc(xnT_ready, -1)
            low_rank(1)
            with pe.Fori(0, B // 2 - 1):
                pair(True)
            pair(False)


def attend_phase(nc, a, scr, splits):
    with ExitStack() as ctx:
        def sb(name, shape, dt):
            return ctx.enter_context(nc.sbuf_tensor("p2_" + name, shape, dt))

        def ps(name, shape):
            return ctx.enter_context(nc.psum_tensor("p2_" + name, shape, F32))

        def sem(name):
            return ctx.enter_context(nc.semaphore("p2_" + name))

        ident = sb("ident", [P, P], F32)
        ident_b = sb("ident_b", [P, P], BF16)
        SB = 3
        mask = sb("mask", [P, P], F32)
        mask_b = sb("mask_b", [P, P], BF16)
        qs = sb("qs", [P, 2, H, S], BF16)
        ks = sb("ks", [P, 2, KVH, S], BF16)
        v = sb("v", [P, 2, KVH, TT, 2 * D], F32)
        mx = sb("mx", [P, H, TT], F32)
        mparts = [sb(f"mpart{i}", [H * TT, P], BF16) for i in range(MROWS)]
        mrem = sb("mrem", [H * TT, P], F32)
        widths = [S - P * j for j in range(TT)]
        starts = [G * sum(widths[:j]) for j in range(TT)]
        probs = sb("probs", [P, 2, G * sum(widths)], F32)
        o = sb("o", [P, 2, S], F32)

        stage = [sb(f"stage{i}", [P, SPLIT], F32) for i in range(2)]

        psA = [ps(f"psA{i}", [P, 2, S]) for i in range(2)]
        psS = [ps(f"psS{i}", [P, S]) for i in range(SB)]
        psO = ps("psO", [P, S])

        loaded = sem("loaded")
        minus_set = sem("minus_set")
        consts_pe = sem("consts_pe")
        stack_in = [[sem(f"stack_in{k}_{g}") for g in range(KVH)] for k in range(2)]
        A_ready = sem("A_ready")
        A_free = sem("A_free")
        mT_ready = sem("mT_ready")
        dve_step = sem("dve_step")
        m_ready = sem("m_ready")
        m_in = [sem(f"m_in{k}") for k in range(2)]
        S_ready = sem("S_ready")
        exp_done = sem("exp_done")
        tile_done = sem("tile_done")
        masked = sem("masked")
        O_ready = sem("O_ready")
        o_ready = sem("o_ready")
        o_out = [sem(f"o_out{i}") for i in range(2)]

        stage_in = [sem(f"stage_in{i}") for i in range(2)]
        hi_done = sem("hi_done")
        lo_done = sem("lo_done")

        EARLY = 15
        SPLIT_BATCHES = -(-(len(splits) - EARLY) // (KVH * TT // 2))

        OUT_AT = 3
        PV2_AT = 1
        PV0_AT, PV1_AT = 7, 10
        ROWS_BY = 36

        NIN = 2 * PARTS + 1

        SUNITS = [(0, r, 1) for r in range(G)] + [(1, r, 1) for r in range(G)] + [(2, 0, 2), (2, 2, 2), (3, 0, 4)]
        LAST = [3, 7, 9, 10]
        AUNITS = [(i, rp) for i in range(TT) for rp in range(G // 2)]

        block = ctx.enter_context(nc.Block())

        @block.sync
        def _(sp):
            for dst, src in ((ident[:, :], a["ident"]), (mask[:, :], a["mask"])):
                sp.dma_start(dst, src).then_inc(loaded, 16)

            def load(b, k, g):
                row = 0
                for pq in range(PARTS):
                    n = sum(p == pq for p, _ in PAIRS)
                    rows = slice(row * D, (row + n) * D)
                    sp.dma_start(qs[rows, k, g * G:(g + 1) * G, :].rearrange("p h t -> p (h t)"),
                                 scr["q"][pq, g, :, b, :].unsqueeze(0).broadcast_to([n, D, G * S])).then_inc(stack_in[k][g], 16)
                    sp.dma_start(ks[rows, k, g, :], scr["k"][0:n, g * D:(g + 1) * D, b, :]).then_inc(stack_in[k][g], 16)
                    row += n
                sp.dma_start(v[:, k, g].rearrange("p t n -> p (t n)"), scr["v"][b, g]).then_inc(stack_in[k][g], 16)

            def maxima(k):
                sp.wait_ge(m_ready, 1)
                sp.sem_inc(m_ready, -1)
                for i in range(MROWS):
                    row = SROWS + i
                    sp.dma_start(qs[row:row + 1, k].rearrange("o h (t q) -> o (h t) q", t=TT), mparts[i][:, :]
                                 ).then_inc(m_in[k], 16)

            def store(b, g):
                sp.wait_ge(o_ready, 1)
                sp.sem_inc(o_ready, -1)
                for r in range(G):
                    sp.dma_start(scr["o"][b, g * G + r], o[32 * r:32 * r + D + 1, g % 2, :]).then_inc(o_out[g % 2], 16)

            def batch(b, k, refill, has_next):
                for g in range(KVH):
                    if g == KVH - 2 and has_next:
                        maxima(1 - k)
                    store(b, g)
                    if refill:
                        load(b + 2, k, g)

            for k in range(2):
                for g in range(KVH):
                    load(k, k, g)
            maxima(0)
            with sp.Fori(0, B // 2 - 1) as it:
                for k in range(2):
                    batch(2 * it + k, k, True, True)
            batch(B - 2, 0, False, True)
            batch(B - 1, 1, False, False)
            for i in range(2):
                sp.wait_ge(o_out[i], 16 * G)

        @block.vector
        def _(dve):
            dve.wait_ge(loaded, 2 * 16)
            dve.sem_inc(loaded, -(2 * 16))
            nc.vector.tensor_copy(ident_b[:, :], ident[:, :])
            nc.vector.tensor_copy(mask_b[:, :], mask[:, :]).then_inc(consts_pe, 1)
            nc.vector.memset(ks[SROWS:P, :, :, :], -1.0).then_inc(minus_set, 1)

            def maxima(g):
                for i, rp in AUNITS:
                    buf = (i * 2 + rp) % 2
                    h = g * G + 2 * rp
                    dve.wait_ge(A_ready, 1)
                    dve.sem_inc(A_ready, -1)
                    nc.vector.tensor_reduce(mx[:, h:h + 2, i], psA[buf][:, :, 0:P * (i + 1)], AX_X,
                                            ALU.max).then_inc(A_free, 1)

            def parts():
                dve.wait_ge(mT_ready, 1)
                dve.sem_inc(mT_ready, -1)
                mT = psA[0][0:H * TT, 0, 0:P]
                nc.vector.tensor_copy(mparts[0][:, :], mT).then_inc(dve_step, 1)
                dve.wait_ge(dve_step, 1)
                dve.sem_inc(dve_step, -1)
                nc.vector.tensor_tensor(mrem[:, :], mT, mparts[0][:, :], ALU.subtract).then_inc(dve_step, 1)
                nc.vector.engine_nop().then_inc(A_free, 2)
                dve.wait_ge(dve_step, 1)
                dve.sem_inc(dve_step, -1)
                nc.vector.tensor_copy(mparts[1][:, :], mrem[:, :]).then_inc(dve_step, 1)
                dve.wait_ge(dve_step, 1)
                dve.sem_inc(dve_step, -1)
                nc.vector.tensor_tensor(mparts[2][:, :], mrem[:, :], mparts[1][:, :], ALU.subtract).then_inc(m_ready, 1)

            def batch():
                for g in range(KVH):
                    maxima(g)
                parts()

            batch()
            with dve.Fori(0, B - 1):
                batch()

        @block.gpsimd
        def _(pool):
            def causal(g, j):
                square = probs[:, g % 2, starts[j]:starts[j] + G * widths[j]].rearrange("p (r q) -> p r q", r=G)[:, :, 0:P]
                pool.wait_ge(tile_done, 1)
                pool.sem_inc(tile_done, -1)
                nc.gpsimd.affine_select(square, square, [[0, G], [1, P]], ALU.is_ge, 0.0, base=0, channel_multiplier=-1
                                        ).then_inc(masked, 1)

            weight, pieces = weight_splitter(nc, pool, stage, stage_in, hi_done, lo_done, splits)
            done = EARLY
            for i in range(EARLY):
                weight(i)
            for _b in range(SPLIT_BATCHES):
                for g in range(KVH):
                    for j in range(TT):
                        causal(g, j)
                        if j in (0, TT - 1) and done < pieces:
                            weight(done)
                            done += 1
            with pool.Fori(SPLIT_BATCHES, B):
                for g in range(KVH):
                    for j in range(TT):
                        causal(g, j)

        @block.scalar
        def _(act):
            for i in range(2):
                act.sem_inc(o_out[i], 16 * G)

            def out(g):
                act.wait_ge(O_ready, 1)
                act.sem_inc(O_ready, -1)
                act.wait_ge(o_out[g % 2], 16 * G)
                act.sem_inc(o_out[g % 2], -(16 * G))
                nc.scalar.activation(o[:, g % 2, :], psO[:, :], ACT.Copy).then_inc(o_ready, 1)

            with act.Fori(0, B):
                for g in range(KVH):
                    for s, (j, r0, n) in enumerate(SUNITS):
                        w = widths[j]
                        at = starts[j] + r0 * w
                        act.wait_ge(S_ready, 1)
                        act.sem_inc(S_ready, -1)
                        nc.scalar.activation(probs[:, g % 2, at:at + n * w], psS[(g * len(SUNITS) + s) % SB][:, 0:n * w], ACT.Exp,
                                             scale=SCALE).then_inc(exp_done, 1)
                        if s in LAST:
                            act.drain().then_inc(tile_done, 1)
                        if s == OUT_AT and g >= 1:
                            out(g - 1)
                out(KVH - 1)

        @block.tensor
        def _(pe):
            pe.wait_ge(consts_pe, 1)
            pe.sem_inc(consts_pe, -1)
            pe.sem_inc(A_free, 2)

            def score_rows(k, g, i, rp):
                buf = (i * 2 + rp) % 2
                pe.wait_ge(A_free, 1)
                pe.sem_inc(A_free, -1)
                n = P * (i + 1)
                for z in range(2):
                    h = g * G + 2 * rp + z
                    nc.tensor.matmul(psA[buf][:, z, 0:n], qs[0:SROWS, k, h, i * P:(i + 1) * P], ks[0:SROWS, k, g, 0:n],
                                     start=True, stop=False)
                    last = nc.tensor.matmul(psA[buf][:, z, n - P:n], ident_b[:, :], mask_b[:, :], start=False, stop=True)
                last.then_inc(A_ready, 1)

            def maxima():
                pe.wait_ge(A_free, 2)
                pe.sem_inc(A_free, -2)
                nc.tensor.transpose(psA[0][0:H * TT, 0, 0:P], mx[:, :, :].rearrange("p h t -> p (h t)"),
                                    ident[:, :]).then_inc(mT_ready, 1)

            def score_cols(k, g, s):
                j, r0, n = SUNITS[s]
                w = widths[j]
                bank = psS[(g * len(SUNITS) + s) % SB]
                key = ks[0:SROWS + MROWS, k, g, j * P:(j + 1) * P]
                for z in range(n):
                    h = g * G + r0 + z
                    last = nc.tensor.matmul(bank[:, z * w:(z + 1) * w], key, qs[0:SROWS + MROWS, k, h, j * P:S],
                                            start=True, stop=True)
                last.then_inc(S_ready, 1)

            def values(k, g, j):
                pe.wait_ge(masked, 1)
                pe.sem_inc(masked, -1)
                w = widths[j]
                for r in range(G):
                    at = starts[j] + r * w
                    last = nc.tensor.matmul(psO[32 * r:32 * r + 32, j * P:S], v[:, k, g, j, :],
                                            probs[:, g % 2, at:at + w], start=(j == 0), stop=(j == TT - 1))
                if j == TT - 1:
                    last.then_inc(O_ready, 1)

            def batch(k, has_next):
                used = [0]

                def exps(n):
                    if n > used[0]:
                        pe.wait_ge(exp_done, n - used[0])
                        pe.sem_inc(exp_done, -(n - used[0]))
                        used[0] = n

                pe.wait_ge(m_in[k], 16 * MROWS)
                pe.sem_inc(m_in[k], -(16 * MROWS))
                for g in range(KVH):
                    first = g * len(SUNITS)
                    for s in range(len(SUNITS)):
                        if first + s >= SB:
                            exps(first + s - SB + 1)
                        score_cols(k, g, s)
                        n = first + s
                        before, upto = (min(KVH * len(AUNITS), x * KVH * len(AUNITS) // ROWS_BY) for x in (n, n + 1))
                        ag, au = divmod(before, len(AUNITS))
                        if has_next and upto > before:
                            if au == 0:
                                pe.wait_ge(stack_in[1 - k][ag], 16 * NIN)
                                pe.sem_inc(stack_in[1 - k][ag], -(16 * NIN))
                            score_rows(1 - k, ag, *AUNITS[au])
                        if has_next and n == ROWS_BY:
                            maxima()
                        if s == PV2_AT and g >= 1:
                            for j in (2, 3):
                                exps(first - len(SUNITS) + LAST[j] + 1)
                                values(k, g - 1, j)
                        if s == PV0_AT:
                            exps(first + OUT_AT + 2)
                            values(k, g, 0)
                        if s == PV1_AT:
                            exps(first + LAST[1] + 1)
                            values(k, g, 1)
                for j in (2, 3):
                    exps(KVH * len(SUNITS) - len(SUNITS) + LAST[j] + 1)
                    values(k, KVH - 1, j)

            for g in range(KVH):
                pe.wait_ge(stack_in[0][g], 16 * NIN)
                pe.sem_inc(stack_in[0][g], -(16 * NIN))
                for i, rp in AUNITS:
                    score_rows(0, g, i, rp)
            maxima()
            pe.wait_ge(minus_set, 1)
            pe.sem_inc(minus_set, -1)
            with pe.Fori(0, B // 2 - 1):
                batch(0, True)
                batch(1, True)
            batch(0, True)
            batch(1, False)


def prepare_phase(nc, a, scr, w, cw):
    with ExitStack() as ctx:
        def sb(name, shape, dt):
            return ctx.enter_context(nc.sbuf_tensor("p3_" + name, shape, dt))

        def ps(name, shape):
            return ctx.enter_context(nc.psum_tensor("p3_" + name, shape, F32))

        def sem(name):
            return ctx.enter_context(nc.semaphore("p3_" + name))

        BT = P // CTX
        NTILE = B // BT
        WN = 2048
        ident = sb("ident", [P, P], F32)
        ones = sb("ones", [P, P], F32)
        stage = [sb(f"stage{i}", [P, WN], F32) for i in range(2)]
        abs_sum = sb("abs_sum", [P, 2], F32)
        half = sb("half", [P, 1], F32)
        vecs = sb("vecs", [w["ncols"], P], F32)
        thr = sb("thr", [P, 1], F32)
        nthr = sb("nthr", [P, 1], F32)
        sums = sb("sums", [B * H, S], F32)
        eps = sb("eps", [P, 1], F32)
        mhalf = sb("mhalf", [P, XH], F32)
        cx = sb("cx", [P, E], F32)
        stats = sb("stats", [P, 6], F32)
        mv = sb("mv", [P, 2], F32)
        var = sb("var", [P, 1], F32)
        rstd = sb("rstd", [P, 1], F32)
        cn = sb("cn", [P, E], F32)
        cnT = sb("cnT", [P, C, P], F32)
        cnh, cnl = sb("cnh", [P, C, P], F32R), sb("cnl", [P, C, P], F32R)
        k = sb("k", [P, XI], F32)
        v = sb("v", [P, XI], F32)
        k2 = sb("k2", [P, XI], F32)
        n2 = sb("n2", [P, XH], F32)
        rn = sb("rn", [P, XH], F32)
        woh, wol = sb("woh", [P, XT, E], F32R), sb("wol", [P, XT, E], F32R)
        bdh, bdl = sb("bdh", [P, XT, P], F32R), sb("bdl", [P, XT, P], F32R)
        nh = sb("nh", [P, BT, XT, E], F32R)
        nl = sb("nl", [P, BT, XT, E], F32R)

        absw = nh[:, :, :, :].bitcast(F32).rearrange("p z t n -> p z (t n)")
        tern = nl[:, 0, :, :].bitcast(F32).rearrange("p t n -> p (t n)")
        wo = nl[:, 1, :, :].bitcast(F32)

        psK = [ps(f"psK{i}", [P, S]) for i in range(2)]
        psV = [ps(f"psV{i}", [P, S]) for i in range(2)]
        psM = [ps(f"psM{i}", [P, S]) for i in range(2)]
        psN = [ps(f"psN{i}", [P, S]) for i in range(2)]

        const_in = sem("const_in")
        small_in = sem("small_in")
        cols_ready = sem("cols_ready")
        cols_done = sem("cols_done")
        stage_in = [sem(f"stage_in{i}") for i in range(2)]
        staged = sem("staged")
        sum_pe = sem("sum_pe")
        total = sem("total")
        step = sem("step")
        tern_ready = sem("tern_ready")
        ternT_ready = sem("ternT_ready")
        ternT_free = sem("ternT_free")
        wo_in = sem("wo_in")
        woh_ready = sem("woh_ready")
        wo_parts = sem("wo_parts")
        sums_in = sem("sums_in")
        rden_ready = sem("rden_ready")
        rden_out = sem("rden_out")
        cx_in = sem("cx_in")
        cx_free = sem("cx_free")
        var_ready = sem("var_ready")
        rs_ready = sem("rs_ready")
        pool_step = sem("pool_step")
        cn_ready = sem("cn_ready")
        T_ready = sem("T_ready")
        cnT_done = sem("cnT_done")
        cn_parts = sem("cn_parts")
        KV_ready = sem("KV_ready")
        k_ready = sem("k_ready")
        kn_ready = sem("kn_ready")
        M_ready = sem("M_ready")
        bdh_ready = sem("bdh_ready")
        bd_ready = sem("bd_ready")
        N_ready = sem("N_ready")
        nh_ready = sem("nh_ready")
        nl_ready = sem("nl_ready")
        n_ready = sem("n_ready")
        n_out = sem("n_out")

        terns = [(a["L0_ffn_W1"].rearrange("(c p) n -> p c n", p=P), FT, E),
                 (a["L0_ffn_W2"].rearrange("(c p) n -> p c n", p=P), C, FT * P)]

        block = ctx.enter_context(nc.Block())

        @block.sync
        def _(sp):
            tiles = a["ctx_1024"].rearrange("(t b) s f -> t (b s) f", b=BT)

            def load(t):
                sp.dma_start(cx[:, :], tiles[t]).then_inc(cx_in, 16)

            def store(t):
                for z in range(BT):
                    sp.wait_ge(n_ready, 1)
                    sp.sem_inc(n_ready, -1)
                    for part, src in enumerate((nh, nl)):
                        sp.dma_start(scr["n"][BT * t + z, part], src[:, z].rearrange("p t n -> p (t n)").bitcast(F32)).then_inc(n_out, 16)

            load(0)
            sp.dma_start(ident[:, :], a["ident"]).then_inc(const_in, 16)
            for name, at, n in w["vectors"]:
                sp.dma_start(vecs[at:at + n, :], a[name].rearrange("(c p) -> c p", p=P)).then_inc(small_in, 16)
            sp.wait_ge(cx_free, 1)
            sp.sem_inc(cx_free, -1)
            load(1)
            for i, (src, cc, _) in enumerate(terns):
                sp.dma_start(stage[i][:, :].rearrange("p (c n) -> p c n", c=cc), src).then_inc(stage_in[i], 16)
            sp.dma_start(sums[:, :], scr["o"][:, :, D, :].rearrange("b h t -> (b h) t")).then_inc(sums_in, 16)
            sp.dma_start(wo, a["L0_xattn_wo"].rearrange("(c p) n -> p c n", p=P)).then_inc(wo_in, 16)
            sp.wait_ge(cx_free, 1)
            sp.sem_inc(cx_free, -1)
            load(2)
            sp.wait_ge(rden_ready, 1)
            sp.sem_inc(rden_ready, -1)
            sp.dma_start(scr["rden"].rearrange("b h t -> (b h) t"), sums[:, :]).then_inc(rden_out, 16)
            store(0)
            sp.wait_ge(cx_free, 1)
            sp.sem_inc(cx_free, -1)
            load(3)
            for t in range(1, NTILE):
                store(t)
            sp.wait_ge(cx_free, 1)
            sp.sem_inc(cx_free, -1)
            sp.wait_ge(rden_out, 16)
            sp.sem_inc(rden_out, -16)
            sp.wait_ge(n_out, 16 * 2 * BT)

        @block.gpsimd
        def _(pool):
            def of_rows():
                pool.wait_ge(var_ready, 1)
                pool.sem_inc(var_ready, -1)
                nc.gpsimd.tensor_tensor(var[:, :], mv[:, 1:2], eps[:, :], ALU.add).then_inc(pool_step, 1)
                pool.wait_ge(pool_step, 1)
                pool.sem_inc(pool_step, -1)
                nc.gpsimd.tensor_tensor(rstd[:, :], var[:, :], mhalf[:, 0:1], ALU.pow).then_inc(rs_ready, 1)

            def of_heads():
                pool.wait_ge(var_ready, 1)
                pool.sem_inc(var_ready, -1)
                nc.gpsimd.tensor_tensor(rn[:, :], n2[:, :], mhalf[:, :], ALU.pow).then_inc(rs_ready, 1)

            of_rows()
            of_rows()
            of_heads()
            with pool.Fori(0, NTILE - 2):
                of_rows()
                of_heads()
            of_heads()

        @block.scalar
        def _(act):
            def affine():
                act.wait_ge(T_ready, 1)
                act.sem_inc(T_ready, -1)
                for c in range(C):
                    last = nc.scalar.activation(cnT[:, c, :], psM[0][:, c * P:(c + 1) * P], ACT.Identity,
                                                bias=w["ln1_b"][:, c:c + 1], scale=w["ln1_g"][:, c:c + 1])
                last.then_inc(cnT_done, 1)

            def keys():
                act.wait_ge(KV_ready, 1)
                act.sem_inc(KV_ready, -1)
                for dst, bank in ((k, psK), (v, psV)):
                    for i in range(2):
                        last = nc.scalar.activation(dst[:, i * S:(i + 1) * S], bank[i][:, :], ACT.Copy)
                last.then_inc(k_ready, 1)

            def tile(ahead, follows):
                for z in range(BT):
                    for i in range(2):
                        act.wait_ge(M_ready, 1)
                        act.sem_inc(M_ready, -1)
                        m = psM[i][:, :].rearrange("p (t n) -> p t n", t=4)
                        for side in range(2):
                            r = slice(side * XD, (side + 1) * XD)
                            last = nc.scalar.activation(bdh[r, 4 * i:4 * i + 4, r], m[r, :, r], ACT.Copy)
                        last.then_inc(bdh_ready, 1)
                    if z == 1 and follows:
                        keys()
                    if z == 1 and ahead:
                        affine()
                    if z == 0:
                        act.wait_ge(n_out, 16 * 2 * BT)
                        act.sem_inc(n_out, -(16 * 2 * BT))
                    for i in range(XT // 2):
                        act.wait_ge(N_ready, 1)
                        act.sem_inc(N_ready, -1)
                        nc.scalar.activation(nh[:, z, 2 * i:2 * i + 2, :].rearrange("p t n -> p (t n)"), psN[i % 2][:, :],
                                             ACT.Copy).then_inc(nh_ready, 1)

            act.wait_ge(cols_ready, 1)
            act.sem_inc(cols_ready, -1)
            nc.scalar.activation(w["all_columns"][:, :], psN[1][:, 0:w["ncols"]], ACT.Copy).then_inc(cols_done, 1)
            act.wait_ge(cols_done, 1)
            act.sem_inc(cols_done, -1)
            affine()
            keys()
            affine()
            for i in range(2):
                act.wait_ge(stage_in[i], 16)
                act.sem_inc(stage_in[i], -16)
                nc.scalar.activation(absw[:, i, :], stage[i][:, :], ACT.Abs, accum_out=abs_sum[:, i:i + 1]).then_inc(staged, 1)
            act.wait_ge(wo_in, 16)
            act.sem_inc(wo_in, -16)
            nc.scalar.activation(woh[:, :, :], wo, ACT.Copy).then_inc(woh_ready, 1)
            act.sem_inc(n_out, 16 * 2 * BT)
            with act.Fori(0, NTILE - 2):
                tile(True, True)
            tile(False, True)
            tile(False, False)

        @block.vector
        def _(dve):
            def rows():
                dve.wait_ge(cx_in, 16)
                dve.sem_inc(cx_in, -16)
                nc.vector.bn_stats(stats[:, :], cx[:, :]).then_inc(step, 1)
                dve.wait_ge(step, 1)
                dve.sem_inc(step, -1)
                nc.vector.bn_aggr(mv[:, :], stats[:, :]).then_inc(var_ready, 1)
                dve.wait_ge(rs_ready, 1)
                dve.sem_inc(rs_ready, -1)
                nc.vector.tensor_scalar(cn[:, :], cx[:, :], mv[:, 0:1], rstd[:, 0:1], ALU.subtract, ALU.mult).then_inc(cn_ready, 1)
                nc.vector.engine_nop().then_inc(cx_free, 1)

            def row_parts():
                dve.wait_ge(cnT_done, 1)
                dve.sem_inc(cnT_done, -1)
                nc.vector.tensor_copy(cnh[:, :, :], cnT[:, :, :]).then_inc(step, 1)
                dve.wait_ge(step, 1)
                dve.sem_inc(step, -1)
                nc.vector.tensor_tensor(cnl[:, :, :], cnT[:, :, :], cnh[:, :, :].bitcast(F32), ALU.subtract).then_inc(cn_parts, 1)

            def normalise_keys():
                dve.wait_ge(k_ready, 1)
                dve.sem_inc(k_ready, -1)
                nc.vector.tensor_tensor(k2[:, :], k[:, :], k[:, :], ALU.mult).then_inc(step, 1)
                dve.wait_ge(step, 1)
                dve.sem_inc(step, -1)
                nc.vector.tensor_reduce(n2[:, :], k2[:, :].rearrange("p (h d) -> p h d", h=XH), AX_X, ALU.add).then_inc(step, 1)
                dve.wait_ge(step, 1)
                dve.sem_inc(step, -1)
                nc.vector.tensor_scalar(n2[:, :], n2[:, :], 1e-24, None, ALU.max).then_inc(var_ready, 1)
                dve.wait_ge(rs_ready, 1)
                dve.sem_inc(rs_ready, -1)
                nc.vector.tensor_tensor(k[:, :].rearrange("p (h d) -> p h d", h=XH), k[:, :].rearrange("p (h d) -> p h d", h=XH),
                                        rn[:, :].unsqueeze(2).broadcast_to([P, XH, XD]), ALU.mult).then_inc(kn_ready, 1)

            def ternary(i, cc, nn):
                dve.wait_ge(staged, 1)
                dve.sem_inc(staged, -1)
                nc.vector.engine_nop().then_inc(sum_pe, 1)
                dve.wait_ge(total, 1)
                dve.sem_inc(total, -1)
                nc.vector.tensor_scalar(thr[:, :], psN[0][:, 0:1], 1.0 / (cc * nn * P), 1e-8, ALU.mult, ALU.max).then_inc(step, 1)
                dve.wait_ge(step, 1)
                dve.sem_inc(step, -1)
                nc.vector.tensor_scalar(nthr[:, :], thr[:, :], -0.5, None, ALU.mult)
                nc.vector.tensor_scalar(half[:, :], thr[:, :], 0.5, None, ALU.mult).then_inc(step, 1)
                dve.wait_ge(step, 1)
                dve.sem_inc(step, -1)
                wst = stage[i]
                nc.vector.tensor_scalar(tern[:, :], wst[:, :], nthr[:, 0:1], None, ALU.is_lt).then_inc(step, 1)
                dve.wait_ge(step, 1)
                dve.sem_inc(step, -1)
                nc.vector.scalar_tensor_tensor(out=tern[:, :], in0=wst[:, :], scalar=half[:, 0:1], in1=tern[:, :],
                                               op0=ALU.is_gt, op1=ALU.subtract).then_inc(tern_ready, 1)
                for q in range(4):
                    dve.wait_ge(ternT_ready, 1)
                    dve.sem_inc(ternT_ready, -1)
                    src = psM[q % 2] if q < 2 else psN[q % 2]
                    if i == 0:
                        dst = w["t1"][:, :, 2 * q * P:(2 * q + 2) * P]
                        s = src[:, :].rearrange("p (c n) -> p c n", c=C)
                    else:
                        dst = w["t2"][:, 2 * q:2 * q + 2, :]
                        s = src[:, :].rearrange("p (t n) -> p t n", t=2)
                    last = nc.vector.tensor_copy(dst, s)
                last.then_inc(ternT_free, 1)

            def tile(ahead, follows):
                for z in range(BT):
                    for i in range(2):
                        dve.wait_ge(bdh_ready, 1)
                        dve.sem_inc(bdh_ready, -1)
                        m = psM[i][:, :].rearrange("p (t n) -> p t n", t=4)
                        for side in range(2):
                            r = slice(side * XD, (side + 1) * XD)
                            last = nc.vector.tensor_tensor(bdl[r, 4 * i:4 * i + 4, r], m[r, :, r],
                                                           bdh[r, 4 * i:4 * i + 4, r].bitcast(F32), ALU.subtract)
                        last.then_inc(bd_ready, 1)
                    if z == 0 and ahead:
                        rows()
                    for i in range(XT // 2):
                        dve.wait_ge(nh_ready, 1)
                        dve.sem_inc(nh_ready, -1)
                        high = nh[:, z, 2 * i:2 * i + 2, :].rearrange("p t n -> p (t n)").bitcast(F32)
                        nc.vector.tensor_tensor(nl[:, z, 2 * i:2 * i + 2, :].rearrange("p t n -> p (t n)"), psN[i % 2][:, :],
                                                high, ALU.subtract).then_inc(nl_ready, 1)
                    nc.vector.engine_nop().then_inc(n_ready, 1)
                if ahead:
                    row_parts()
                if follows:
                    normalise_keys()

            nc.vector.memset(ones[:, :], 1.0)
            nc.vector.memset(eps[:, :], EPS)
            nc.vector.memset(mhalf[:, :], -0.5)
            nc.vector.memset(bdh[:, :, :].bitcast(F32), 0.0)
            nc.vector.memset(bdl[:, :, :].bitcast(F32), 0.0)
            rows()
            row_parts()
            rows()
            normalise_keys()
            row_parts()
            dve.wait_ge(sums_in, 16)
            dve.sem_inc(sums_in, -16)
            nc.vector.reciprocal(sums[:, :], sums[:, :]).then_inc(rden_ready, 1)
            for i, (_, cc, nn) in enumerate(terns):
                ternary(i, cc, nn)
            dve.wait_ge(woh_ready, 1)
            dve.sem_inc(woh_ready, -1)
            nc.vector.tensor_tensor(wol[:, :, :], wo, woh[:, :, :].bitcast(F32), ALU.subtract).then_inc(wo_parts, 1)
            with dve.Fori(0, NTILE - 2):
                tile(True, True)
            tile(False, True)
            tile(False, False)

        @block.tensor
        def _(pe):
            def transpose_rows():
                pe.wait_ge(cn_ready, 1)
                pe.sem_inc(cn_ready, -1)
                for c in range(C):
                    last = nc.tensor.transpose(psM[0][:, c * P:(c + 1) * P], cn[:, c * P:(c + 1) * P], ident[:, :])
                last.then_inc(T_ready, 1)

            def project_rows():
                pe.wait_ge(cn_parts, 1)
                pe.sem_inc(cn_parts, -1)
                for bank, (whi, wlo) in ((psK, cw["wk"]), (psV, cw["wv"])):
                    for i in range(2):
                        cols = slice(i * S, (i + 1) * S)
                        for c in range(C):
                            nc.tensor.matmul(bank[i][:, :], cnh[:, c, :], whi[:, c, cols], start=(c == 0), stop=False)
                            nc.tensor.matmul(bank[i][:, :], cnh[:, c, :], wlo[:, c, cols], start=False, stop=False)
                            last = nc.tensor.matmul(bank[i][:, :], cnl[:, c, :], whi[:, c, cols], start=False, stop=(c == C - 1))
                last.then_inc(KV_ready, 1)

            def ternary(i, cc):
                pe.wait_ge(sum_pe, 1)
                pe.sem_inc(sum_pe, -1)
                nc.tensor.matmul(psN[0][:, 0:1], ones[:, :], abs_sum[:, i:i + 1], start=True, stop=True).then_inc(total, 1)
                pe.wait_ge(tern_ready, 1)
                pe.sem_inc(tern_ready, -1)
                t = tern[:, :].rearrange("p (c n) -> p c n", c=cc)
                for q in range(4):
                    dst = psM[q % 2] if q < 2 else psN[q % 2]
                    for y in range(2):
                        for c in range(C):
                            if i == 0:
                                out, src = dst[:, (c * 2 + y) * P:(c * 2 + y + 1) * P], t[:, 2 * q + y, c * P:(c + 1) * P]
                            else:
                                out, src = dst[:, (y * 2 + c) * P:(y * 2 + c + 1) * P], t[:, c, (2 * q + y) * P:(2 * q + y + 1) * P]
                            last = nc.tensor.transpose(out, src, ident[:, :])
                    last.then_inc(ternT_ready, 1)
                pe.wait_ge(ternT_free, 1)
                pe.sem_inc(ternT_free, -1)

            def tile(ahead):
                pe.wait_ge(kn_ready, 1)
                pe.sem_inc(kn_ready, -1)
                for z in range(BT):
                    rows = slice(z * CTX, (z + 1) * CTX)
                    for t in range(XT):
                        cols = slice(t * P, (t + 1) * P)
                        last = nc.tensor.matmul(psM[t // 4][:, (t % 4) * P:(t % 4 + 1) * P], v[rows, cols], k[rows, cols],
                                                start=True, stop=True)
                        if t % 4 == 3:
                            last.then_inc(M_ready, 1)
                    pe.wait_ge(bd_ready, 1)
                    pe.sem_inc(bd_ready, -1)
                    if z == 1 and ahead:
                        transpose_rows()
                    for i in range(XT // 2):
                        if i >= 2:
                            pe.wait_ge(nl_ready, 1)
                            pe.sem_inc(nl_ready, -1)
                        if i == 2:
                            pe.wait_ge(bd_ready, 1)
                            pe.sem_inc(bd_ready, -1)
                        for y in range(2):
                            t = 2 * i + y
                            bank = psN[i % 2][:, y * E:(y + 1) * E]
                            nc.tensor.matmul(bank, bdh[:, t, :], woh[:, t, :], start=True, stop=False)
                            nc.tensor.matmul(bank, bdh[:, t, :], wol[:, t, :], start=False, stop=False)
                            last = nc.tensor.matmul(bank, bdl[:, t, :], woh[:, t, :], start=False, stop=True)
                        last.then_inc(N_ready, 1)
                    pe.wait_ge(nl_ready, 2)
                    pe.sem_inc(nl_ready, -2)
                if ahead:
                    project_rows()

            pe.wait_ge(const_in, 16)
            pe.sem_inc(const_in, -16)
            pe.wait_ge(small_in, 16 * len(w["vectors"]))
            pe.sem_inc(small_in, -(16 * len(w["vectors"])))
            nc.tensor.transpose(psN[1][:, 0:w["ncols"]], vecs[0:w["ncols"], :], ident[0:w["ncols"], 0:w["ncols"]]).then_inc(cols_ready, 1)
            transpose_rows()
            project_rows()
            transpose_rows()
            project_rows()
            for i, (_, cc, _) in enumerate(terns):
                ternary(i, cc)
            pe.wait_ge(wo_parts, 1)
            pe.sem_inc(wo_parts, -1)
            with pe.Fori(0, NTILE - 2):
                tile(True)
            tile(False)
            tile(False)


def mix_phase(nc, a, scr, w, out):
    with ExitStack() as ctx:
        def sb(name, shape, dt):
            return ctx.enter_context(nc.sbuf_tensor("p4_" + name, shape, dt))

        def ps(name, shape):
            return ctx.enter_context(nc.psum_tensor("p4_" + name, shape, F32))

        def sem(name):
            return ctx.enter_context(nc.semaphore("p4_" + name))

        RING = 3
        ident = sb("ident", [P, P], F32)
        eps = sb("eps", [P, TT], F32)
        mhalf = sb("mhalf", [P, TT], F32)
        o = sb("o", [P, C, S], F32)
        rden = sb("rden", [P, C, S], F32)
        xin = sb("xin", [P, TT, E], F32)
        x1 = sb("x1", [P, TT, E], F32)
        q0 = sb("q0", [P, TT, E], F32)
        z = sb("z", [P, TT, E], F32)
        base = sb("base", [P, TT, E], F32)
        x2 = sb("x2", [P, TT, E], F32)
        stats = sb("stats", [P, TT, 6], F32)
        mv = sb("mv", [P, TT, 2], F32)
        var = sb("var", [P, TT], F32)
        rstd = sb("rstd", [P, TT], F32)
        feat_f = sb("feat_f", [P, C, S], F32)
        feat_b = sb("feat_b", [P, C, S], F32)
        fh, fl = sb("fh", [P, C, S], F32R), sb("fl", [P, C, S], F32R)
        bh, bl = sb("bh", [P, C, S], F32R), sb("bl", [P, C, S], F32R)
        q = sb("q", [P, XT, S], F32)
        sq = sb("sq", [P, RING, S], F32)
        sh, sl = sb("sh", [P, RING, S], F32R), sb("sl", [P, RING, S], F32R)
        h = sb("h", [P, RING, S], F32)
        hh, hl = sb("hh", [P, RING, S], F32R), sb("hl", [P, RING, S], F32R)
        nw = [sb(f"n{i}", [P, XT, E], F32R) for i in range(2)]

        n2 = sb("n2", [P, P], F32)
        rh, rl = sb("rh", [P, P], F32R), sb("rl", [P, P], F32R)
        rstack = sb("rstack", [P, 2, S], F32R)
        idle = sb("idle", [P, 1], F32)

        psG = [ps(f"psG{i}", [P, S]) for i in range(RING)]
        psY = [ps(f"psY{i}", [P, S]) for i in range(C)]
        psT = [ps(f"psT{i}", [P, S]) for i in range(C)]
        psN = ps("psN", [P, S])

        oh, ol = hh[:, 0:C, :], hl[:, 0:C, :]

        const_in = sem("const_in")
        consts = sem("consts")
        act_go = sem("act_go")
        fetched = sem("fetched")
        o_in = sem("o_in")
        x_in = sem("x_in")
        ox_free = sem("ox_free")
        n_in = sem("n_in")
        n_free = sem("n_free")
        out_ready = sem("out_ready")
        out_done = sem("out_done")
        o_parts = sem("o_parts")
        step = sem("step")
        pool_step = sem("pool_step")
        var_ready = sem("var_ready")
        rs_ready = sem("rs_ready")
        z_ready = sem("z_ready")
        Y_ready = sem("Y_ready")
        feat_ready = sem("feat_ready")
        T_ready = sem("T_ready")
        u_ready = sem("u_ready")
        u_parts = sem("u_parts")
        tok_ready = sem("tok_ready")
        tok_free = sem("tok_free")
        q_ready = sem("q_ready")
        sq_ready = sem("sq_ready")
        sq_parts = sem("sq_parts")
        n2_ready = sem("n2_ready")
        norm_ready = sem("norm_ready")
        rn_ready = sem("rn_ready")
        g_ready = sem("g_ready")
        h_ready = sem("h_ready")
        h_parts = sem("h_parts")
        s_ready = sem("s_ready")
        qn_ready = sem("qn_ready")
        qh_ready = sem("qh_ready")
        qn_parts = sem("qn_parts")

        Z1_AT = 6
        W2_BACK = 1
        Z3_AT = 6
        HALF = XT // 2
        NORMS_AT = (HALF + RING - 2, 1)
        X2_AT, X1_AT = 1, 4
        O_BACK = 2
        CROSS_AT = (2, 3, 3, 6)
        X2_SUM, X2_NORM, BASE_AT = 1, 3, 7
        F_AT = (0, 2, 4)
        O_AT = 3
        Y_BACK = 1
        Z2_AT = 8
        Q_AT, S_AT, T_AT = FT, FT + XT, FT + 2 * XT

        out_ap = out

        block = ctx.enter_context(nc.Block())

        @block.sync
        def _(sp):
            def load_o(b):
                for c in range(C):
                    heads = slice(c * H // C, (c + 1) * H // C)
                    sp.dma_start(o[:, c, :], scr["o"][b, heads, 0:D, :]).then_inc(o_in, 16)
                    sp.dma_start(rden[:, c, :], scr["rden"][b, heads, :].unsqueeze(1).broadcast_to([H // C, D, S])
                                 ).then_inc(o_in, 16)

            def load_x(b):
                sp.dma_start(xin[:, :, :], a["x"][b].rearrange("(t p) f -> p t f", p=P)).then_inc(x_in, 16)

            def load_n(b):
                for i in range(2):
                    sp.dma_start(nw[i][:, :, :].rearrange("p t n -> p (t n)").bitcast(F32), scr["n"][b, i]).then_inc(n_in, 16)

            def store(b):
                sp.wait_ge(out_ready, 1)
                sp.sem_inc(out_ready, -1)
                sp.dma_start(out_ap[b].rearrange("(t p) f -> p t f", p=P), x2[:, :, :]).then_inc(out_done, 16)

            def round_(b, old, more_o, more_n):
                if old:
                    store(b - 2)
                if more_o:
                    sp.wait_ge(ox_free, 1)
                    sp.sem_inc(ox_free, -1)
                    load_o(b + 2)
                    load_x(b + 2)
                if more_n:
                    sp.wait_ge(n_free, 1)
                    sp.sem_inc(n_free, -1)
                    load_n(b + 1)

            sp.dma_start(ident[:, :], a["ident"]).then_inc(const_in, 16)
            load_o(0)
            load_x(0)
            load_n(0)
            sp.wait_ge(ox_free, 1)
            sp.sem_inc(ox_free, -1)
            load_o(1)
            load_x(1)
            round_(0, False, True, True)
            round_(1, False, True, True)
            with sp.Fori(2, B - 2) as b:
                round_(b, True, True, True)
            round_(B - 2, True, False, True)
            round_(B - 1, True, False, False)
            store(B - 2)
            store(B - 1)
            sp.wait_ge(out_done, 16)

        @block.gpsimd
        def _(pool):
            def rsqrt():
                pool.wait_ge(var_ready, 1)
                pool.sem_inc(var_ready, -1)
                nc.gpsimd.tensor_tensor(var[:, :], mv[:, :, 1], eps[:, :], ALU.add).then_inc(pool_step, 1)
                pool.wait_ge(pool_step, 1)
                pool.sem_inc(pool_step, -1)
                nc.gpsimd.tensor_tensor(rstd[:, :], var[:, :], mhalf[:, :], ALU.pow).then_inc(rs_ready, 1)

            def low(m):
                s = m % RING
                pool.wait_ge(sq_ready, 1)
                pool.sem_inc(sq_ready, -1)
                nc.gpsimd.tensor_tensor(sl[:, s, :], sq[:, s, :], sh[:, s, :].bitcast(F32), ALU.subtract).then_inc(sq_parts, 1)

            def round_(back, front):
                if front:
                    rsqrt()
                    rsqrt()
                for m in range(XT):
                    if front:
                        low(m)
                    if back and m == X2_AT:
                        rsqrt()
                if front:
                    rsqrt()

            round_(False, True)
            with pool.Fori(1, B):
                round_(True, True)
            round_(True, False)

        @block.scalar
        def _(act):
            def evacuate(dst, bias):
                for c in range(C):
                    act.wait_ge(Y_ready, 1)
                    act.sem_inc(Y_ready, -1)
                    nc.scalar.activation(dst[:, c, :], psY[c][:, :], ACT.Identity, bias=bias[:, c:c + 1]).then_inc(feat_ready, 1)

            def affine(dst, g, b):
                act.wait_ge(T_ready, 1)
                act.sem_inc(T_ready, -1)
                for c in range(C):
                    nc.scalar.activation(dst[:, c, :], psT[c][:, :], ACT.Identity, bias=b[:, c:c + 1],
                                         scale=g[:, c:c + 1]).then_inc(u_ready, 1)

            def gelu(bias, m, bank):
                act.wait_ge(g_ready, 1)
                act.sem_inc(g_ready, -1)
                nc.scalar.activation(h[:, m % RING, :], psG[bank][:, :], ACT.Gelu, bias=bias[:, m:m + 1])
                nc.scalar.activation(hh[:, m % RING, :], psG[bank][:, :], ACT.Gelu, bias=bias[:, m:m + 1]).then_inc(h_ready, 1)

            def preload(func):
                nc.scalar.activation(idle[:, :], eps[:, 0:1], func).then_inc(fetched, 1)
                act.wait_ge(fetched, 1)
                act.sem_inc(fetched, -1)

            def norms(half):
                act.wait_ge(n2_ready, 1)
                act.sem_inc(n2_ready, -1)
                for t in range(TT):
                    rows = slice(32 * t, 32 * (t + 1))
                    last = nc.scalar.activation(n2[rows, :], (psY[0], psN)[half][rows, t * P:(t + 1) * P], ACT.Sqrt)
                last.then_inc(norm_ready, 1)

            def round_(old, back, front, more):
                if old:
                    evacuate(feat_f, w["fb2"])
                if back:
                    for m in range(FT):
                        gelu(w["b1"], m, m % RING)
                        if front and m == Z1_AT:
                            affine(feat_f, w["ln1_g"], w["ln1_b"])
                    evacuate(feat_b, w["b2"])
                elif front:
                    affine(feat_f, w["ln1_g"], w["ln1_b"])
                for m in range(XT):
                    if front:
                        bank = (Q_AT + m) % RING
                        act.wait_ge(q_ready, 1)
                        act.sem_inc(q_ready, -1)
                        nc.scalar.activation(q[:, m, :], psG[bank][:, :], ACT.Copy)
                        nc.scalar.activation(sq[:, m % RING, :], psG[bank][:, :], ACT.Square)
                        nc.scalar.activation(sh[:, m % RING, :], psG[bank][:, :], ACT.Square).then_inc(sq_ready, 1)
                        if m == NORMS_AT[0] - 1:
                            preload(ACT.Sqrt)
                        if m == NORMS_AT[0]:
                            norms(0)
                    if back and m == Z3_AT:
                        act.wait_ge(T_ready, 1)
                        act.sem_inc(T_ready, -1)
                        for c in range(C):
                            nc.scalar.activation(bh[:, c, :], psT[c][:, :], ACT.Copy).then_inc(u_ready, 1)
                if front:
                    if more:
                        evacuate(feat_f, w["bout"])
                    norms(1)
                    for m in range(XT):
                        act.wait_ge(qn_ready, 1)
                        act.sem_inc(qn_ready, -1)
                        nc.scalar.activation(sh[:, m % RING, :], sq[:, m % RING, :], ACT.Copy).then_inc(qh_ready, 1)
                    preload(ACT.Gelu)
                    evacuate(feat_f, w["bo"])
                if back:
                    for m in range(FT):
                        gelu(w["fb1"], m, (T_AT + m) % RING)
                if front:
                    affine(feat_b, w["ln2_g"], w["ln2_b"])

            act.wait_ge(act_go, 1)
            act.sem_inc(act_go, -1)
            preload(ACT.Gelu)
            evacuate(feat_f, w["bout"])
            round_(False, False, True, True)
            round_(False, True, True, True)
            with act.Fori(2, B - 1):
                round_(True, True, True, True)
            round_(True, True, True, False)
            round_(True, True, False, False)
            evacuate(feat_f, w["fb2"])

        @block.vector
        def _(dve):
            flat = "p c n -> p (c n)"

            def prepare_o():
                dve.wait_ge(o_in, 16 * 2 * C)
                dve.sem_inc(o_in, -(16 * 2 * C))
                nc.vector.tensor_tensor(o[:, :, :], o[:, :, :], rden[:, :, :], ALU.mult).then_inc(step, 1)
                dve.wait_ge(step, 1)
                dve.sem_inc(step, -1)
                nc.vector.tensor_copy(oh, o[:, :, :]).then_inc(step, 1)
                dve.wait_ge(step, 1)
                dve.sem_inc(step, -1)
                nc.vector.tensor_tensor(ol, o[:, :, :], oh.bitcast(F32), ALU.subtract).then_inc(o_parts, 1)

            def variance(src):
                for t in range(TT):
                    last = nc.vector.bn_stats(stats[:, t], src[:, t, :])
                last.then_inc(step, 1)
                dve.wait_ge(step, 1)
                dve.sem_inc(step, -1)
                for t in range(TT):
                    last = nc.vector.bn_aggr(mv[:, t, :], stats[:, t])
                last.then_inc(var_ready, 1)

            def normalise(dst, src, sem_):
                dve.wait_ge(rs_ready, 1)
                dve.sem_inc(rs_ready, -1)
                for t in range(TT):
                    last = nc.vector.tensor_scalar(dst[:, t, :], src[:, t, :], mv[:, t, 0:1], rstd[:, t:t + 1],
                                                   ALU.subtract, ALU.mult)
                last.then_inc(sem_, 1)

            def parts(hi, lo, src):
                for c in range(C):
                    dve.wait_ge(u_ready, 1)
                    dve.sem_inc(u_ready, -1)
                    nc.vector.tensor_copy(hi[:, c, :], src[:, c, :]).then_inc(step, 1)
                    dve.wait_ge(step, 1)
                    dve.sem_inc(step, -1)
                    nc.vector.tensor_tensor(lo[:, c, :], src[:, c, :], hi[:, c, :].bitcast(F32), ALU.subtract).then_inc(u_parts, 1)

            def add_back(dst, src, sem_):
                dve.wait_ge(tok_ready, 1)
                dve.sem_inc(tok_ready, -1)
                for i in range(2):
                    last = nc.vector.tensor_tensor(dst[:, 2 * i:2 * i + 2, :].rearrange("p t n -> p (t n)"), psT[i][:, :],
                                                   src[:, 2 * i:2 * i + 2, :].rearrange("p t n -> p (t n)"), ALU.add)
                last.then_inc(sem_, 1)
                nc.vector.engine_nop().then_inc(tok_free, 1)

            def hidden(m):
                s = m % RING
                dve.wait_ge(h_ready, 1)
                dve.sem_inc(h_ready, -1)
                nc.vector.tensor_tensor(hl[:, s, :], h[:, s, :], hh[:, s, :].bitcast(F32), ALU.subtract).then_inc(h_parts, 1)

            def inverse_norms(half):
                dve.wait_ge(norm_ready, 1)
                dve.sem_inc(norm_ready, -1)
                nc.vector.tensor_scalar(n2[:, :], n2[:, :], 1e-12, None, ALU.max).then_inc(step, 1)
                dve.wait_ge(step, 1)
                dve.sem_inc(step, -1)
                nc.vector.reciprocal(n2[:, :], n2[:, :]).then_inc(step, 1)
                dve.wait_ge(step, 1)
                dve.sem_inc(step, -1)
                nc.vector.tensor_copy(rh[:, :], n2[:, :]).then_inc(step, 1)
                dve.wait_ge(step, 1)
                dve.sem_inc(step, -1)
                nc.vector.tensor_tensor(rl[:, :], n2[:, :], rh[:, :].bitcast(F32), ALU.subtract).then_inc(step, 1)
                dve.wait_ge(step, 1)
                dve.sem_inc(step, -1)
                for row, src in ((0, rh), (32, rl)):
                    for t in range(TT):
                        last = nc.vector.tensor_copy(rstack[row:row + XH, half, t * P:(t + 1) * P],
                                                     src[32 * t:32 * t + XH, :].bitcast(F32))
                last.then_inc(rn_ready, 1)

            def add_x1():
                dve.wait_ge(x_in, 16)
                dve.sem_inc(x_in, -16)
                add_back(x1, xin, step)
                dve.wait_ge(step, 1)
                dve.sem_inc(step, -1)
                nc.vector.engine_nop().then_inc(ox_free, 1)

            def norm_x1():
                normalise(q0, x1, step)
                dve.wait_ge(step, 1)
                dve.sem_inc(step, -1)
                variance(q0)

            def add_mlp(old):
                if old:
                    dve.wait_ge(out_done, 16)
                    dve.sem_inc(out_done, -16)
                add_back(x2, base, step)
                dve.wait_ge(step, 1)
                dve.sem_inc(step, -1)
                variance(x2)

            def low_z3():
                for c in range(C):
                    dve.wait_ge(u_ready, 1)
                    dve.sem_inc(u_ready, -1)
                    nc.vector.tensor_tensor(bl[:, c, :], psT[c][:, :], bh[:, c, :].bitcast(F32), ALU.subtract).then_inc(u_parts, 1)

            def add_cross(dst, signal):
                for i in range(2):
                    d = dst[:, 2 * i:2 * i + 2, :].rearrange("p t n -> p (t n)")
                    last = nc.vector.tensor_tensor(d, psT[i][:, :], d, ALU.add)
                last.then_inc(signal, 1)

            def cross_q0():
                dve.wait_ge(tok_ready, 1)
                dve.sem_inc(tok_ready, -1)
                add_cross(q0, step)
                nc.vector.engine_nop().then_inc(n_free, 1)

            def variance_q0():
                dve.wait_ge(step, 1)
                dve.sem_inc(step, -1)
                variance(q0)

            def spread(m):
                if m < XT:
                    dve.wait_ge(s_ready, 1)
                    dve.sem_inc(s_ready, -1)
                    nc.vector.tensor_tensor(sq[:, m % RING, :], psG[(S_AT + m) % RING][:, :], q[:, m, :], ALU.mult).then_inc(qn_ready, 1)
                if m >= 1:
                    s = (m - 1) % RING
                    dve.wait_ge(qh_ready, 1)
                    dve.sem_inc(qh_ready, -1)
                    nc.vector.tensor_tensor(sl[:, s, :], sq[:, s, :], sh[:, s, :].bitcast(F32), ALU.subtract).then_inc(qn_parts, 1)

            def none(m):
                pass

            def beside(first, end, tile, extras):
                for m in range(first, end):
                    tile(m)
                    for f in extras.get(m, ()):
                        f()

            def round_(old, back, front, more):
                if back:
                    parts(bh, bl, feat_b)
                extras = {m: [] for m in range(-1, FT + 1)}
                if old:
                    extras[1].append(lambda: add_back(x2, x2, out_ready))
                if front:
                    extras[F_AT[0]].append(lambda: variance(x1))
                    extras[F_AT[1]].append(norm_x1)
                    extras[F_AT[2]].append(lambda: normalise(z, q0, z_ready))
                    extras[Z1_AT].append(lambda: parts(fh, fl, feat_f))
                beside(0, FT, hidden if back else none, extras)
                extras = {m: [] for m in range(-1, FT + 1)}
                if back:
                    extras[X2_SUM].append(lambda: add_mlp(old))
                    extras[X2_NORM].append(lambda: normalise(z, x2, z_ready))
                if front:
                    extras[BASE_AT].append(lambda: nc.vector.tensor_tensor(base[:, :, :], x1[:, :, :], q0[:, :, :], ALU.add))
                if front:
                    extras[NORMS_AT[0]].append(lambda: inverse_norms(0))
                if more:
                    extras[O_AT].append(prepare_o)
                if back:
                    extras[Z3_AT].append(low_z3)
                beside(0, XT, none, extras)
                if front:
                    extras = {NORMS_AT[1]: [lambda: inverse_norms(1)]}
                    if more:
                        extras[X1_AT] = [add_x1]
                    beside(0, XT + 1, spread, extras)
                extras = {m: [] for m in range(-1, FT + 1)}
                if front:
                    extras[CROSS_AT[0]].append(cross_q0)
                    extras[CROSS_AT[1]].append(variance_q0)
                    extras[CROSS_AT[2]].append(lambda: add_cross(base, tok_free))
                    extras[CROSS_AT[3]].append(lambda: normalise(z, q0, z_ready))
                beside(0, FT, hidden if back else none, extras)

            nc.vector.memset(eps[:, :], EPS)
            nc.vector.memset(mhalf[:, :], -0.5)
            nc.vector.memset(rstack[:, :, :].bitcast(F32), 0.0).then_inc(step, 1)
            dve.wait_ge(step, 1)
            dve.sem_inc(step, -1)
            nc.vector.engine_nop().then_inc(act_go, 1)
            dve.wait_ge(const_in, 16)
            dve.sem_inc(const_in, -16)
            nc.vector.engine_nop().then_inc(consts, 1)
            prepare_o()
            add_x1()
            round_(False, False, True, True)
            round_(False, True, True, True)
            with dve.Fori(2, B - 1):
                round_(True, True, True, True)
            round_(True, True, True, False)
            round_(True, True, False, False)
            add_back(x2, x2, out_ready)

        @block.tensor
        def _(pe):
            def product(bank, hi, lo, whi, wlo, start, stop):
                terms = [(whi, hi), (whi, lo)] + ([(wlo, hi)] if wlo is not None else [])
                for i, (ww, xx) in enumerate(terms):
                    last = nc.tensor.matmul(bank, ww, xx, start=start and i == 0, stop=stop and i == len(terms) - 1)
                return last

            def product_of(hi, lo, k, whi, wlo, first, last_):
                for c in range(C):
                    cols = slice(c * P, (c + 1) * P)
                    done = product(psY[c][:, :], hi, lo, whi[:, k, cols], wlo[:, k, cols] if wlo is not None else None, first, last_)
                    if last_:
                        done.then_inc(Y_ready, 1)

            def tile_of(bank, hi, lo, whi, wlo, m, signal, fresh=False):
                cols = slice(m * P, (m + 1) * P)
                for c in range(C):
                    if fresh:
                        pe.wait_ge(u_parts, 1)
                        pe.sem_inc(u_parts, -1)
                    done = product(psG[bank % RING][:, :], hi[:, c, :], lo[:, c, :], whi[:, c, cols],
                                   wlo[:, c, cols] if wlo is not None else None, c == 0, c == C - 1)
                done.then_inc(signal, 1)

            def transpose_rows():
                pe.wait_ge(z_ready, 1)
                pe.sem_inc(z_ready, -1)
                for t in range(TT):
                    for c in range(C):
                        last = nc.tensor.transpose(psT[c][:, t * P:(t + 1) * P], z[:, t, c * P:(c + 1) * P], ident[:, :])
                last.then_inc(T_ready, 1)

            def transpose_back(src):
                for t in range(TT):
                    for c in range(C):
                        at = ((t % 2) * C + c) * P
                        last = nc.tensor.transpose(psT[t // 2][:, at:at + P], src[:, c, t * P:(t + 1) * P], ident[:, :])
                last.then_inc(tok_ready, 1)

            def project_o():
                pe.wait_ge(o_parts, 1)
                pe.sem_inc(o_parts, -1)
                for k in range(C):
                    product_of(oh[:, k, :], ol[:, k, :], k, w["wout"][0], w["wout"][1], k == 0, k == C - 1)

            def second(k, w2):
                product_of(hh[:, k % RING, :], hl[:, k % RING, :], k, w2[0], w2[1], k == 0, k == FT - 1)

            def mlp(old, front):
                if old:
                    pe.wait_ge(feat_ready, C)
                    pe.sem_inc(feat_ready, -C)
                    transpose_back(feat_f)
                for m in range(FT + RING):
                    if m >= RING:
                        pe.wait_ge(h_parts, 1)
                        pe.sem_inc(h_parts, -1)
                        second(m - RING, w["w2"])
                    if m < FT:
                        tile_of(m, bh, bl, w["w1"][0], w["w1"][1], m, g_ready, m == 0)
                    if old and m == Z1_AT - 1:
                        pe.wait_ge(tok_free, 1)
                        pe.sem_inc(tok_free, -1)
                    if front and m == Z1_AT:
                        transpose_rows()

            def queries(back, more):
                for m in range(XT + RING):
                    if m >= RING:
                        k = m - RING
                        sums = (psY[0], psN)[k // HALF]
                        pe.wait_ge(sq_parts, 1)
                        pe.sem_inc(sq_parts, -1)
                        nc.tensor.matmul(sums[:, :], w["sum_sel"][:, k, :], sh[:, k % RING, :], start=(k % HALF == 0), stop=False)
                        last = nc.tensor.matmul(sums[:, :], w["sum_sel"][:, k, :], sl[:, k % RING, :], start=False,
                                                stop=(k % HALF == HALF - 1))
                        if k % HALF == HALF - 1:
                            last.then_inc(n2_ready, 1)
                    if m < XT:
                        tile_of(Q_AT + m, fh, fl, w["wq"][0], w["wq"][1], m, q_ready, m == 0)
                    if back and m == W2_BACK:
                        pe.wait_ge(feat_ready, C)
                        pe.sem_inc(feat_ready, -C)
                        transpose_back(feat_b)
                    if back and m == Z3_AT:
                        pe.wait_ge(tok_free, 1)
                        pe.sem_inc(tok_free, -1)
                        transpose_rows()
                    if m == XT:
                        pe.wait_ge(rn_ready, 1)
                        pe.sem_inc(rn_ready, -1)
                        if more:
                            project_o()
                    if m > XT:
                        spread(m - XT - 1)

            def spread(m):
                nc.tensor.matmul(psG[(S_AT + m) % RING][:, :], w["spread_sel"][:, m, :], rstack[:, m // HALF, :], start=True,
                                 stop=True).then_inc(s_ready, 1)

            def cross(back, more):
                if back:
                    pe.wait_ge(u_parts, C)
                    pe.sem_inc(u_parts, -C)
                pe.wait_ge(n_in, 32)
                pe.sem_inc(n_in, -32)
                for m in range(2, XT + RING):
                    if m >= RING:
                        k = m - RING
                        pe.wait_ge(qn_parts, 1)
                        pe.sem_inc(qn_parts, -1)
                        product_of(sh[:, k % RING, :], sl[:, k % RING, :], k, nw[0], nw[1], k == 0, k == XT - 1)
                    if m == HALF:
                        pe.wait_ge(rn_ready, 1)
                        pe.sem_inc(rn_ready, -1)
                    if m < XT:
                        spread(m)
                    if more and m == O_BACK:
                        pe.wait_ge(feat_ready, C)
                        pe.sem_inc(feat_ready, -C)
                        transpose_back(feat_f)
                if more:
                    pe.wait_ge(tok_free, 1)
                    pe.sem_inc(tok_free, -1)

            def ternary(front):
                for m in range(FT + RING):
                    if m >= RING:
                        pe.wait_ge(h_parts, 1)
                        pe.sem_inc(h_parts, -1)
                        second(m - RING, (w["t2"], None))
                    if m < FT:
                        tile_of(T_AT + m, bh, bl, w["t1"], None, m, g_ready)
                    if front and m == Y_BACK:
                        pe.wait_ge(feat_ready, C)
                        pe.sem_inc(feat_ready, -C)
                        transpose_back(feat_f)
                    if front and m == Z2_AT:
                        pe.wait_ge(tok_free, 1)
                        pe.sem_inc(tok_free, -1)
                        transpose_rows()

            def round_(old, back, front, more):
                if back:
                    mlp(old, front)
                elif front:
                    transpose_rows()
                if front:
                    queries(back, more)
                else:
                    pe.wait_ge(feat_ready, C)
                    pe.sem_inc(feat_ready, -C)
                    transpose_back(feat_b)
                    pe.wait_ge(tok_free, 1)
                    pe.sem_inc(tok_free, -1)
                    transpose_rows()
                    pe.wait_ge(u_parts, C)
                    pe.sem_inc(u_parts, -C)
                if front:
                    cross(back, more)
                if back:
                    ternary(front)
                else:
                    pe.wait_ge(feat_ready, C)
                    pe.sem_inc(feat_ready, -C)
                    transpose_back(feat_f)
                    pe.wait_ge(tok_free, 1)
                    pe.sem_inc(tok_free, -1)
                    transpose_rows()

            pe.wait_ge(consts, 1)
            pe.sem_inc(consts, -1)
            project_o()
            pe.wait_ge(feat_ready, C)
            pe.sem_inc(feat_ready, -C)
            transpose_back(feat_f)
            pe.wait_ge(tok_free, 1)
            pe.sem_inc(tok_free, -1)
            round_(False, False, True, True)
            round_(False, True, True, True)
            with pe.Fori(2, B - 1):
                round_(True, True, True, True)
            round_(True, True, True, False)
            round_(True, True, False, False)
            pe.wait_ge(feat_ready, C)
            pe.sem_inc(feat_ready, -C)
            transpose_back(feat_f)


def decoder_block(nc, a, out):
    def dram(name, shape, dt=F32):
        return nc.dram_tensor(name, shape, dt).ap()

    scr = {"q": dram("q_parts", [3, KVH, D, B, G * S], BF16), "k": dram("k_parts", [3, KVH * D, B, S], BF16),
           "v": dram("v_ones", [B, KVH, P, TT * 2 * D]), "o": dram("o_sums", [B, H, D + 1, S]),
           "rden": dram("rden", [B, H, S]), "n": dram("n_parts", [B, 2, P, XT * E])}
    project_phase(nc, a, scr)
    with ExitStack() as ctx:
        w = mixing_weights(nc, ctx)
        with ExitStack() as until_n:
            cw = context_weights(nc, until_n)
            attend_phase(nc, a, scr, split_list(a, w, cw))
            prepare_phase(nc, a, scr, w, cw)
        mix_phase(nc, a, scr, w, out)


def mixing_weights(nc, ctx):
    def sb(name, shape, dt):
        return ctx.enter_context(nc.sbuf_tensor("w_" + name, shape, dt))

    w = {name: (sb(name + "_hi", [P, k, n], F32R), sb(name + "_lo", [P, k, n], F32R))
         for name, k, n in (("wout", C, E), ("wq", C, XI), ("w1", C, FT * P), ("w2", FT, E))}
    w["t1"] = sb("t1", [P, C, FT * P], F32R)
    w["t2"] = sb("t2", [P, FT, E], F32R)
    w["sum_sel"] = sb("sum_sel", [P, XT, P], F32R)
    w["spread_sel"] = sb("spread_sel", [P, XT, P], F32R)
    vectors = (("bout", "L0_attn_bout", C), ("ln1_g", "L0_xattn_ln1_g", C), ("ln1_b", "L0_xattn_ln1_b", C),
               ("ln2_g", "L0_xattn_ln2_g", C), ("ln2_b", "L0_xattn_ln2_b", C), ("bo", "L0_xattn_bo", C),
               ("b1", "L0_xattn_b1", FT), ("b2", "L0_xattn_b2", C), ("fb1", "L0_ffn_b1", FT), ("fb2", "L0_ffn_b2", C))
    w["ncols"] = sum(k for _, _, k in vectors)
    w["all_columns"] = sb("columns", [P, w["ncols"]], F32)
    w["vectors"] = []
    at = 0
    for name, source, k in vectors:
        w[name] = w["all_columns"][:, at:at + k]
        w["vectors"].append((source, at, k))
        at += k
    return w


def context_weights(nc, ctx):
    return {name: tuple(ctx.enter_context(nc.sbuf_tensor(f"c_{name}_{part}", [P, k, n], F32R)) for part in ("hi", "lo"))
            for name, k, n in (("wk", C, XI), ("wv", C, XI))}


def split_list(a, w, cw):
    some = SPLIT // P
    selectors = [(a["selectors"][i, t:t + some].rearrange("t p m -> p t m"), dst[:, t:t + some, :], None)
                 for i, dst in enumerate((w["sum_sel"], w["spread_sel"])) for t in range(0, XT, some)]
    def piece(at, n):
        return slice(at, min(at + SPLIT, n))

    return selectors + [(a[source][c * P:(c + 1) * P, piece(at, hi.shape[2])], hi[:, c, piece(at, hi.shape[2])], lo[:, c, piece(at, hi.shape[2])])
            for source, (hi, lo) in (("L0_xattn_wk", cw["wk"]), ("L0_xattn_wv", cw["wv"]),
                                     ("L0_attn_Wout", w["wout"]), ("L0_xattn_w1", w["w1"]), ("L0_xattn_w2", w["w2"]),
                                     ("L0_xattn_wq", w["wq"]))
            for c in range(hi.shape[1]) for at in range(0, hi.shape[2], SPLIT)]


def weight_splitter(nc, pool, stage, stage_in, hi_done, lo_done, splits):
    def staged(i):
        shape = splits[i][0].shape
        if len(shape) == 3:
            return stage[i % 2][:, 0:shape[1] * shape[2]].rearrange("p (t m) -> p t m", t=shape[1])
        return stage[i % 2][:, 0:shape[1]]

    def load(i):
        pool.dma_start(staged(i), splits[i][0]).then_inc(stage_in[i % 2], 16)

    def weight(i):
        _, hi, lo = splits[i]
        if i + 1 < len(splits):
            if i >= 1:
                pool.wait_ge(lo_done, 1)
                pool.sem_inc(lo_done, -1)
            load(i + 1)
        pool.wait_ge(stage_in[i % 2], 16 * (i // 2 + 1))
        if lo is None:
            nc.gpsimd.tensor_copy(hi, staged(i)).then_inc(lo_done, 1)
            return
        nc.gpsimd.tensor_copy(hi, staged(i)).then_inc(hi_done, 1)
        pool.wait_ge(hi_done, 1)
        pool.sem_inc(hi_done, -1)
        nc.gpsimd.tensor_tensor(lo, staged(i), hi.bitcast(F32), ALU.subtract).then_inc(lo_done, 1)

    load(0)
    return weight, len(splits)


_INS = ["x", "ctx_1024", "L0_attn_Wqa", "L0_attn_Wqb", "L0_attn_Wkva", "L0_attn_Wkvb", "L0_attn_Wout", "L0_attn_bout",
        "L0_xattn_wq", "L0_xattn_wk", "L0_xattn_wv", "L0_xattn_wo", "L0_xattn_bo", "L0_xattn_w1", "L0_xattn_b1",
        "L0_xattn_w2", "L0_xattn_b2", "L0_xattn_ln1_g", "L0_xattn_ln1_b", "L0_xattn_ln2_g", "L0_xattn_ln2_b",
        "L0_ffn_W1", "L0_ffn_b1", "L0_ffn_W2", "L0_ffn_b2"]


def kernel(**inputs):
    import numpy as _np
    import concourse.bacc as _bacc
    from concourse import mybir as _mybir
    from concourse.bass_utils import run_bass_kernel_spmd as _run

    nc = _bacc.Bacc("TRN2", target_bir_lowering=False, num_devices=1)
    given = {name: _np.ascontiguousarray(inputs[name]) for name in _INS}
    given["rope"] = rope_tables()
    given["ident"] = _np.eye(P, dtype=_np.float32)
    given["mask"] = causal_mask()
    given["selectors"] = head_selectors()
    arrays, args = {}, {}
    for name, array in given.items():
        arrays[f"in_{name}_dram"] = array
        args[name] = nc.dram_tensor(f"in_{name}_dram", array.shape, _mybir.dt.from_np(array.dtype), kind="ExternalInput").ap()
    out = nc.dram_tensor("out_0_dram", (B, S, E), F32, kind="ExternalOutput").ap()
    decoder_block(nc, args, out)
    r = _run(nc, [arrays], core_ids=[0])
    return r.results[0]["out_0_dram"]
```
